# Optimizing a Trainium2 kernel written in Bass

```python
import numpy as np
import jax
import jax.numpy as jnp

def _softmax(x, axis=-1):
    return jax.nn.softmax(x, axis=axis)

def _gelu(x):
    return jax.nn.gelu(x, approximate=True)

def _silu(x):
    return jax.nn.silu(x)

def _sigmoid(x):
    return jax.nn.sigmoid(x)

def _layernorm(x, axis=-1, eps=1e-05):
    m = jnp.mean(x, axis=axis, keepdims=True)
    v = jnp.var(x, axis=axis, keepdims=True)
    return (x - m) / jnp.sqrt(v + eps)

def _scatter_add(tgt, idx, src, axis=0):
    return tgt.at[idx].add(src)

def _segment_sum(src, seg, n):
    return jax.ops.segment_sum(src, seg, n)
kernel_name = 'mk_hybrid_d1_jaxref_r8_18f616'

def setup_inputs(seed: int=0):
    np.random.seed(seed)
    _w = jnp.asarray

    def _L0_attn_a_setup():
        import jax, jax.numpy as jnp
        import numpy as np
        N_HEAD = 16
        LATENT = 32

        def _rotate_half(x):
            xe = x[..., ::2]
            xo = x[..., 1::2]
            return jnp.stack((-xo, xe), axis=-1).reshape(x.shape)

        def _rope_tables(T, latent_dim, dtype):
            inv_freq = 1.0 / 10000.0 ** (jnp.arange(0, latent_dim, 2, dtype=jnp.float32) / latent_dim)
            t = jnp.arange(T, dtype=jnp.float32)
            freqs = jnp.outer(t, inv_freq)
            cos = jnp.repeat(jnp.cos(freqs), 2, axis=-1)[:, :latent_dim]
            sin = jnp.repeat(jnp.sin(freqs), 2, axis=-1)[:, :latent_dim]
            return (cos.astype(dtype), sin.astype(dtype))
        key = jax.random.key(seed)
        ks = jax.random.split(key, 14)
        C = 128
        hd = C // N_HEAD
        L = LATENT
        s = 0.02
        return {'x': jax.random.normal(ks[0], (4, 256, C), jnp.float32), 'c_attn_w': jax.random.normal(ks[1], (3 * C, C), jnp.float32) * s, 'c_attn_b': jnp.zeros((3 * C,), jnp.float32), 'q2l_w': jax.random.normal(ks[2], (L, hd), jnp.float32) * s, 'q2l_b': jnp.zeros((L,), jnp.float32), 'kv2l_w': jax.random.normal(ks[3], (L, hd), jnp.float32) * s, 'kv2l_b': jnp.zeros((L,), jnp.float32), 'l2o_w': jax.random.normal(ks[4], (hd, L), jnp.float32) * s, 'l2o_b': jnp.zeros((hd,), jnp.float32), 'wqk_w': jax.random.normal(ks[5], (L, L), jnp.float32) * s, 'wqk_b': jnp.zeros((L,), jnp.float32), 'cproj_w': jax.random.normal(ks[6], (C, C), jnp.float32) * s, 'cproj_b': jnp.zeros((C,), jnp.float32)}
    _L0_attn_a_in = _L0_attn_a_setup()

    def _L0_attn_b_setup():
        import jax, jax.numpy as jnp
        import numpy as np
        B, S, H, NH = (2, 256, 128, 16)
        HD = H // NH
        key = jax.random.key(seed)
        ks = jax.random.split(key, 9)
        w = lambda k: jax.random.normal(k, (H, H), dtype=jnp.float32) * 0.02
        b = lambda k: jax.random.normal(k, (H,), dtype=jnp.float32) * 0.02
        return {'hidden_states': jax.random.normal(ks[0], (B, S, H), dtype=jnp.float32), 'Wq': w(ks[1]), 'bq': b(ks[2]), 'Wk': w(ks[3]), 'bk': b(ks[4]), 'Wv': w(ks[5]), 'bv': b(ks[6]), 'Wo': w(ks[7]), 'bo': b(ks[8])}
    _L0_attn_b_in = _L0_attn_b_setup()

    def _L0_ffn_setup():
        import jax, jax.numpy as jnp
        import numpy as np
        from jax import lax
        D = 128
        E = 8
        F = 512
        TOP_K = 2
        key = jax.random.key(seed)
        ks = jax.random.split(key, 8)
        s = 0.02
        return {'x': jax.random.normal(ks[0], (4, 256, D), dtype=jnp.float32), 'gate_w': jax.random.normal(ks[1], (D, E), dtype=jnp.float32) * s, 'gate_b': jnp.zeros((E,), dtype=jnp.float32), 'w1': jax.random.normal(ks[2], (E, D, F), dtype=jnp.float32) * s, 'b1': jnp.zeros((E, F), dtype=jnp.float32), 'w2': jax.random.normal(ks[3], (E, F, D), dtype=jnp.float32) * s, 'b2': jnp.zeros((E, D), dtype=jnp.float32)}
    _L0_ffn_in = _L0_ffn_setup()
    _d = {'L0_attn_a_x': _L0_attn_a_in['x'], 'L0_attn_a_c_attn_w': _L0_attn_a_in['c_attn_w'], 'L0_attn_a_c_attn_b': _L0_attn_a_in['c_attn_b'], 'L0_attn_a_q2l_w': _L0_attn_a_in['q2l_w'], 'L0_attn_a_q2l_b': _L0_attn_a_in['q2l_b'], 'L0_attn_a_kv2l_w': _L0_attn_a_in['kv2l_w'], 'L0_attn_a_kv2l_b': _L0_attn_a_in['kv2l_b'], 'L0_attn_a_l2o_w': _L0_attn_a_in['l2o_w'], 'L0_attn_a_l2o_b': _L0_attn_a_in['l2o_b'], 'L0_attn_a_wqk_w': _L0_attn_a_in['wqk_w'], 'L0_attn_a_wqk_b': _L0_attn_a_in['wqk_b'], 'L0_attn_a_cproj_w': _L0_attn_a_in['cproj_w'], 'L0_attn_a_cproj_b': _L0_attn_a_in['cproj_b'], 'L0_attn_b_Wq': _L0_attn_b_in['Wq'], 'L0_attn_b_bq': _L0_attn_b_in['bq'], 'L0_attn_b_Wk': _L0_attn_b_in['Wk'], 'L0_attn_b_bk': _L0_attn_b_in['bk'], 'L0_attn_b_Wv': _L0_attn_b_in['Wv'], 'L0_attn_b_bv': _L0_attn_b_in['bv'], 'L0_attn_b_Wo': _L0_attn_b_in['Wo'], 'L0_attn_b_bo': _L0_attn_b_in['bo'], 'L0_ffn_gate_w': _L0_ffn_in['gate_w'], 'L0_ffn_gate_b': _L0_ffn_in['gate_b'], 'L0_ffn_w1': _L0_ffn_in['w1'], 'L0_ffn_b1': _L0_ffn_in['b1'], 'L0_ffn_w2': _L0_ffn_in['w2'], 'L0_ffn_b2': _L0_ffn_in['b2']}
    _x0 = _d['L0_attn_a_x']
    _d['L0_attn_a_x'] = jax.random.normal(jax.random.fold_in(jax.random.key(seed), 1), (16, 256, 128), dtype=_x0.dtype)
    del _x0
    return _d

def reference(L0_attn_a_x, L0_attn_a_c_attn_w, L0_attn_a_c_attn_b, L0_attn_a_q2l_w, L0_attn_a_q2l_b, L0_attn_a_kv2l_w, L0_attn_a_kv2l_b, L0_attn_a_l2o_w, L0_attn_a_l2o_b, L0_attn_a_wqk_w, L0_attn_a_wqk_b, L0_attn_a_cproj_w, L0_attn_a_cproj_b, L0_attn_b_Wq, L0_attn_b_bq, L0_attn_b_Wk, L0_attn_b_bk, L0_attn_b_Wv, L0_attn_b_bv, L0_attn_b_Wo, L0_attn_b_bo, L0_ffn_gate_w, L0_ffn_gate_b, L0_ffn_w1, L0_ffn_b1, L0_ffn_w2, L0_ffn_b2):

    def _L0_attn_a_ref(x, c_attn_w, c_attn_b, q2l_w, q2l_b, kv2l_w, kv2l_b, l2o_w, l2o_b, wqk_w, wqk_b, cproj_w, cproj_b):
        import jax, jax.numpy as jnp
        import numpy as np
        N_HEAD = 16
        LATENT = 32

        def _rotate_half(x):
            xe = x[..., ::2]
            xo = x[..., 1::2]
            return jnp.stack((-xo, xe), axis=-1).reshape(x.shape)

        def _rope_tables(T, latent_dim, dtype):
            inv_freq = 1.0 / 10000.0 ** (jnp.arange(0, latent_dim, 2, dtype=jnp.float32) / latent_dim)
            t = jnp.arange(T, dtype=jnp.float32)
            freqs = jnp.outer(t, inv_freq)
            cos = jnp.repeat(jnp.cos(freqs), 2, axis=-1)[:, :latent_dim]
            sin = jnp.repeat(jnp.sin(freqs), 2, axis=-1)[:, :latent_dim]
            return (cos.astype(dtype), sin.astype(dtype))
        B, T, C = x.shape
        H = N_HEAD
        hd = C // H
        L = q2l_w.shape[0]
        qkv = x @ c_attn_w.T + c_attn_b
        q, k, v = jnp.split(qkv, 3, axis=2)

        def heads(t):
            return t.reshape(B, T, H, hd).transpose(0, 2, 1, 3)
        q, k, v = (heads(q), heads(k), heads(v))
        q_lat = q @ q2l_w.T + q2l_b
        k_lat = k @ kv2l_w.T + kv2l_b
        v_lat = v @ kv2l_w.T + kv2l_b
        cos, sin = _rope_tables(T, L, x.dtype)
        cos = cos[None, None]
        sin = sin[None, None]
        q_lat = q_lat * cos + _rotate_half(q_lat) * sin
        k_lat = k_lat * cos + _rotate_half(k_lat) * sin
        q_for_k = q_lat @ wqk_w.T + wqk_b
        att = jnp.einsum('bhql,bhkl->bhqk', q_for_k, k_lat) * L ** (-0.5)
        causal = jnp.tril(jnp.ones((T, T), dtype=bool))
        att = jnp.where(causal[None, None], att, -jnp.inf)
        att = jax.nn.softmax(att, axis=-1)
        y_lat = jnp.einsum('bhqk,bhkl->bhql', att, v_lat)
        y = y_lat @ l2o_w.T + l2o_b
        y = y.transpose(0, 2, 1, 3).reshape(B, T, C)
        return y @ cproj_w.T + cproj_b

    def _L0_attn_b_ref(hidden_states, Wq, bq, Wk, bk, Wv, bv, Wo, bo):
        import jax, jax.numpy as jnp
        import numpy as np
        B, S, H, NH = (2, 256, 128, 16)
        HD = H // NH
        b, s, h = hidden_states.shape
        nh, hd = (NH, h // NH)

        def proj(W, bias):
            y = hidden_states @ W.T + bias
            return y.reshape(b, s, nh, hd).transpose(0, 2, 1, 3)
        q = proj(Wq, bq)
        k = proj(Wk, bk)
        v = proj(Wv, bv)
        scale = jnp.sqrt(jnp.asarray(hd, dtype=q.dtype))
        scores = jnp.einsum('bhqd,bhkd->bhqk', q, k) / scale
        pos = jnp.arange(s)
        causal = pos[:, None] < pos[None, :]
        scores = jnp.where(causal[None, None], -jnp.inf, scores)
        attn = jax.nn.softmax(scores, axis=-1)
        out = jnp.einsum('bhqk,bhkd->bhqd', attn, v)
        out = out.transpose(0, 2, 1, 3).reshape(b, s, h)
        return out @ Wo.T + bo

    def _L0_ffn_ref(x, gate_w, gate_b, w1, b1, w2, b2):
        import jax, jax.numpy as jnp
        import numpy as np
        from jax import lax
        D = 128
        E = 8
        F = 512
        TOP_K = 2
        B, S, _ = x.shape
        flat = x.reshape(-1, D)
        T = flat.shape[0]
        logits = flat @ gate_w + gate_b
        topv, topi = lax.top_k(logits, TOP_K)
        topw = jax.nn.softmax(topv.astype(jnp.float32), axis=-1).astype(x.dtype)
        routing = jnp.zeros_like(logits).at[jnp.arange(T)[:, None], topi].set(topw)

        def body(acc, params):
            W1e, b1e, W2e, b2e, we = params
            h = jax.nn.gelu(flat @ W1e + b1e, approximate=False)
            out = h @ W2e + b2e
            return (acc + out * we[:, None], None)
        init = jnp.zeros_like(flat)
        final, _ = lax.scan(body, init, (w1, b1, w2, b2, routing.T))
        return final.reshape(B, S, D)
    x = L0_attn_a_x
    x = x + _L0_attn_a_ref(_layernorm(x, axis=-1), L0_attn_a_c_attn_w, L0_attn_a_c_attn_b, L0_attn_a_q2l_w, L0_attn_a_q2l_b, L0_attn_a_kv2l_w, L0_attn_a_kv2l_b, L0_attn_a_l2o_w, L0_attn_a_l2o_b, L0_attn_a_wqk_w, L0_attn_a_wqk_b, L0_attn_a_cproj_w, L0_attn_a_cproj_b)
    x = x + _L0_ffn_ref(_layernorm(x, axis=-1), L0_ffn_gate_w, L0_ffn_gate_b, L0_ffn_w1, L0_ffn_b1, L0_ffn_w2, L0_ffn_b2)
    x = x + _L0_attn_b_ref(_layernorm(x, axis=-1), L0_attn_b_Wq, L0_attn_b_bq, L0_attn_b_Wk, L0_attn_b_bk, L0_attn_b_Wv, L0_attn_b_bv, L0_attn_b_Wo, L0_attn_b_bo)
    x = x + _L0_ffn_ref(_layernorm(x, axis=-1), L0_ffn_gate_w, L0_ffn_gate_b, L0_ffn_w1, L0_ffn_b1, L0_ffn_w2, L0_ffn_b2)
    return x

_drawn_inputs = setup_inputs


def setup_inputs(seed=0):
    import zlib

    import numpy as np

    out = dict(_drawn_inputs(seed))
    spreads = {'L0_attn_a_c_attn_b': (0.0, 0.8),
     'L0_attn_a_q2l_b': (0.0, 0.8),
     'L0_attn_a_kv2l_b': (0.0, 0.8),
     'L0_attn_a_l2o_b': (0.0, 0.274),
     'L0_attn_a_wqk_b': (0.0, 0.8),
     'L0_attn_a_cproj_b': (0.0, 0.1),
     'L0_ffn_gate_b': (0.0, 0.1),
     'L0_ffn_b1': (0.0, 0.1),
     'L0_ffn_b2': (0.0, 0.1)}
    factors = {'L0_attn_a_c_attn_w': 8.0,
     'L0_attn_a_q2l_w': 8.0,
     'L0_attn_a_kv2l_w': 8.0,
     'L0_attn_a_l2o_w': 8.0,
     'L0_attn_a_wqk_w': 8.0,
     'L0_attn_b_Wq': 8.0,
     'L0_attn_b_bq': 8.0,
     'L0_attn_b_Wk': 8.0,
     'L0_attn_b_bk': 64.0,
     'L0_attn_b_Wv': 5.22,
     'L0_attn_b_bv': 8.0,
     'L0_attn_b_Wo': 4.591,
     'L0_attn_b_bo': 3.28}
    for name, (base, spread) in spreads.items():
        noise = np.random.default_rng([zlib.crc32(name.encode()), seed]).standard_normal(out[name].shape)
        drawn = base * np.exp(spread * noise) if base else spread * noise
        out[name] = jnp.asarray(drawn.astype(out[name].dtype))
    for name, factor in factors.items():
        out[name] = (out[name] * factor).astype(out[name].dtype)
    return out
```

```python
from contextlib import ExitStack

import numpy as np

import concourse.bass as bass
from concourse import mybir

F32 = mybir.dt.float32
F32R = mybir.dt.float32r
BF16 = mybir.dt.bfloat16
I32 = mybir.dt.int32
ALU = mybir.AluOpType
ACT = mybir.ActivationFunctionType
AX = mybir.AxisListType.X

P = 128
B, S, D = 16, 256, 128
T = B * S
NT = T // P
H, HD, L = 16, 8, 32
G = 4
CH = 512
NCH = T // CH
CT = CH // P
UNITS = 8
E, F = 8, 512
FT = F // P
SLOT_TILES = 2 * NT + E
EPS = 1e-5
MASKED = -1e30
CLEAR = 512

_COLS = {}
_at = 0
for _name, _n in (("ident", P), ("head_mask", H), ("group_mask", G), ("rep8", P), ("rep32", P), ("rot32", P),
                  ("cos", S), ("sin", S), ("causal", P), ("before", P), ("tile_no", SLOT_TILES), ("prefer", E)):
    _COLS[_name] = (_at, _at + _n)
    _at += _n
CONST_W = _at


def constants():
    c = np.zeros((P, CONST_W), np.float32)

    def put(name, a):
        c[:a.shape[0], _COLS[name][0]:_COLS[name][1]] = a

    p = np.arange(P)
    put("ident", np.eye(P, dtype=np.float32))
    put("head_mask", (p[:, None] // HD == np.arange(H)).astype(np.float32))
    put("group_mask", (p[:, None] // L == np.arange(G)).astype(np.float32))
    put("rep8", (np.arange(HD)[:, None] == p % HD).astype(np.float32))
    put("rep32", (np.arange(L)[:, None] == p % L).astype(np.float32))
    rot = np.zeros((L, P), np.float32)
    for q in range(P):
        l = q % L
        rot[l + 1 if l % 2 == 0 else l - 1, q] = -1.0 if l % 2 == 0 else 1.0
    put("rot32", rot)
    inv = (np.float32(1.0) / np.power(np.float32(10000.0), np.arange(0, L, 2, dtype=np.float32) / np.float32(L))).astype(np.float32)
    ang = np.outer(np.arange(S, dtype=np.float32), inv).astype(np.float32)
    cos = np.repeat(np.cos(ang), 2, axis=1).T
    sin = np.repeat(np.sin(ang), 2, axis=1).T
    put("cos", np.tile(cos, (G, 1)).astype(np.float32))
    put("sin", np.tile(sin, (G, 1)).astype(np.float32))
    put("causal", np.where(np.arange(P)[None, :] > p[:, None], np.float32(MASKED), np.float32(0)))
    put("before", (p[:, None] < np.arange(P)[None, :]).astype(np.float32))
    put("tile_no", np.broadcast_to(np.arange(SLOT_TILES, dtype=np.float32), (P, SLOT_TILES)))
    put("prefer", np.broadcast_to(E - np.arange(E, dtype=np.float32), (P, E)))
    return c


class Order:

    def __init__(self, eng, sem):
        self.eng, self.sem, self.base, self.n = eng, sem, 0, 0

    def did(self, ins):
        self.n += 1
        return ins.then_inc(self.sem, 1)

    def settle(self):
        self.eng.wait_ge(self.sem, self.n + self.base)

    def then(self, ins):
        self.did(ins)
        self.settle()

    def loop(self, i, per):
        self.outside, self.per = self.n, per
        self.base, self.n = i * per + self.outside, 0

    def end(self, iterations):
        assert self.n == self.per, (self.n, self.per)
        self.base, self.n = 0, self.outside + iterations * self.per


class Steps:

    def __init__(self, layer):
        self.rotary = layer == "a"
        self.make = {(0, 1): [("prep", 0)], (0, 2): [("value", 0)]}
        for g in range(G):
            self.make[(2 + g, 0)] = [("query", g)]
            self.make[(2 + g, 1)] = [("key", g)]
            if self.rotary:
                self.make[(2 + g, 2)] = [("query2", g)]
        self.close = {(1, 1): [("out_t", 0)], (1, 2): [("out", 0)]}
        self.n_make, self.n_close = sum(map(len, self.make.values())), 2

    def at(self, u, nb, make, close):
        return (self.make.get((u, nb), []) if make else []) + (self.close.get((u, nb), []) if close else [])

    def all_make(self):
        return [s for k in sorted(self.make) for s in self.make[k]]

    def made(self, c, step):
        if isinstance(c, int) and c == 0:
            return self.all_make().index(step) + 1
        closing = not (isinstance(c, int) and c == 1)
        order = [s for u in range(UNITS) for nb in range(3) for s in self.at(u, nb, True, closing)]
        return self.before(c - 1) + (order.index(step) + 1)

    def before(self, c):
        if isinstance(c, int) and c == 0:
            return self.n_make
        return (c - 1) * (self.n_make + self.n_close) + 2 * self.n_make


def periods(eng, period, own=None, per=0):
    period(0, 0, True, False)
    with eng.Fori(0, NCH // 2 - 1) as i:
        if own:
            own.loop(i, per)
        period(i * 2 + 1, 1, False, False)
        period(i * 2 + 2, 0, False, False)
    if own:
        own.end(NCH // 2 - 1)
    period(NCH - 1, 1, False, True)


def stores_before(i, r, least):
    return 16 * (i // 4) if isinstance(i, int) else i * 4 - 4 * r


def loads_until(i, r, least):
    return 16 * (i // 4 + 1) if isinstance(i, int) else i * 4 + (16 - 4 * r)


PEEL = 8


def tile_slots(eng, slot):
    for i in range(PEEL):
        slot(i, i % 4, i)
    with eng.Fori(0, (SLOT_TILES - PEEL) // 4 - 1) as it:
        for r in range(4):
            slot(it * 4 + (PEEL + r), r, PEEL + r)
    for i in range(SLOT_TILES - 4, SLOT_TILES):
        slot(i, i % 4, i)


def program(nc, x, c_attn_w, c_attn_b, q2l_w, q2l_b, kv2l_w, kv2l_b, l2o_w, l2o_b, wqk_w, wqk_b, cproj_w, cproj_b,
            Wq, bq, Wk, bk, Wv, bv, Wo, bo, gate_w, gate_b, w1, b1, w2, b2, const, out):
    x_tiles = x.rearrange("b s d -> (b s) d").rearrange("(t p) d -> p t d", p=P)
    out_tiles = out.rearrange("b s d -> (b s) d").rearrange("(t p) d -> p t d", p=P)
    rows_in = nc.dram_tensor("sorted_rows", [SLOT_TILES * P, D], F32, kind="Internal").ap()
    rows_out = nc.dram_tensor("expert_rows", [SLOT_TILES * P, D], F32, kind="Internal").ap()

    with ExitStack() as ctx:
        def sb(name, shape, dt=F32, scope=ctx):
            return scope.enter_context(nc.sbuf_tensor(name, shape, dt))

        def sem(name):
            return ctx.enter_context(nc.semaphore(name))

        X = sb("X", [P, NT, D])
        C = sb("C", [P, CONST_W])
        ident = C[:, _COLS["ident"][0]:_COLS["ident"][1]]
        con = lambda name, rows=P: C[0:rows, _COLS[name][0]:_COLS[name][1]]
        ident_b = sb("ident_b", [P, P], BF16)
        causal_b = sb("causal_b", [P, P], BF16)
        before_b = sb("before_b", [P, P], BF16)
        ones_b = sb("ones_b", [P, P], BF16)
        W1 = sb("W1", [P, E * F])
        W2 = sb("W2", [P, E * FT * D])
        gate = sb("gate", [P, E])
        gate_bias = sb("gate_bias", [P, E])
        stats = sb("stats", [P, CT, 6])
        mv = sb("mv", [P, CT, 2])
        rstd = sb("rstd", [P, CT])
        var_eps = sb("var_eps", [P, CT])
        scratch1 = sb("scratch1", [1, 1])
        scratch2 = sb("scratch2", [1, 1])
        neg_half = sb("neg_half", [P, CT])
        xn = sb("xn", [P, CT, D])
        layers = {}
        for name, n_mats in (("a", 4), ("b", 2)):
            layers[name] = dict(
                hi=[sb(f"{name}_proj{m}_hi", [P, H * L], F32R) for m in range(n_mats)],
                lo=[sb(f"{name}_proj{m}_lo", [P, H * L], F32R) for m in range(n_mats)],
                v_hi=sb(f"{name}_v_hi", [P, D], F32R), v_lo=sb(f"{name}_v_lo", [P, D], F32R),
                bias=sb(f"{name}_bias", [P, n_mats, G]), v_bias=sb(f"{name}_v_bias", [P, D]),
                out_w=sb(f"{name}_out_w", [P, D]), out_b=sb(f"{name}_out_b", [P, D]))
        wqk_blk = sb("wqk_blk", [P, P])
        wqk_bias = sb("wqk_bias", [P, 1])
        zero_rows = sb("zero_rows", [P, CLEAR])

        with ExitStack() as att:
            xt_hi = sb("xt_hi", [P, CH], F32R, att)
            xt_lo = sb("xt_lo", [P, CH], F32R, att)
            q_hi = sb("q_hi", [P, 2, G, CH], F32R, att)
            q_lo = sb("q_lo", [P, 2, G, CH], F32R, att)
            k_hi = sb("k_hi", [P, 2, G, CH], F32R, att)
            k_lo = sb("k_lo", [P, 2, G, CH], F32R, att)
            prob = sb("prob", [P, 3, 512], F32, att)
            prob_t = sb("prob_t", [P, 2, 3, 512], F32, att)
            v_aug = sb("v_aug", [P, 2, CT, H, L], F32, att)
            o_t = sb("o_t", [P, 2, S], F32, att)
            Y = sb("Y", [P, 2, CT, D], F32, att)
            y_t = sb("y_t", [P, CH], F32, att)
            rope_q = sb("rope_q", [P, 2, CH], F32, att)
            rope_k = sb("rope_k", [P, 2, CH], F32, att)
            neg_max = sb("neg_max", [P, 3, G], F32, att)
            inv_sum = sb("inv_sum", [P, 2, G], F32, att)
        with ExitStack() as moe:
            XN = sb("XN", [P, NT, D], F32, moe)
            xt_plain = sb("xt_plain", [P, CH], F32, moe)
            B1 = sb("B1", [P, E * F], F32, moe)
            B2 = sb("B2", [P, E * D], F32, moe)
            xg = sb("xg", [P, 4, D], F32, moe)
            xg_t = sb("xg_t", [P, 2, P], F32, moe)
            pre_act = sb("pre_act", [P, 2, F], F32, moe)
            hid = sb("hid", [P, 2, F], F32, moe)
            hid_t = sb("hid_t", [P, 2, F], F32, moe)
            y_rows = sb("y_rows", [P, 4, D], F32, moe)
            got = sb("got", [P, 8, D], F32, moe)
            logit = sb("logit", [P, NT, E], F32, moe)
            route = [sb(f"route{k}", [P, NT, E], F32, moe) for k in range(6)]
            chosen_b = sb("chosen_b", [P, NT, E], BF16, moe)
            col = [sb(f"col{k}", [P, NT], F32, moe) for k in range(5)]
            weight = [sb(f"weight{k}", [P, NT], F32, moe) for k in range(2)]
            ecol = [sb(f"ecol{k}", [P, E], F32, moe) for k in range(5)]
            ecol_i = [sb(f"ecol_i{k}", [P, E], I32, moe) for k in range(2)]
            slot_of = sb("slot_of", [P, 2 * NT], I32, moe)
            emap_f = sb("emap_f", [1, SLOT_TILES, E], F32, moe)
            emap_s = sb("emap_s", [1, 2, SLOT_TILES], F32, moe)
            expert_of = sb("expert_of", [1, SLOT_TILES], I32, moe)
        with ExitStack() as prep:
            cw = sb("cw", [P, 3, D], F32, prep)
            cp = sb("cp", [P, D], F32, prep)
            wb = sb("wb", [P, 4, D], F32, prep)
            q2l_t = sb("q2l_t", [HD, L], F32, prep)
            kv2l_t = sb("kv2l_t", [HD, L], F32, prep)
            kv2l_n = sb("kv2l_n", [L, HD], F32, prep)
            l2o_t = sb("l2o_t", [L, HD], F32, prep)
            wqk_t = sb("wqk_t", [L, L], F32, prep)
            b3 = sb("b3", [P, 3], F32, prep)
            lat_b = sb("lat_b", [L, 3], F32, prep)
            l2o_row = sb("l2o_row", [1, HD], F32, prep)
            rep = sb("rep", [P, 104], F32, prep)
            m_t = sb("m_t", [HD, HD], F32, prep)
            blk = [sb(f"blk{k}", [P, H, L], F32, prep) for k in range(4)]
            blk_v = sb("blk_v", [P, H, HD], F32, prep)
            blk_vb = sb("blk_vb", [P, H, HD], F32, prep)
            kvb_rep = sb("kvb_rep", [L, P], F32, prep)
            ones = sb("ones", [P, P], F32, prep)
            pad = [sb(f"pad{k}", [P, H, L], F32, prep) for k in range(2)]
            bqk = sb("bqk", [P, 2, G], F32, prep)

        bank = [ctx.enter_context(nc.psum_tensor(f"bank{k}", [P, 512], F32)) for k in range(8)]
        s_bank, t_bank, o_bank, w_bank = bank[0:3], bank[3:5], bank[5], bank[6:8]
        y_bank = [bank[5], bank[2]]

        loaded = sem("loaded")
        experts_loaded = sem("experts_loaded")
        rows_cleared = sem("rows_cleared")
        zeroed = sem("zeroed")
        pe_prep = sem("pe_prep")
        dve_prep = sem("dve_prep")
        dve_own = sem("dve_own")
        att_sems = {n: {k: sem(f"{n}_{k}") for k in (
            "scores_ready", "max_ready", "probs_ready", "pt_ready", "pt_copied_act", "pt_copied_dve", "pv_ready",
            "o_copied", "o_ready", "y_ready", "shared_ready", "shared_free", "ln_ready", "var_ready", "rstd_ready", "hi_ready",
            "rope_summed", "key_hi_ready", "key_lo_ready")} for n in "ab"}
        moe_sems = {n: {k: sem(f"m{n}_{k}") for k in (
            "bias_loaded", "ln_ready", "var_ready", "rstd_ready", "ln_kept", "lnt_ready", "lnt_copied", "logit_ready", "logit_copied",
            "gap_ready", "exp_ready", "mask_ready", "rank_ready", "slots_ready", "scattered",
            "row0", "row1", "row2", "row3", "xt_ready", "xt_copied", "up_ready", "biased", "gelu_ready",
            "ht_ready", "ht_copied", "down_ready", "y_biased", "stored0", "stored1", "stored2", "stored3",
            "got0", "got1", "got2", "got3", "got4", "got5", "got6", "got7", "got_used")} for n in "12"}
        attended = {n: sem(f"attended_{n}") for n in "ab"}
        stored = sem("stored")

        block = ctx.enter_context(nc.Block())

        N_LOADS = 0

        @block.sync
        def _(sp):
            nonlocal N_LOADS

            def load(dst, src):
                nonlocal N_LOADS
                N_LOADS += 1
                sp.dma_start(dst, src).then_inc(loaded, 16)

            load(C[:, :], const)
            load(cw[:, :, :], c_attn_w.rearrange("(s p) c -> p s c", p=P))
            with nc.allow_non_contiguous_dma(reason="small transposed weights"):
                load(q2l_t[:, :], q2l_w.rearrange("l d -> d l"))
                load(kv2l_t[:, :], kv2l_w.rearrange("l d -> d l"))
                load(l2o_t[:, :], l2o_w.rearrange("o l -> l o"))
                load(wqk_t[:, :], wqk_w.rearrange("o l -> l o"))
                load(b3[:, :], c_attn_b.rearrange("(s p) -> p s", p=P))
                for k, v in enumerate((q2l_b, kv2l_b, wqk_b)):
                    load(lat_b[:, k:k + 1], v.rearrange("(l a) -> l a", a=1))
            load(kv2l_n[:, :], kv2l_w)
            load(l2o_row[:, :], l2o_b.rearrange("(a o) -> a o", a=1))
            load(cp[:, :], cproj_w)
            for k, w in enumerate((Wq, Wk, Wv, Wo)):
                load(wb[:, k, :], w)
            load(layers["a"]["out_b"][:, :], cproj_b.partition_broadcast(P))
            load(layers["b"]["out_b"][:, :], bo.partition_broadcast(P))
            load(layers["b"]["v_bias"][:, :], bv.partition_broadcast(P))
            load(gate_bias[:, :], gate_b.partition_broadcast(P))
            load(gate[:, :], gate_w)
            load(X[:, :, :], x_tiles)
            sp.wait_ge(zeroed, 1)
            with nc.allow_non_contiguous_dma(reason="biases spread over quadrants"):
                for m, v in enumerate((bq, bk)):
                    for j in range(G):
                        load(bqk[L * j:L * j + HD, m, :], v.rearrange("(g j d) -> j d g", j=G, d=HD)[j])
            sp.dma_start(W1[:, :].rearrange("p (e f) -> p e f", e=E), w1.rearrange("e d f -> d e f")).then_inc(experts_loaded, 16)
            sp.dma_start(W2[:, :].rearrange("p (e k d) -> p e k d", e=E, k=FT), w2.rearrange("e (k p) d -> p e k d", p=P)).then_inc(experts_loaded, 16)
            clear = rows_in.rearrange("(p r) d -> p (r d)", p=P)
            for k in range(SLOT_TILES * P // CLEAR):
                sp.dma_start(clear[:, CLEAR * k:CLEAR * k + CLEAR], zero_rows[:, :]).then_inc(rows_cleared, 16)

            for n in "12":
                m = moe_sems[n]
                sp.wait_ge(attended["a" if n == "1" else "b"], 1)
                sp.dma_start(B1[:, :], b1.rearrange("e f -> (e f)").partition_broadcast(P)).then_inc(m["bias_loaded"], 16)
                sp.dma_start(B2[:, :], b2.rearrange("e d -> (e d)").partition_broadcast(P)).then_inc(m["bias_loaded"], 16)
                sp.wait_ge(m["scattered"], 16 * 2 * NT)

                def fetch(i, r):
                    sp.dma_start(xg[:, r, :], rows_in[bass.ds(i * P, P), :]).then_inc(m[f"row{r}"], 16)

                for i in range(4):
                    fetch(i, i)
                with sp.Fori(0, SLOT_TILES // 4 - 1) as it:
                    for r in range(4):
                        sp.wait_ge(m["xt_ready"], it * 4 + (r + 1))
                        fetch(it * 4 + (4 + r), r)
            for c in range(NCH):
                sp.wait_ge(moe_sems["2"]["got_used"], 2 * CT * (c + 1))
                sp.dma_start(out_tiles[:, c * CT:(c + 1) * CT, :], X[:, c * CT:(c + 1) * CT, :]).then_inc(stored, 16)
            sp.wait_ge(stored, 16 * NCH)

        @block.gpsimd
        def _(pool):
            nc.gpsimd.memset(bqk[:, :, :], 0.0)
            nc.gpsimd.memset(neg_half[:, :], -0.5)
            nc.gpsimd.memset(zero_rows[:, :], 0.0).then_inc(zeroed, 1)
            pool.wait_ge(zeroed, 1)

            def inverse_root(m, nth):
                pool.wait_ge(m["var_ready"], nth)
                nc.gpsimd.tensor_tensor(rstd[:, :], var_eps[:, :], neg_half[:, :], ALU.pow).then_inc(m["rstd_ready"], 1)

            def rotary(c, par):
                m, steps = att_sems["a"], Steps("a")
                inverse_root(m, c + 1)
                for g in range(G):
                    pool.wait_ge(m["shared_free"], steps.made(c, ("query", g)))
                    nc.gpsimd.tensor_tensor(rope_q[:, 0, :], rope_q[:, 0, :], rope_q[:, 1, :], ALU.add).then_inc(m["rope_summed"], 1)
                    pool.wait_ge(m["shared_free"], steps.made(c, ("key", g)))
                    nc.gpsimd.tensor_tensor(rope_k[:, 0, :], rope_k[:, 0, :], rope_k[:, 1, :], ALU.add).then_inc(m["rope_summed"], 1)
                    pool.wait_ge(m["key_hi_ready"], c * G + (g + 1))
                    nc.gpsimd.tensor_tensor(k_lo[:, par, g, :], rope_k[:, 0, :], k_hi[:, par, g, :].bitcast(F32), ALU.subtract).then_inc(m["key_lo_ready"], 1)

            rotary(0, 0)
            rotary(1, 1)
            with pool.Fori(0, 3) as i:
                rotary(i * 2 + 2, 0)
                rotary(i * 2 + 3, 1)

            for n in "12":
                m = moe_sems[n]
                if n == "2":
                    with pool.Fori(0, NCH) as c:
                        inverse_root(att_sems["b"], c + 1)
                with pool.Fori(0, NCH) as c:
                    inverse_root(m, c + 1)
                    pool.wait_ge(m["ln_ready"], c + 1)
                    nc.gpsimd.tensor_copy(XN[:, bass.ds(c * CT, CT), :], xn[:, :, :]).then_inc(m["ln_kept"], 1)
                if n == "1":
                    pool.wait_ge(rows_cleared, 16 * (SLOT_TILES * P // CLEAR))
                pool.wait_ge(m["slots_ready"], 1)
                pool.wait_ge(m["ln_kept"], NCH)
                for k in range(2 * NT):
                    nc.gpsimd.indirect_dma_start(
                        out=rows_in, out_offset=bass.IndirectOffsetOnAxis(ap=slot_of[:, k:k + 1], axis=0),
                        in_=XN[:, k % NT, :], in_offset=None).then_inc(m["scattered"], 16)

                def store(i, r):
                    pool.wait_ge(m["y_biased"], i + 1)
                    pool.dma_start(rows_out[bass.ds(i * P, P), :], y_rows[:, r, :]).then_inc(m[f"stored{r}"], 16)

                with pool.Fori(0, SLOT_TILES // 4) as it:
                    for r in range(4):
                        store(it * 4 + r, r)
                for r in range(4):
                    pool.wait_ge(m[f"stored{r}"], 16 * (SLOT_TILES // 4))
                for k in range(2 * NT):
                    t, which = k // 2, k % 2
                    if k >= 8:
                        pool.wait_ge(m["got_used"], k - 7)
                    nc.gpsimd.indirect_dma_start(
                        out=got[:, k % 8, :], out_offset=None, in_=rows_out,
                        in_offset=bass.IndirectOffsetOnAxis(ap=slot_of[:, which * NT + t:which * NT + t + 1], axis=0)).then_inc(m[f"got{k % 8}"], 16)

        @block.vector
        def _(dve):
            own = Order(dve, dve_own)
            v = nc.vector

            v.memset(ones[:, :], 1.0).then_inc(dve_own, 1)
            own.n = 1
            dve.wait_ge(loaded, 16 * N_LOADS)
            own.settle()
            for dst, src in ((ident_b, "ident"), (causal_b, "causal"), (before_b, "before")):
                own.did(v.tensor_copy(dst[:, :], con(src)))
            own.did(v.memset(ones_b[:, :], 1.0))
            own.did(v.tensor_scalar(kvb_rep[:, :], ones[0:L, :], lat_b[:, 1:2], None, ALU.mult))
            own.did(v.tensor_scalar(wqk_t[:, :], wqk_t[:, :], float(L) ** -0.5, None, ALU.mult))
            own.did(v.tensor_scalar(lat_b[:, 2:3], lat_b[:, 2:3], float(L) ** -0.5, None, ALU.mult))
            own.did(v.tensor_copy(layers["b"]["bias"][:, 1, :], bqk[:, 1, :]))
            own.did(v.tensor_scalar(layers["b"]["bias"][:, 0, :], bqk[:, 0, :], float(HD) ** -0.5, None, ALU.mult))
            for k in range(2):
                own.did(v.memset(pad[k][:, :, :], 0.0))
            own.settle()
            v.memset(scratch1[:, :], 0.0).then_inc(dve_prep, 1)
            dve.wait_ge(pe_prep, 1)
            v.tensor_copy(m_t[:, :], bank[0][0:HD, 0:HD]).then_inc(dve_prep, 1)
            dve.wait_ge(pe_prep, 2)
            own.then(v.tensor_copy(rep[:, :], bank[1][:, 0:104]))
            mask_h = con("head_mask").unsqueeze(2).broadcast_to([P, H, L])
            for k, lo_ in ((0, 0), (2, L)):
                own.did(v.tensor_tensor(blk[k][:, :, :], rep[:, lo_:lo_ + L].unsqueeze(1).broadcast_to([P, H, L]), mask_h, ALU.mult))
            own.did(v.tensor_tensor(wqk_blk[:, :].rearrange("p (j l) -> p j l", j=G),
                                    rep[:, 2 * L:3 * L].unsqueeze(1).broadcast_to([P, G, L]),
                                    con("group_mask").unsqueeze(2).broadcast_to([P, G, L]), ALU.mult))
            own.did(v.tensor_tensor(blk_v[:, :, :], rep[:, 96:104].unsqueeze(1).broadcast_to([P, H, HD]),
                                    con("head_mask").unsqueeze(2).broadcast_to([P, H, HD]), ALU.mult))
            own.settle()
            for k in (0, 2):
                src = blk[k][:, :, :].rearrange("p h (i two) -> p (h i) two", two=2)
                dst = blk[k + 1][:, :, :].rearrange("p h (i two) -> p (h i) two", two=2)
                own.did(v.tensor_scalar(dst[:, :, 0:1], src[:, :, 1:2], -1.0, None, ALU.mult))
                own.did(v.tensor_copy(dst[:, :, 1:2], src[:, :, 0:1]))
            own.did(v.tensor_scalar(blk_vb[:, :, :], blk_v[:, :, :], b3[:, 2:3], None, ALU.mult))
            own.settle()
            v.memset(scratch1[:, :], 0.0).then_inc(dve_prep, 1)
            la, lb = layers["a"], layers["b"]

            def halves(hi, lo_, src):
                own.then(v.tensor_copy(hi, src))
                own.did(v.tensor_tensor(lo_, src, hi.bitcast(F32), ALU.subtract))

            for k in range(4):
                dve.wait_ge(pe_prep, 3 + k)
                halves(la["hi"][k][:, :], la["lo"][k][:, :], bank[k][:, :])
            dve.wait_ge(pe_prep, 7)
            halves(la["v_hi"][:, :], la["v_lo"][:, :], bank[4][:, 0:D])
            own.did(v.tensor_copy(la["v_bias"][:, :], bank[4][:, D:2 * D]))
            own.did(v.tensor_copy(la["bias"][:, :, :], bank[5][:, 0:4 * G].rearrange("p (m g) -> p m g", m=4)))
            own.did(v.tensor_copy(wqk_bias[:, :], bank[5][:, 4 * G:4 * G + 1]))
            dve.wait_ge(pe_prep, 8)
            own.did(v.tensor_copy(la["out_w"][:, :], bank[6][:, 0:D]))
            own.did(v.tensor_copy(lb["out_w"][:, :], bank[6][:, D:2 * D]))
            own.did(v.tensor_scalar(pad[0][:, :, 0:HD], bank[7][:, 0:D].rearrange("p (h d) -> p h d", h=H), float(HD) ** -0.5, None, ALU.mult))
            own.did(v.tensor_copy(pad[1][:, :, 0:HD], bank[7][:, D:2 * D].rearrange("p (h d) -> p h d", h=H)))
            own.settle()
            halves(lb["v_hi"][:, :], lb["v_lo"][:, :], bank[7][:, 2 * D:3 * D])
            for k in range(2):
                halves(lb["hi"][k][:, :], lb["lo"][k][:, :], pad[k][:, :, :].rearrange("p h l -> p (h l)"))
            own.settle()
            v.memset(scratch1[:, :], 0.0).then_inc(dve_prep, 1)

            def layer_norm(m, c, nth):
                first_tile = c * CT
                for t in range(CT):
                    own.did(v.bn_stats(stats[:, t, :], X[:, bass.ds(first_tile + t, 1), :].rearrange("p a d -> p (a d)")))
                own.settle()
                v.memset(scratch2[:, :], 0.0)
                for t in range(CT):
                    own.did(v.bn_aggr(mv[:, t, :], stats[:, t, :]))
                own.settle()
                v.tensor_scalar(var_eps[:, :].unsqueeze(2), mv[:, :, 1:2], EPS, None, ALU.add).then_inc(m["var_ready"], 1)
                dve.wait_ge(m["rstd_ready"], nth)
                for t in range(CT):
                    ins = v.tensor_scalar(xn[:, t, :], X[:, bass.ds(first_tile + t, 1), :].rearrange("p a d -> p (a d)"),
                                          mv[:, t, 0:1], rstd[:, t:t + 1], ALU.subtract, ALU.mult)
                return ins
            LN_OWN = 2 * CT

            def attention(n):
                m, w, steps = att_sems[n], layers[n], Steps(n)
                v.memset(v_aug[:, :, :, :, :].rearrange("p a t h l -> p (a t h) l"), 0.0).then_inc(dve_own, 1)
                own.n += 1
                own.settle()
                own.then(v.memset(v_aug[:, :, :, :, HD:HD + 1].rearrange("p a t h l -> p (a t h) l"), 1.0))

                def step(kind, g, c, par, k):
                    dve.wait_ge(m["shared_ready"], k + 1)
                    free = m["shared_free"]
                    a0, a1 = w_bank[0], w_bank[1]
                    hi_per = 1 + (G if steps.rotary else 2 * G)
                    two = lambda ap: ap.rearrange("p (b s) -> p b s", b=2)
                    if kind == "prep":
                        dve.wait_ge(m["hi_ready"], c * hi_per + 1)
                        v.tensor_tensor(xt_lo[:, :], a0[:, :], xt_hi[:, :].bitcast(F32), ALU.subtract).then_inc(free, 1)
                    elif kind == "value":
                        v.tensor_tensor(v_aug[:, par, :, :, 0:HD], a1[:, :].rearrange("p (t h d) -> p t h d", t=CT, h=H),
                                        w["v_bias"][:, :].rearrange("p (h d) -> p h d", h=H).unsqueeze(1).broadcast_to([P, CT, H, HD]),
                                        ALU.add).then_inc(free, 1)
                    elif kind in ("query", "key") and steps.rotary:
                        dst, w0 = (rope_q, 0) if kind == "query" else (rope_k, 2)
                        if kind == "key" and not (isinstance(c, int) and c == 0 and g == 0):
                            dve.wait_ge(m["key_lo_ready"], c * G + g)
                        for part, (bank_, table) in enumerate(((a0, "cos"), (a1, "sin"))):
                            ins = v.scalar_tensor_tensor(two(dst[:, part, :]), two(bank_[:, :]), w["bias"][:, w0 + part, g:g + 1],
                                                         con(table).unsqueeze(1).broadcast_to([P, 2, S]), ALU.add, ALU.mult)
                        ins.then_inc(free, 1)
                    elif kind in ("query2", "query", "key"):
                        hi, lo_ = (k_hi, k_lo) if kind == "key" else (q_hi, q_lo)
                        at = (g + 1) if kind == "query2" else (2 * g + 1 if kind == "query" else 2 * g + 2)
                        bias = wqk_bias[:, 0:1] if kind == "query2" else w["bias"][:, 0 if kind == "query" else 1, g:g + 1]
                        dve.wait_ge(m["hi_ready"], c * hi_per + (1 + at))
                        v.scalar_tensor_tensor(lo_[:, par, g, :], a0[:, :], bias, hi[:, par, g, :].bitcast(F32),
                                               ALU.add, ALU.subtract).then_inc(free, 1)
                    elif kind == "out_t":
                        v.tensor_copy(y_t[:, :], a0[:, :]).then_inc(free, 1)
                    elif kind == "out":
                        xs = X[:, bass.ds(c * CT, CT), :]
                        own.then(v.tensor_tensor(xs, a1[:, :].rearrange("p (t d) -> p t d", t=CT), xs, ALU.add))
                        v.tensor_tensor(xs, xs, w["out_b"][:, :].unsqueeze(1).broadcast_to([P, CT, D]), ALU.add).then_inc(free, 1)

                def row_max(unit, nb):
                    heads = G if nb == 0 else 2
                    dve.wait_ge(m["scores_ready"], unit * 3 + (nb + 1))
                    v.tensor_reduce(neg_max[:, nb, 0:heads], s_bank[nb][:, :].rearrange("p (h k) -> p h k", h=heads), AX, ALU.max,
                                    negate=True).then_inc(m["max_ready"], 1)

                def copy_o(unit, slot):
                    dve.wait_ge(m["pv_ready"], unit + 1)
                    v.tensor_copy(o_t[:, slot, :], o_bank[:, 0:S]).then_inc(m["o_copied"], 1)

                def normalise(unit, u, par):
                    b_, j = u // G, u % G
                    dve.wait_ge(m["o_ready"], unit + 1)
                    o = o_bank[:, S:2 * S].rearrange("p (q g l) -> p q g l", q=2, g=G)
                    own.then(v.reciprocal(inv_sum[:, :, :].unsqueeze(3), o[:, :, :, HD:HD + 1]))
                    v.tensor_tensor(Y[:, par, 2 * b_:2 * b_ + 2, :].rearrange("p q (g j d) -> p q g j d", g=G, j=G)[:, :, :, j, :],
                                    o[:, :, :, 0:HD], inv_sum[:, :, :].unsqueeze(3).broadcast_to([P, 2, G, HD]),
                                    ALU.mult).then_inc(m["y_ready"], 1)

                layer_norm(m, 0, 1).then_inc(m["ln_ready"], 1)
                for k, (kind, g) in enumerate(steps.all_make()):
                    step(kind, g, 0, 0, k)
                for nb in range(3):
                    row_max(0, nb)

                def period(c, par, first, last):
                    k = steps.before(c)
                    if not last:
                        layer_norm(m, c + 1, c + 2).then_inc(m["ln_ready"], 1)
                    for u in range(UNITS):
                        unit = c * UNITS + u
                        prev = not (first and u == 0)
                        prev_par = par if u else 1 - par
                        for nb in range(3):
                            if nb == 1:
                                dve.wait_ge(m["pt_ready"], unit * 3 + 2)
                                v.tensor_copy(prob_t[:, u % 2, 1, :], t_bank[(3 * u + 1) % 2][:, :]).then_inc(m["pt_copied_dve"], 1)
                            if not (last and u == UNITS - 1):
                                row_max(unit + 1, nb)
                            if nb == 0 and prev:
                                copy_o(unit - 1, (u - 1) % 2)
                            if nb == 2 and prev:
                                normalise(unit - 1, (u - 1) % UNITS, prev_par)
                            for kind, g in steps.at(u, nb, not last, not first):
                                if kind in ("out_t", "out"):
                                    step(kind, g, c - 1, 1 - par, k)
                                else:
                                    step(kind, g, c + 1, 1 - par, k)
                                k = k + 1

                periods(dve, period, own, 2 * (UNITS + LN_OWN + 1))
                end = NCH * UNITS - 1
                copy_o(end, (UNITS - 1) % 2)
                normalise(end, UNITS - 1, 1)
                k = steps.before(NCH - 1) + steps.n_close
                step("out_t", 0, NCH - 1, 1, k)
                step("out", 0, NCH - 1, 1, k + 1)
                dve.wait_ge(m["shared_free"], k + 2)
                v.memset(scratch1[:, :], 0.0).then_inc(attended[n], 1)
                dve.wait_ge(attended[n], 1)

            def experts(n):
                m = moe_sems[n]

                def gate_chunk(c, first):
                    if not first:
                        dve.wait_ge(m["ln_kept"], c)
                        dve.wait_ge(m["lnt_ready"], c)
                    layer_norm(m, c, c + 1).then_inc(m["ln_ready"], 1)
                    dve.wait_ge(m["lnt_ready"], c + 1)
                    v.tensor_copy(xt_plain[:, :], w_bank[0][:, :]).then_inc(m["lnt_copied"], 1)
                    dve.wait_ge(m["logit_ready"], c + 1)
                    v.tensor_tensor(logit[:, bass.ds(c * CT, CT), :], w_bank[1][:, 0:CT * E].rearrange("p (t e) -> p t e", t=CT),
                                    gate_bias[:, :].unsqueeze(1).broadcast_to([P, CT, E]), ALU.add).then_inc(m["logit_copied"], 1)

                gate_chunk(0, True)
                with dve.Fori(1, NCH) as c:
                    own.loop(c - 1, LN_OWN)
                    gate_chunk(c, False)
                own.end(NCH - 1)
                dve.wait_ge(m["logit_copied"], NCH)

                over_t = lambda ap: ap.unsqueeze(1).broadcast_to([P, NT, E])
                over_e = lambda ap: ap.unsqueeze(2).broadcast_to([P, NT, E])
                best, scratch = col[0:2], col[2:5]
                first_hot, second_hot, rest, work, cum_a, cum_b = route

                def choose(values, top, hot):
                    own.then(v.tensor_reduce(top[:, :], values[:, :, :], AX, ALU.max))
                    own.then(v.tensor_tensor(work[:, :, :], values[:, :, :], over_e(top[:, :]), ALU.is_equal))
                    own.then(v.tensor_tensor(work[:, :, :], work[:, :, :], over_t(con("prefer")), ALU.mult))
                    own.then(v.tensor_reduce(scratch[0][:, :], work[:, :, :], AX, ALU.max))
                    own.then(v.tensor_tensor(hot[:, :, :], work[:, :, :], over_e(scratch[0][:, :]), ALU.is_equal))

                choose(logit, best[0], first_hot)
                own.then(v.scalar_tensor_tensor(rest[:, :, :], first_hot[:, :, :], -3e38, logit[:, :, :], ALU.mult, ALU.add))
                choose(rest, best[1], second_hot)
                v.tensor_tensor(scratch[1][:, :], best[1][:, :], best[0][:, :], ALU.subtract).then_inc(m["gap_ready"], 1)
                v.tensor_tensor(chosen_b[:, :, :], first_hot[:, :, :], second_hot[:, :, :], ALU.add).then_inc(m["mask_ready"], 1)
                dve.wait_ge(m["exp_ready"], 1)
                own.then(v.tensor_scalar(scratch[0][:, :], scratch[2][:, :], 1.0, None, ALU.add))
                own.then(v.reciprocal(weight[0][:, :], scratch[0][:, :]))
                own.then(v.tensor_tensor(weight[1][:, :], weight[0][:, :], scratch[2][:, :], ALU.mult))
                dve.wait_ge(m["rank_ready"], 1)
                flat = lambda ap: ap[:, :, :].rearrange("p t e -> p (t e)")
                own.then(v.tensor_copy(flat(cum_a), w_bank[1][:, 0:NT * E]))
                a, b_ = cum_a, cum_b
                shift = 1
                while shift < NT:
                    own.did(v.tensor_copy(b_[:, 0:shift, :], a[:, 0:shift, :]))
                    own.then(v.tensor_tensor(b_[:, shift:NT, :], a[:, shift:NT, :], a[:, 0:NT - shift, :], ALU.add))
                    a, b_ = b_, a
                    shift *= 2
                own.then(v.tensor_scalar(ecol[0][:, :], a[:, NT - 1, :], float(P - 1), None, ALU.add))
                own.then(v.tensor_copy(ecol_i[0][:, :], ecol[0][:, :]))
                own.then(v.tensor_scalar(ecol_i[1][:, :], ecol_i[0][:, :], P.bit_length() - 1, None, ALU.logical_shift_right))
                own.then(v.tensor_copy(ecol[1][:, :], ecol_i[1][:, :]))
                ca, cb = ecol[1], ecol[2]
                spare = [ecol[2], ecol[3], ecol[4]]
                for k, shift in enumerate((1, 2, 4)):
                    cb = spare[k]
                    own.did(v.tensor_copy(cb[:, 0:shift], ca[:, 0:shift]))
                    own.then(v.tensor_tensor(cb[:, shift:E], ca[:, shift:E], ca[:, 0:E - shift], ALU.add))
                    ca = cb
                own.then(v.tensor_tensor(ecol[0][:, :], ca[:, :], ecol[1][:, :], ALU.subtract))
                own.then(v.tensor_scalar(ecol[0][:, :], ecol[0][:, :], float(P), None, ALU.mult))
                own.then(v.tensor_tensor(flat(b_), flat(a), w_bank[1][:, 0:NT * E], ALU.subtract))
                own.then(v.tensor_tensor(flat(a), w_bank[0][:, 0:NT * E], flat(b_), ALU.add))
                own.then(v.tensor_tensor(b_[:, :, :], a[:, :, :], over_t(ecol[0][:, :]), ALU.add))
                for k, hot in enumerate((first_hot, second_hot)):
                    own.then(v.tensor_tensor(work[:, :, :], hot[:, :, :], b_[:, :, :], ALU.mult))
                    own.then(v.tensor_reduce(scratch[0][:, :], work[:, :, :], AX, ALU.add))
                    own.then(v.tensor_copy(slot_of[:, k * NT:(k + 1) * NT], scratch[0][:, :]))
                own.then(v.tensor_tensor(emap_f[:, :, :], con("tile_no", 1).unsqueeze(2).broadcast_to([1, SLOT_TILES, E]),
                                         ca[0:1, :].unsqueeze(1).broadcast_to([1, SLOT_TILES, E]), ALU.is_ge))
                own.then(v.tensor_reduce(emap_s[:, 0, :], emap_f[:, :, :], AX, ALU.add))
                own.then(v.tensor_scalar(emap_s[:, 1, :], emap_s[:, 0, :], float(E - 1), None, ALU.min))
                v.tensor_copy(expert_of[:, :], emap_s[:, 1, :]).then_inc(m["slots_ready"], 1)
                dve.wait_ge(m["slots_ready"], 1)
                dve.wait_ge(m["bias_loaded"], 32)

                def take_rows(i, r):
                    dve.wait_ge(m["xt_ready"], i + 1)
                    v.tensor_copy(xg_t[:, r % 2, :], w_bank[r % 2][:, 0:P]).then_inc(m["xt_copied"], 1)

                def add_b1(i, r, least):
                    e = dve.value_load(expert_of[0:1, bass.ds(i, 1)], min_val=0, max_val=E - 1)
                    dve.wait_ge(m["up_ready"], i + 1)
                    if least >= 2:
                        dve.wait_ge(m["gelu_ready"], i - 1)
                    v.tensor_tensor(pre_act[:, r % 2, :], s_bank[r % 2][:, :], B1[:, bass.ds(e * F, F)], ALU.add).then_inc(m["biased"], 1)

                def add_b2(i, r, least):
                    e = dve.value_load(expert_of[0:1, bass.ds(i, 1)], min_val=0, max_val=E - 1)
                    dve.wait_ge(m["down_ready"], i + 1)
                    if least >= 4:
                        dve.wait_ge(m[f"stored{r}"], stores_before(i, r, least))
                    v.tensor_tensor(y_rows[:, r, :], y_bank[r % 2][:, 0:D], B2[:, bass.ds(e * D, D)], ALU.add).then_inc(m["y_biased"], 1)

                take_rows(0, 0)
                take_rows(1, 1)
                add_b1(0, 0, 0)

                def slot(i, r, least):
                    if least + 1 < SLOT_TILES:
                        add_b1(i + 1, (r + 1) % 4, least + 1)
                    if least + 2 < SLOT_TILES:
                        take_rows(i + 2, (r + 2) % 4)
                    if least >= 1:
                        add_b2(i - 1, (r - 1) % 4, least - 1)

                tile_slots(dve, slot)
                add_b2(SLOT_TILES - 1, 3, SLOT_TILES - 1)
                for k in range(2 * NT):
                    t, which = k // 2, k % 2
                    dve.wait_ge(m[f"got{k % 8}"], 16 * (k // 8 + 1))
                    if which:
                        dve.wait_ge(m["got_used"], k)
                    v.scalar_tensor_tensor(X[:, t, :], got[:, k % 8, :], weight[which][:, t:t + 1], X[:, t, :],
                                           ALU.mult, ALU.add).then_inc(m["got_used"], 1)
                dve.wait_ge(m["got_used"], 2 * NT)

            attention("a")
            experts("1")
            attention("b")
            experts("2")

        @block.scalar
        def _(act):
            s = nc.scalar

            def attention(n):
                m, w, steps = att_sems[n], layers[n], Steps(n)
                hi_per = 1 + (G if steps.rotary else 2 * G)

                def probs(unit, nb):
                    heads, width = (G, P) if nb == 0 else (2, S)
                    act.wait_ge(m["max_ready"], unit * 3 + (nb + 1))
                    for h in range(heads):
                        cols = slice(h * width, (h + 1) * width)
                        ins = s.activation(prob[:, nb, cols], s_bank[nb][:, cols], ACT.Exp, bias=neg_max[:, nb, h:h + 1])
                    ins.then_inc(m["probs_ready"], 1)

                def copy_t(unit, u, nb):
                    act.wait_ge(m["pt_ready"], unit * 3 + (nb + 1))
                    s.activation(prob_t[:, u % 2, nb, :], t_bank[(3 * u + nb) % 2][:, :], ACT.Copy).then_inc(m["pt_copied_act"], 1)

                def step(kind, g, c, par, k):
                    if kind == "prep":
                        act.wait_ge(m["shared_ready"], k + 1)
                        s.activation(xt_hi[:, :], w_bank[0][:, :], ACT.Copy).then_inc(m["hi_ready"], 1)
                    elif kind == "query2" or (kind in ("query", "key") and not steps.rotary):
                        hi = k_hi if kind == "key" else q_hi
                        bias = wqk_bias[:, 0:1] if kind == "query2" else w["bias"][:, 0 if kind == "query" else 1, g:g + 1]
                        act.wait_ge(m["shared_ready"], k + 1)
                        s.activation(hi[:, par, g, :], w_bank[0][:, :], ACT.Identity, bias=bias).then_inc(m["hi_ready"], 1)
                        if kind == "query2":
                            act.wait_ge(m["rope_summed"], c * 2 * G + (2 * g + 2))
                            s.activation(k_hi[:, par, g, :], rope_k[:, 0, :], ACT.Copy).then_inc(m["key_hi_ready"], 1)

                for k, (kind, g) in enumerate(steps.all_make()):
                    step(kind, g, 0, 0, k)
                for nb in range(3):
                    probs(0, nb)

                def period(c, par, first, last):
                    k = steps.before(c)
                    for u in range(UNITS):
                        unit = c * UNITS + u
                        for nb in range(3):
                            if nb != 1:
                                copy_t(unit, u, nb)
                            if not (last and u == UNITS - 1):
                                probs(unit + 1, nb)
                            for kind, g in steps.at(u, nb, not last, not first):
                                step(kind, g, c + 1, 1 - par, k)
                                k = k + 1

                periods(act, period)

            def experts(n):
                m = moe_sems[n]
                act.wait_ge(m["gap_ready"], 1)
                s.activation(col[4][:, :], col[3][:, :], ACT.Exp).then_inc(m["exp_ready"], 1)

                def gelu(i, r, least):
                    act.wait_ge(m["biased"], i + 1)
                    if least >= 2:
                        act.wait_ge(m["ht_ready"], i - 1)
                    s.activation(hid[:, r % 2, :], pre_act[:, r % 2, :], ACT.Gelu).then_inc(m["gelu_ready"], 1)

                def copy_ht(i, r, least):
                    act.wait_ge(m["ht_ready"], i + 1)
                    if least >= 2:
                        act.wait_ge(m["down_ready"], i - 1)
                    s.activation(hid_t[:, r % 2, :], t_bank[r % 2][:, :], ACT.Copy).then_inc(m["ht_copied"], 1)

                gelu(0, 0, 0)

                def slot(i, r, least):
                    if least + 1 < SLOT_TILES:
                        gelu(i + 1, (r + 1) % 4, least + 1)
                    copy_ht(i, r, least)

                tile_slots(act, slot)

            attention("a")
            experts("1")
            attention("b")
            experts("2")

        @block.tensor
        def _(pe):
            t_ = nc.tensor

            pe.wait_ge(dve_prep, 1)
            t_.matmul(bank[0][0:HD, 0:HD], kv2l_n[:, :], l2o_t[:, :], start=True, stop=True).then_inc(pe_prep, 1)
            pe.wait_ge(dve_prep, 2)
            for k, (lhs, rhs) in enumerate(((con("rep8", HD), q2l_t), (con("rep8", HD), kv2l_t), (con("rep32", L), wqk_t))):
                t_.matmul(bank[1][:, k * L:(k + 1) * L], lhs, rhs[:, :], start=True, stop=True)
            t_.matmul(bank[1][:, 3 * L:3 * L + HD], con("rep8", HD), m_t[:, :], start=True, stop=True).then_inc(pe_prep, 1)
            pe.wait_ge(dve_prep, 3)
            for k in range(4):
                t_.matmul(bank[k][:, :], cw[:, k // 2, :], blk[k][:, :, :].rearrange("p h l -> p (h l)"), start=True, stop=True).then_inc(pe_prep, 1)
            t_.matmul(bank[4][:, 0:D], cw[:, 2, :], blk_v[:, :, :].rearrange("p h d -> p (h d)"), start=True, stop=True)
            t_.matmul(bank[4][:, D:2 * D], ones[:, :], blk_vb[:, :, :].rearrange("p h d -> p (h d)"), start=True, stop=False)
            t_.matmul(bank[4][:, D:2 * D], kvb_rep[:, :], l2o_t[:, :].unsqueeze(1).broadcast_to([L, H, HD]), start=False, stop=False)
            t_.matmul(bank[4][:, D:2 * D], ones[0:1, :], l2o_row[:, :].unsqueeze(1).broadcast_to([1, H, HD]), start=False, stop=True)
            for k in range(4):
                for g in range(G):
                    o = bank[5][:, k * G + g:k * G + g + 1]
                    t_.matmul(o, blk[k][:, g * G:(g + 1) * G, :].rearrange("p h l -> p (h l)"), b3[:, k // 2:k // 2 + 1], start=True, stop=False)
                    t_.matmul(o, con("rot32" if k % 2 else "rep32", L), lat_b[:, k // 2:k // 2 + 1], start=False, stop=True)
            t_.matmul(bank[5][:, 4 * G:4 * G + 1], con("rep32", L), lat_b[:, 2:3], start=True, stop=True).then_inc(pe_prep, 1)
            for dst, src in ((bank[6][:, 0:D], cp[:, :]), (bank[6][:, D:2 * D], wb[:, 3, :]), (bank[7][:, 0:D], wb[:, 0, :]),
                             (bank[7][:, D:2 * D], wb[:, 1, :]), (bank[7][:, 2 * D:3 * D], wb[:, 2, :])):
                ins = t_.transpose(dst, src, ident)
            ins.then_inc(pe_prep, 1)
            pe.wait_ge(dve_prep, 4)

            def product(o, w_hi, w_lo, x_hi, x_lo, start=True):
                t_.matmul(o, w_hi, x_hi, start=start, stop=False, skip_group_check=True)
                t_.matmul(o, w_lo, x_hi, start=False, stop=False, skip_group_check=True)
                return t_.matmul(o, w_hi, x_lo, start=False, stop=True, skip_group_check=True)

            def attention(n):
                m, w, steps = att_sems[n], layers[n], Steps(n)
                made_end = lambda c: steps.before(c) + (steps.n_make if isinstance(c, int) and c == 0 else steps.n_make + steps.n_close)

                def step(kind, g, c, par, k):
                    if not (isinstance(k, int) and k == 0):
                        pe.wait_ge(m["shared_free"], k)
                    a0, a1 = w_bank[0], w_bank[1]
                    if kind == "prep":
                        pe.wait_ge(m["ln_ready"], c + 1)
                        for t in range(CT):
                            ins = t_.transpose(a0[:, t * P:(t + 1) * P], xn[:, t, :], ident)
                    elif kind == "value":
                        for t in range(CT):
                            cols = slice(t * P, (t + 1) * P)
                            ins = product(a1[:, cols], xt_hi[:, cols], xt_lo[:, cols], w["v_hi"][:, :], w["v_lo"][:, :])
                    elif kind in ("query", "key"):
                        mats = (((a0, 0), (a1, 1)) if kind == "query" else ((a0, 2), (a1, 3))) if steps.rotary else ((a0, 0 if kind == "query" else 1),)
                        cols = slice(g * P, (g + 1) * P)
                        for bank_, k_ in mats:
                            ins = product(bank_[:, :], w["hi"][k_][:, cols], w["lo"][k_][:, cols], xt_hi[:, :], xt_lo[:, :])
                    elif kind == "query2":
                        pe.wait_ge(m["rope_summed"], c * 2 * G + (2 * g + 1))
                        ins = t_.matmul(a0[:, :], wqk_blk[:, :], rope_q[:, 0, :], start=True, stop=True)
                    elif kind == "out_t":
                        for t in range(CT):
                            ins = t_.transpose(a0[:, t * P:(t + 1) * P], Y[:, par, t, :], ident)
                    elif kind == "out":
                        for t in range(CT):
                            ins = t_.matmul(a1[:, t * P:(t + 1) * P], y_t[:, t * P:(t + 1) * P], w["out_w"][:, :], start=True, stop=True)
                    ins.then_inc(m["shared_ready"], 1)

                def scores(u, par, nb):
                    b_, j = u // G, u % G
                    rows = slice(j * L, (j + 1) * L)
                    heads = range(G) if nb == 0 else range(2 * nb - 2, 2 * nb)
                    width = P if nb == 0 else S
                    q0 = b_ * S + (0 if nb == 0 else P)
                    for k, g in enumerate(heads):
                        kk = slice(b_ * S, b_ * S + width)
                        product(s_bank[nb][:, k * width:(k + 1) * width], q_hi[rows, par, g, q0:q0 + P], q_lo[rows, par, g, q0:q0 + P],
                                k_hi[rows, par, g, kk], k_lo[rows, par, g, kk], start=(k == 0))
                    o = s_bank[nb][:, :].rearrange("p (h k) -> p h k", h=len(heads))[:, :, width - P:width]
                    t_.matmul(o, ident_b[:, :], causal_b[:, :].unsqueeze(1).broadcast_to([P, len(heads), P]), start=False, stop=True,
                              skip_group_check=True).then_inc(m["scores_ready"], 1)

                def transposes(unit, u, nb, first):
                    pe.wait_ge(m["probs_ready"], unit * 3 + (nb + 1))
                    if nb == 0 and not first:
                        pe.wait_ge(m["pt_copied_dve"], unit)
                    elif nb == 1 and not first:
                        pe.wait_ge(m["pt_copied_act"], unit * 2)
                    elif nb == 2:
                        pe.wait_ge(m["pt_copied_act"], unit * 2 + 1)
                    for k in range(4):
                        cols = slice(k * P, (k + 1) * P)
                        ins = t_.transpose(t_bank[(3 * u + nb) % 2][:, cols], prob[:, nb, cols], ident)
                    ins.then_inc(m["pt_ready"], 1)

                def weighted(unit, u, par, first):
                    b_, j = u // G, u % G
                    pe.wait_ge(m["pt_copied_dve"], unit + 1)
                    pe.wait_ge(m["pt_copied_act"], unit * 2 + 2)
                    if not first:
                        pe.wait_ge(m["y_ready"], unit)
                    pt = prob_t[:, u % 2, :, :]
                    for q, kb in ((0, 0), (1, 0), (1, 1)):
                        for g in range(G):
                            if q == 0:
                                rhs = pt[:, 0, g * P:(g + 1) * P]
                            else:
                                at = ((g % 2) * 2 + kb) * P
                                rhs = pt[:, 1 + g // 2, at:at + P]
                            ins = t_.matmul(o_bank[g * L:(g + 1) * L, q * P:(q + 1) * P], v_aug[:, par, 2 * b_ + kb, g * G + j, :], rhs,
                                            start=(q == 0), stop=(kb == q), skip_group_check=True)
                    ins.then_inc(m["pv_ready"], 1)

                def turn_back(unit, u):
                    pe.wait_ge(m["o_copied"], unit + 1)
                    for q in range(2):
                        ins = t_.transpose(o_bank[:, S + q * P:S + (q + 1) * P], o_t[:, u % 2, q * P:(q + 1) * P], ident)
                    ins.then_inc(m["o_ready"], 1)

                def operands(c_next, k_end):
                    pe.wait_ge(m["shared_free"], k_end)
                    if steps.rotary:
                        pe.wait_ge(m["key_lo_ready"], c_next * G + G)

                for k, (kind, g) in enumerate(steps.all_make()):
                    step(kind, g, 0, 0, k)
                operands(0, steps.n_make)
                for nb in range(3):
                    scores(0, 0, nb)

                def period(c, par, first, last):
                    k = steps.before(c)
                    for u in range(UNITS):
                        unit = c * UNITS + u
                        prev = not (first and u == 0)
                        prev_par = par if u else 1 - par
                        for nb in range(3):
                            transposes(unit, u, nb, first and u == 0)
                            if u < UNITS - 1:
                                scores(u + 1, par, nb)
                            elif not last:
                                if nb == 0:
                                    operands(c + 1, made_end(c))
                                scores(0, 1 - par, nb)
                            if nb == 0 and prev:
                                weighted(unit - 1, (u - 1) % UNITS, prev_par, first and u == 1)
                            if nb == 2 and prev:
                                turn_back(unit - 1, (u - 1) % UNITS)
                            for kind, g in steps.at(u, nb, not last, not first):
                                step(kind, g, c - 1 if kind in ("out_t", "out") else c + 1, 1 - par, k)
                                k = k + 1

                periods(pe, period)
                end = NCH * UNITS - 1
                weighted(end, UNITS - 1, 1, False)
                turn_back(end, UNITS - 1)
                pe.wait_ge(m["y_ready"], end + 1)
                k = steps.before(NCH - 1) + steps.n_close
                step("out_t", 0, NCH - 1, 1, k)
                step("out", 0, NCH - 1, 1, k + 1)

            def experts(n):
                m = moe_sems[n]
                if n == "1":
                    pe.wait_ge(experts_loaded, 32)

                def gate_chunk(c, first):
                    pe.wait_ge(m["ln_ready"], c + 1)
                    if first:
                        pe.wait_ge(attended["a" if n == "1" else "b"], 1)
                    for t in range(CT):
                        ins = t_.transpose(w_bank[0][:, t * P:(t + 1) * P], xn[:, t, :], ident)
                    ins.then_inc(m["lnt_ready"], 1)
                    pe.wait_ge(m["lnt_copied"], c + 1)
                    if not first:
                        pe.wait_ge(m["logit_copied"], c)
                    for t in range(CT):
                        ins = t_.matmul(w_bank[1][:, t * E:(t + 1) * E], xt_plain[:, t * P:(t + 1) * P], gate[:, :], start=True, stop=True)
                    ins.then_inc(m["logit_ready"], 1)

                gate_chunk(0, True)
                with pe.Fori(1, NCH) as c:
                    gate_chunk(c, False)
                pe.wait_ge(m["mask_ready"], 1)
                mask = chosen_b[:, :, :].rearrange("p t e -> p (t e)")
                t_.matmul(w_bank[0][:, 0:NT * E], before_b[:, :], mask, start=True, stop=True)
                t_.matmul(w_bank[1][:, 0:NT * E], ones_b[:, :], mask, start=True, stop=True).then_inc(m["rank_ready"], 1)
                pe.wait_ge(m["slots_ready"], 1)

                def turn_rows(i, r, least):
                    pe.wait_ge(m[f"row{r}"], loads_until(i, r, least))
                    if least >= 2:
                        pe.wait_ge(m["xt_copied"], i - 1)
                    t_.transpose(w_bank[r % 2][:, 0:P], xg[:, r, :], ident).then_inc(m["xt_ready"], 1)

                def up(i, r, least):
                    e = pe.value_load(expert_of[0:1, bass.ds(i, 1)], min_val=0, max_val=E - 1)
                    pe.wait_ge(m["xt_copied"], i + 1)
                    if least >= 2:
                        pe.wait_ge(m["biased"], i - 1)
                    t_.matmul(s_bank[r % 2][:, :], xg_t[:, r % 2, :], W1[:, bass.ds(e * F, F)], start=True, stop=True).then_inc(m["up_ready"], 1)

                def turn_hidden(i, r, least):
                    pe.wait_ge(m["gelu_ready"], i + 1)
                    if least >= 2:
                        pe.wait_ge(m["ht_copied"], i - 1)
                    for k in range(FT):
                        ins = t_.transpose(t_bank[r % 2][:, k * P:(k + 1) * P], hid[:, r % 2, k * P:(k + 1) * P], ident)
                    ins.then_inc(m["ht_ready"], 1)

                def down(i, r, least):
                    e = pe.value_load(expert_of[0:1, bass.ds(i, 1)], min_val=0, max_val=E - 1)
                    pe.wait_ge(m["ht_copied"], i + 1)
                    if least >= 2:
                        pe.wait_ge(m["y_biased"], i - 1)
                    for k in range(FT):
                        ins = t_.matmul(y_bank[r % 2][:, 0:D], hid_t[:, r % 2, k * P:(k + 1) * P],
                                        W2[:, bass.ds(e * (FT * D) + k * D, D)], start=(k == 0), stop=(k == FT - 1))
                    ins.then_inc(m["down_ready"], 1)

                turn_rows(0, 0, 0)
                turn_rows(1, 1, 1)
                up(0, 0, 0)

                def slot(i, r, least):
                    if least + 1 < SLOT_TILES:
                        up(i + 1, (r + 1) % 4, least + 1)
                    if least + 2 < SLOT_TILES:
                        turn_rows(i + 2, (r + 2) % 4, least + 2)
                    turn_hidden(i, r, least)
                    if least >= 1:
                        down(i - 1, (r - 1) % 4, least - 1)

                tile_slots(pe, slot)
                down(SLOT_TILES - 1, 3, SLOT_TILES - 1)

            attention("a")
            experts("1")
            attention("b")
            experts("2")


_INS = ["L0_attn_a_x"] + [f"L0_attn_a_{k}" for k in (
    "c_attn_w", "c_attn_b", "q2l_w", "q2l_b", "kv2l_w", "kv2l_b", "l2o_w", "l2o_b", "wqk_w", "wqk_b", "cproj_w", "cproj_b")] + [
    f"L0_attn_b_{k}" for k in ("Wq", "bq", "Wk", "bk", "Wv", "bv", "Wo", "bo")] + [
    f"L0_ffn_{k}" for k in ("gate_w", "gate_b", "w1", "b1", "w2", "b2")]
_OUTS = [((B, S, D), "float32")]


def kernel(**inputs):
    import numpy as _np
    import concourse.bacc as _bacc
    from concourse import mybir as _mybir
    from concourse.bass_utils import run_bass_kernel_spmd as _run

    nc = _bacc.Bacc("TRN2", target_bir_lowering=False, num_devices=1)
    arrays, args = {}, []
    for name in _INS:
        a = _np.ascontiguousarray(inputs[name])
        arrays[f"in_{name}_dram"] = a
        args.append(nc.dram_tensor(f"in_{name}_dram", a.shape, _mybir.dt.from_np(a.dtype), kind="ExternalInput").ap())
    arrays["const_dram"] = constants()
    args.append(nc.dram_tensor("const_dram", (P, CONST_W), F32, kind="ExternalInput").ap())
    for i, (shape, dtype) in enumerate(_OUTS):
        dt = _mybir.dt.from_np(_np.dtype(dtype))
        args.append(nc.dram_tensor(f"out_{i}_dram", shape, dt, kind="ExternalOutput").ap())
    program(nc, *args)
    r = _run(nc, [arrays], core_ids=[0])
    return r.results[0]["out_0_dram"]
```

```python
from contextlib import ExitStack

import numpy as np

import concourse.bass as bass
from concourse import mybir

F32 = mybir.dt.float32
F32R = mybir.dt.float32r
BF16 = mybir.dt.bfloat16
I32 = mybir.dt.int32
ALU = mybir.AluOpType
ACT = mybir.ActivationFunctionType
AX = mybir.AxisListType.X

P = 128
B, S, D = 16, 256, 128
T = B * S
NT = T // P
H, HD, L = 16, 8, 32
G = 4
CH = 512
NCH = T // CH
CT = CH // P
UNITS = 8
E, F = 8, 512
FT = F // P
ROWS = 256
RB = ROWS // P
TILES = 2 * T // ROWS + E - 1
BLOCKS = TILES * RB
EPS = 1e-5
MASKED = -1e30

_COLS = {}
_at = 0
for _name, _n in (("ident", P), ("cos", S), ("sin", S), ("block_no", BLOCKS), ("lane_no", P), ("token_no", NT), ("prefer", E),
                  ("stack", 2),
                  ("head_mask", H), ("group_mask", G), ("rep8", P), ("rep32", P), ("rot32", P), ("causal", P), ("before", P)):
    _COLS[_name] = (_at, _at + _n)
    _at += _n
CONST_W = _at
KEPT_W = _COLS["head_mask"][0]


def constants():
    c = np.zeros((P, CONST_W), np.float32)

    def put(name, a):
        c[:a.shape[0], _COLS[name][0]:_COLS[name][1]] = a

    p = np.arange(P)
    put("ident", np.eye(P, dtype=np.float32))
    put("head_mask", (p[:, None] // HD == np.arange(H)).astype(np.float32))
    put("group_mask", (p[:, None] // L == np.arange(G)).astype(np.float32))
    put("rep8", (np.arange(HD)[:, None] == p % HD).astype(np.float32))
    put("rep32", (np.arange(L)[:, None] == p % L).astype(np.float32))
    rot = np.zeros((L, P), np.float32)
    for q in range(P):
        l = q % L
        rot[l + 1 if l % 2 == 0 else l - 1, q] = -1.0 if l % 2 == 0 else 1.0
    put("rot32", rot)
    inv = (np.float32(1.0) / np.power(np.float32(10000.0), np.arange(0, L, 2, dtype=np.float32) / np.float32(L))).astype(np.float32)
    ang = np.outer(np.arange(S, dtype=np.float32), inv).astype(np.float32)
    cos = np.repeat(np.cos(ang), 2, axis=1).T
    sin = np.repeat(np.sin(ang), 2, axis=1).T
    put("cos", np.tile(cos, (G, 1)).astype(np.float32))
    put("sin", np.tile(sin, (G, 1)).astype(np.float32))
    put("causal", np.where(np.arange(P)[None, :] > p[:, None], np.float32(MASKED), np.float32(0)))
    put("before", (p[:, None] < np.arange(P)[None, :]).astype(np.float32))
    put("block_no", np.broadcast_to(np.arange(BLOCKS, dtype=np.float32), (P, BLOCKS)))
    put("lane_no", np.broadcast_to(np.arange(P, dtype=np.float32), (P, P)))
    put("token_no", (p[:, None] + P * np.arange(NT) + 1).astype(np.float32))
    octet = p % L // HD
    put("stack", np.stack([-1.0 * (octet == 2), -1.0 * (octet == 1)], axis=1).astype(np.float32))
    put("prefer", np.broadcast_to(E - np.arange(E, dtype=np.float32), (P, E)))
    return c


class Order:

    def __init__(self, eng, sem):
        self.eng, self.sem, self.base, self.n = eng, sem, 0, 0

    def did(self, ins):
        self.n += 1
        return ins.then_inc(self.sem, 1)

    def settle(self):
        self.eng.wait_ge(self.sem, self.n + self.base)

    def then(self, ins):
        self.did(ins)
        self.settle()

    def loop(self, i, per):
        self.outside, self.per = self.n, per
        self.base, self.n = i * per + self.outside, 0

    def end(self, iterations):
        assert self.n == self.per, (self.n, self.per)
        self.base, self.n = 0, self.outside + iterations * self.per


class Steps:

    def __init__(self, layer):
        self.rotary = layer == "a"
        self.make = {(1, 2): [("prep", 0)], (2, 0): [("value", 0)]}
        for g in range(G):
            self.make[(2 + g, 1)] = [("query", g)]
            self.make[(2 + g, 2)] = [("key", g)]
            if self.rotary:
                self.make[(3 + g, 0)] = [("query2", g)]
        self.last_made = ("query2" if self.rotary else "key", G - 1)
        self.close = {(1, 0): [("out_t", 0)], (1, 1): [("out", 0)], (7, 0): [("gate_t", 0)], (7, 1): [("gate", 0)]}
        self.hi_per = 1 + (G if self.rotary else 2 * G)
        self.add = {} if self.rotary else {(0, 0): range(0, CT), (0, 1): range(CT, 2 * CT)}
        self.norm = ((0, 0), (0, 2)) if self.rotary else ((0, 2), (1, 0))
        self.gate_norm = ((5, 0), (6, 1))
        self.n_make, self.n_close = sum(map(len, self.make.values())), sum(map(len, self.close.values()))

    def at(self, u, nb, make, close):
        return (self.make.get((u, nb), []) if make else []) + (self.close.get((u, nb), []) if close else [])

    def all_make(self):
        return [s for k in sorted(self.make) for s in self.make[k]]

    def made(self, c, step):
        if isinstance(c, int) and c == 0:
            return self.all_make().index(step) + 1
        closing = not (isinstance(c, int) and c == 1)
        order = [s for u in range(UNITS) for nb in range(3) for s in self.at(u, nb, True, closing)]
        return self.before(c - 1) + (order.index(step) + 1)

    def before(self, c):
        if isinstance(c, int) and c == 0:
            return self.n_make
        return (c - 1) * (self.n_make + self.n_close) + 2 * self.n_make


def periods(eng, period, own=None, per=0):
    period(0, 0, True, False)
    with eng.Fori(0, NCH // 2 - 1) as i:
        if own:
            own.loop(i, per)
        period(i * 2 + 1, 1, False, False)
        period(i * 2 + 2, 0, False, False)
    if own:
        own.end(NCH // 2 - 1)
    period(NCH - 1, 1, False, True)


def stores_before(i, r):
    return 16 * (i // 4) if isinstance(i, int) else i * 4 - 4 * r


CLOSING = ("out_t", "out", "gate_t", "gate")


def hot_tiles(eng, do):
    for t in (0, 1):
        for k in (0, 1):
            do(t, k, 2 * t + k)
    with eng.Fori(0, NT // 2 - 2) as i:
        for t in (2, 3):
            for k in (0, 1):
                do(i * 2 + t, k, i * 4 + (2 * t + k))
    for t in (NT - 2, NT - 1):
        for k in (0, 1):
            do(t, k, 2 * t + k)


def norm_no(c):
    return c + 1 if isinstance(c, int) and c < 2 else c * 2 - 1


def gate_norm_no(c):
    return (2 * NCH - 1 if c == NCH - 2 else 2 * NCH) if isinstance(c, int) and c >= NCH - 2 else c * 2 + 4


PEEL = 7
assert (TILES - 4 - PEEL) % 4 == 0


def tile_slots(eng, slot):
    for i in range(PEEL):
        slot(i, i % 4, i)
    with eng.Fori(0, (TILES - 4 - PEEL) // 4) as it:
        for r in range(4):
            slot(it * 4 + (PEEL + r), (PEEL + r) % 4, PEEL + r)
    for i in range(TILES - 4, TILES):
        slot(i, i % 4, i)


def program(nc, x, c_attn_w, c_attn_b, q2l_w, q2l_b, kv2l_w, kv2l_b, l2o_w, l2o_b, wqk_w, wqk_b, cproj_w, cproj_b,
            Wq, bq, Wk, bk, Wv, bv, Wo, bo, gate_w, gate_b, w1, b1, w2, b2, const, out):
    x_tiles = x.rearrange("b s d -> (b s) d").rearrange("(t p) d -> p t d", p=P)
    out_tiles = out.rearrange("b s d -> (b s) d").rearrange("(t p) d -> p t d", p=P)
    normed = nc.dram_tensor("normed", [T, D], F32, kind="Internal").ap()
    normed_tiles = normed.rearrange("(t p) d -> p t d", p=P)
    rows_out = nc.dram_tensor("expert_rows", [TILES * ROWS, D], F32, kind="Internal").ap()

    with ExitStack() as ctx:
        def sb(name, shape, dt=F32, scope=ctx):
            return scope.enter_context(nc.sbuf_tensor(name, shape, dt))

        def sem(name):
            return ctx.enter_context(nc.semaphore(name))

        X = sb("X", [P, NT, D])
        C = sb("C", [P, KEPT_W])
        ident = C[:, _COLS["ident"][0]:_COLS["ident"][1]]

        def con(name, rows=P):
            at, end = _COLS[name]
            return C[0:rows, at:end] if end <= KEPT_W else C_prep[0:rows, at - KEPT_W:end - KEPT_W]

        ident_b = sb("ident_b", [P, P], BF16)
        causal_b = sb("causal_b", [P, P], BF16)
        before_b = sb("before_b", [P, P], BF16)
        ones_b = sb("ones_b", [P, P], BF16)
        W1 = sb("W1", [P, E * F])
        W2 = sb("W2", [P, E * FT * D])
        gate = sb("gate", [P, E])
        gate_bias = sb("gate_bias", [P, E])
        stats = sb("stats", [P, CT, 6])
        mv = sb("mv", [P, CT, 2])
        rstd = sb("rstd", [P, CT])
        var_eps = sb("var_eps", [P, CT])
        scratch1 = sb("scratch1", [1, 1])
        scratch2 = sb("scratch2", [1, 1])
        neg_half = sb("neg_half", [P, CT])
        xn = sb("xn", [P, CT, D])
        layers = {}
        for name, n_mats in (("a", 4), ("b", 2)):
            layers[name] = dict(
                hi=[sb(f"{name}_proj{m}_hi", [P, H * L], F32R) for m in range(n_mats)],
                lo=[sb(f"{name}_proj{m}_lo", [P, H * L], F32R) for m in range(n_mats)],
                v_hi=sb(f"{name}_v_hi", [P, D], F32R), v_lo=sb(f"{name}_v_lo", [P, D], F32R),
                bias=sb(f"{name}_bias", [P, n_mats, G]), v_bias=sb(f"{name}_v_bias", [P, D]),
                out_w=sb(f"{name}_out_w", [P, D]), out_b=sb(f"{name}_out_b", [P, D]))
        wqk_blk = sb("wqk_blk", [P, P])
        wqk_bias = sb("wqk_bias", [P, 1])
        b1_cols = sb("b1_cols", [P, E * FT])
        logit = sb("logit", [P, NT, E])
        slot_of = sb("slot_of", [P, 2 * NT], I32)
        weight = [sb(f"weight{k}", [P, NT]) for k in range(2)]
        got = sb("got", [P, 2 * CT, D])

        with ExitStack() as att:
            xt_hi = sb("xt_hi", [P, CH], F32R, att)
            xt_lo = sb("xt_lo", [P, CH], F32R, att)
            q_hi = sb("q_hi", [P, 2, G, CH], F32R, att)
            q_lo = sb("q_lo", [P, 2, G, CH], F32R, att)
            k_hi = sb("k_hi", [P, 2, G, CH], F32R, att)
            k_lo = sb("k_lo", [P, 2, G, CH], F32R, att)
            prob = sb("prob", [P, 3, 512], F32, att)
            prob_t = sb("prob_t", [P, 2, 3, 512], F32, att)
            v_aug = sb("v_aug", [P, 2, CT, H, L], F32, att)
            o_t = sb("o_t", [P, S], F32, att)
            Y = sb("Y", [P, 2, CT, D], F32, att)
            y_t = sb("y_t", [P, CH], F32, att)
            rope_q = sb("rope_q", [P, 2, CH], F32, att)
            rope_k = sb("rope_k", [P, 2, CH], F32, att)
            neg_max = sb("neg_max", [P, 3, G], F32, att)
            inv_sum = sb("inv_sum", [P, 2, G], F32, att)
        with ExitStack() as moe:
            xg = sb("xg", [P, 4, RB, D], F32, moe)
            xg_hi = sb("xg_hi", [P, 2, ROWS], F32R, moe)
            xg_lo = sb("xg_lo", [P, 2, ROWS], F32R, moe)
            w1_hi = sb("w1_hi", [P, 2, F], F32R, moe)
            w1_lo = sb("w1_lo", [P, 2, F], F32R, moe)
            hid = sb("hid", [P, 2, FT, ROWS], F32, moe)
            b2_rows = sb("b2_rows", [P, E, D], F32, moe)
            y_rows = sb("y_rows", [P, 4, RB, D], F32, moe)
            route = [sb(f"route{k}", [P, NT, E], F32, moe) for k in range(6)]
            chosen_b = sb("chosen_b", [P, NT, E], BF16, moe)
            col = [sb(f"col{k}", [P, NT], F32, moe) for k in range(5)]
            ecol = [sb(f"ecol{k}", [P, E], F32, moe) for k in range(5)]
            ecol_i = [sb(f"ecol_i{k}", [P, E], I32, moe) for k in range(2)]
            slot_f = sb("slot_f", [P, 2 * NT], F32, moe)
            block_i = sb("block_i", [P, 2 * NT], I32, moe)
            block_f = sb("block_f", [P, 2 * NT], F32, moe)
            lane_f = sb("lane_f", [P, 2 * NT], F32, moe)
            lane_hot = sb("lane_hot", [P, 4, P], F32R, moe)
            block_hot = sb("block_hot", [P, 4, BLOCKS], F32R, moe)
            source_f = sb("source_f", [P, 2, BLOCKS], F32, moe)
            source = sb("source", [P, BLOCKS], I32, moe)
            emap_f = sb("emap_f", [1, TILES, E], F32, moe)
            emap_s = sb("emap_s", [1, 2, TILES], F32, moe)
            expert_of = sb("expert_of", [1, TILES], I32, moe)
        with ExitStack() as prep:
            C_prep = sb("C_prep", [P, CONST_W - KEPT_W], F32, prep)
            cw = sb("cw", [P, 3, D], F32, prep)
            cp = sb("cp", [P, D], F32, prep)
            wb = sb("wb", [P, 4, D], F32, prep)
            q2l_t = sb("q2l_t", [HD, L], F32, prep)
            kv2l_t = sb("kv2l_t", [HD, L], F32, prep)
            kv2l_n = sb("kv2l_n", [L, HD], F32, prep)
            l2o_t = sb("l2o_t", [L, HD], F32, prep)
            wqk_t = sb("wqk_t", [L, L], F32, prep)
            b3 = sb("b3", [P, 3], F32, prep)
            lat_b = sb("lat_b", [L, 3], F32, prep)
            l2o_row = sb("l2o_row", [1, HD], F32, prep)
            rep = sb("rep", [P, 104], F32, prep)
            m_t = sb("m_t", [HD, HD], F32, prep)
            blk = [sb(f"blk{k}", [P, H, L], F32, prep) for k in range(4)]
            blk_v = sb("blk_v", [P, H, HD], F32, prep)
            blk_vb = sb("blk_vb", [P, H, HD], F32, prep)
            kvb_rep = sb("kvb_rep", [L, P], F32, prep)
            ones = sb("ones", [P, P], F32, prep)
            pad = [sb(f"pad{k}", [P, H, L], F32, prep) for k in range(2)]
            bqk = sb("bqk", [P, 2, G], F32, prep)

        bank = [ctx.enter_context(nc.psum_tensor(f"bank{k}", [P, 512], F32)) for k in range(8)]
        s_bank, t_bank, o_bank, w_bank = bank[0:3], bank[3:5], bank[5], bank[6:8]
        r_bank, h_bank, y_bank = bank[6:8], (bank[0:2], bank[2:4]), bank[4:6]

        loaded = sem("loaded")
        experts_loaded = sem("experts_loaded")
        zeroed = sem("zeroed")
        pe_prep = sem("pe_prep")
        dve_prep = sem("dve_prep")
        dve_own = sem("dve_own")
        att_sems = {n: {k: sem(f"{n}_{k}") for k in (
            "scores_ready", "max_ready", "probs_ready", "pt_ready", "pt_copied_act", "pt_copied_dve", "pv_ready",
            "o_copied", "o_ready", "y_ready", "shared_ready", "shared_free", "ln_ready", "var_ready", "rstd_ready", "hi_ready",
            "summed", "key_hi_ready", "key_lo_ready")} for n in "ab"}
        moe_sems = {n: {k: sem(f"m{n}_{k}") for k in (
            "gap_ready", "exp_ready", "mask_ready", "rank_ready", "hot_ready", "hot_used", "slots_ready",
            "row0", "row1", "row2", "row3", "turned", "turned_hi", "split", "staged", "up_ready", "gelu_ready",
            "down_ready", "bias_ready", "y_ready", "stored0", "stored1", "stored2", "stored3",
            *(f"got{k}" for k in range(2 * CT)), "got_used")} for n in "12"}
        kept = {n: sem(f"kept_{n}") for n in "ab"}
        attended = {n: sem(f"attended_{n}") for n in "ab"}
        stored = sem("stored")

        block = ctx.enter_context(nc.Block())

        N_LOADS = 0

        @block.sync
        def _(sp):
            nonlocal N_LOADS

            def load(dst, src):
                nonlocal N_LOADS
                N_LOADS += 1
                sp.dma_start(dst, src).then_inc(loaded, 16)

            load(C[:, :], const[:, 0:KEPT_W])
            load(C_prep[:, :], const[:, KEPT_W:CONST_W])
            load(cw[:, :, :], c_attn_w.rearrange("(s p) c -> p s c", p=P))
            with nc.allow_non_contiguous_dma(reason="small transposed weights"):
                load(q2l_t[:, :], q2l_w.rearrange("l d -> d l"))
                load(kv2l_t[:, :], kv2l_w.rearrange("l d -> d l"))
                load(l2o_t[:, :], l2o_w.rearrange("o l -> l o"))
                load(wqk_t[:, :], wqk_w.rearrange("o l -> l o"))
                load(b3[:, :], c_attn_b.rearrange("(s p) -> p s", p=P))
                for k, v in enumerate((q2l_b, kv2l_b, wqk_b)):
                    load(lat_b[:, k:k + 1], v.rearrange("(l a) -> l a", a=1))
            load(kv2l_n[:, :], kv2l_w)
            load(l2o_row[:, :], l2o_b.rearrange("(a o) -> a o", a=1))
            load(cp[:, :], cproj_w)
            for k, w in enumerate((Wq, Wk, Wv, Wo)):
                load(wb[:, k, :], w)
            load(layers["a"]["out_b"][:, :], cproj_b.partition_broadcast(P))
            load(layers["b"]["out_b"][:, :], bo.partition_broadcast(P))
            load(layers["b"]["v_bias"][:, :], bv.partition_broadcast(P))
            load(gate_bias[:, :], gate_b.partition_broadcast(P))
            load(gate[:, :], gate_w)
            load(X[:, :, :], x_tiles)
            with nc.allow_non_contiguous_dma(reason="biases as columns"):
                load(b1_cols[:, :].rearrange("p (e k) -> p e k", e=E), b1.rearrange("e (k p) -> p e k", p=P))
            sp.wait_ge(zeroed, 1)
            with nc.allow_non_contiguous_dma(reason="biases spread over quadrants"):
                for m, v in enumerate((bq, bk)):
                    for j in range(G):
                        for copy in range(3):
                            load(bqk[L * j + HD * copy:L * j + HD * (copy + 1), m, :], v.rearrange("(g j d) -> j d g", j=G, d=HD)[j])
            sp.dma_start(W1[:, :].rearrange("p (e f) -> p e f", e=E), w1.rearrange("e d f -> d e f")).then_inc(experts_loaded, 16)
            sp.dma_start(W2[:, :].rearrange("p (e k d) -> p e k d", e=E, k=FT), w2.rearrange("e (k p) d -> p e k d", p=P)).then_inc(experts_loaded, 16)
            for n, e_ in (("a", "1"), ("b", "2")):
                m, me = att_sems[n], moe_sems[e_]

                def keep(c):
                    sp.wait_ge(m["ln_ready"], gate_norm_no(c))
                    sp.dma_start(normed_tiles[:, bass.ds(c * CT, CT), :], xn[:, :, :]).then_inc(kept[n], 16)

                with sp.Fori(0, NCH - 2) as c:
                    keep(c)
                keep(NCH - 2)
                keep(NCH - 1)

                sp.wait_ge(attended[n], 1)
                sp.dma_start(b2_rows[:, :, :].rearrange("p e d -> p (e d)"), b2.rearrange("e d -> (e d)").partition_broadcast(P)).then_inc(me["bias_ready"], 16)

                def store(i, r, least):
                    sp.wait_ge(me["y_ready"], i + 1)
                    sp.dma_start(rows_out[bass.ds(i * ROWS, ROWS), :].rearrange("(b p) d -> p b d", p=P), y_rows[:, r, :, :]).then_inc(me[f"stored{r}"], 16)

                tile_slots(sp, store)
            for c in range(NCH):
                sp.wait_ge(moe_sems["2"]["got_used"], 2 * CT * (c + 1))
                sp.dma_start(out_tiles[:, c * CT:(c + 1) * CT, :], X[:, c * CT:(c + 1) * CT, :]).then_inc(stored, 16)
            sp.wait_ge(stored, 16 * NCH)

        @block.gpsimd
        def _(pool):
            nc.gpsimd.memset(neg_half[:, :], -0.5)
            nc.gpsimd.memset(bqk[:, :, :], 0.0).then_inc(zeroed, 1)
            pool.wait_ge(zeroed, 1)

            def inverse_root(m, nth):
                pool.wait_ge(m["var_ready"], nth)
                nc.gpsimd.tensor_tensor(rstd[:, :], var_eps[:, :], neg_half[:, :], ALU.pow).then_inc(m["rstd_ready"], 1)

            def rotary(c, par):
                m, steps = att_sems["a"], Steps("a")
                inverse_root(m, norm_no(c))
                for g in range(G):
                    pool.wait_ge(m["shared_free"], steps.made(c, ("query", g)))
                    nc.gpsimd.tensor_tensor(rope_q[:, 0, :], rope_q[:, 0, :], rope_q[:, 1, :], ALU.add).then_inc(m["summed"], 1)
                    pool.wait_ge(m["shared_free"], steps.made(c, ("key", g)))
                    nc.gpsimd.tensor_tensor(rope_k[:, 0, :], rope_k[:, 0, :], rope_k[:, 1, :], ALU.add).then_inc(m["summed"], 1)
                    pool.wait_ge(m["key_hi_ready"], c * G + (g + 1))
                    nc.gpsimd.tensor_tensor(k_lo[:, par, g, :], rope_k[:, 0, :], k_hi[:, par, g, :].bitcast(F32), ALU.subtract).then_inc(m["key_lo_ready"], 1)

            def stacked(c, par):
                m, steps = att_sems["b"], Steps("b")
                inverse_root(m, norm_no(c))
                for g in range(G):
                    for kind, src, dst in (("query", rope_q, q_hi), ("key", rope_k, k_hi)):
                        pool.wait_ge(m["shared_free"], steps.made(c, (kind, g)))
                        nc.gpsimd.tensor_tensor(dst[:, par, g, :], src[:, 0, :], src[:, 1, :], ALU.add).then_inc(m["summed"], 1)
                    if c + 1 < NCH:
                        gather_results("1", c + 1, range(2 * g, 2 * g + 2))

            def gather_results(n, c, rows=range(2 * CT)):
                m = moe_sems[n]
                for k in rows:
                    t, which = c * CT + k // 2, k % 2
                    if c:
                        pool.wait_ge(m["got_used"], 2 * CT * (c - 1) + k + 1)
                    nc.gpsimd.indirect_dma_start(
                        out=got[:, k, :], out_offset=None, in_=rows_out,
                        in_offset=bass.IndirectOffsetOnAxis(ap=slot_of[:, which * NT + t:which * NT + t + 1], axis=0)).then_inc(m[f"got{k}"], 16)

            def gather_rows(n):
                m = moe_sems[n]
                pool.wait_ge(m["slots_ready"], 1)
                pool.wait_ge(kept["a" if n == "1" else "b"], 16 * NCH)
                for i in range(TILES):
                    if i >= 4:
                        pool.wait_ge(m["turned"], i - 3)
                    for b_ in range(RB):
                        k = i * RB + b_
                        nc.gpsimd.indirect_dma_start(
                            out=xg[:, i % 4, b_, :], out_offset=None, in_=normed,
                            in_offset=bass.IndirectOffsetOnAxis(ap=source[:, k:k + 1], axis=0)).then_inc(m[f"row{i % 4}"], 16)
                for r in range(4):
                    pool.wait_ge(m[f"stored{r}"], 16 * len(range(r, TILES, 4)))

            rotary(0, 0)
            rotary(1, 1)
            with pool.Fori(0, NCH // 2 - 1) as i:
                for odd in (0, 1):
                    rotary(i * 2 + (2 + odd), odd)
                    inverse_root(att_sems["a"], gate_norm_no(i * 2 + odd))
            inverse_root(att_sems["a"], gate_norm_no(NCH - 2))
            inverse_root(att_sems["a"], gate_norm_no(NCH - 1))
            gather_rows("1")
            gather_results("1", 0)
            for c in range(NCH):
                stacked(c, c % 2)
                if c >= 2:
                    inverse_root(att_sems["b"], gate_norm_no(c - 2))
            inverse_root(att_sems["b"], gate_norm_no(NCH - 2))
            inverse_root(att_sems["b"], gate_norm_no(NCH - 1))
            gather_rows("2")
            for c in range(NCH):
                gather_results("2", c)

        @block.vector
        def _(dve):
            own = Order(dve, dve_own)
            v = nc.vector

            v.memset(ones[:, :], 1.0).then_inc(dve_own, 1)
            own.n = 1
            dve.wait_ge(loaded, 16 * N_LOADS)
            own.settle()
            for dst, src in ((ident_b, "ident"), (causal_b, "causal"), (before_b, "before")):
                own.did(v.tensor_copy(dst[:, :], con(src)))
            own.did(v.memset(ones_b[:, :], 1.0))
            own.did(v.tensor_scalar(kvb_rep[:, :], ones[0:L, :], lat_b[:, 1:2], None, ALU.mult))
            own.did(v.tensor_scalar(wqk_t[:, :], wqk_t[:, :], float(L) ** -0.5, None, ALU.mult))
            own.did(v.tensor_scalar(lat_b[:, 2:3], lat_b[:, 2:3], float(L) ** -0.5, None, ALU.mult))
            own.did(v.tensor_copy(layers["b"]["bias"][:, 1, :], bqk[:, 1, :]))
            own.did(v.tensor_scalar(layers["b"]["bias"][:, 0, :], bqk[:, 0, :], float(HD) ** -0.5, None, ALU.mult))
            for k in range(2):
                own.did(v.memset(pad[k][:, :, :], 0.0))
            own.settle()
            v.memset(scratch1[:, :], 0.0).then_inc(dve_prep, 1)
            dve.wait_ge(pe_prep, 1)
            v.tensor_copy(m_t[:, :], bank[0][0:HD, 0:HD]).then_inc(dve_prep, 1)
            dve.wait_ge(pe_prep, 2)
            own.then(v.tensor_copy(rep[:, :], bank[1][:, 0:104]))
            mask_h = con("head_mask").unsqueeze(2).broadcast_to([P, H, L])
            for k, lo_ in ((0, 0), (2, L)):
                own.did(v.tensor_tensor(blk[k][:, :, :], rep[:, lo_:lo_ + L].unsqueeze(1).broadcast_to([P, H, L]), mask_h, ALU.mult))
            own.did(v.tensor_tensor(wqk_blk[:, :].rearrange("p (j l) -> p j l", j=G),
                                    rep[:, 2 * L:3 * L].unsqueeze(1).broadcast_to([P, G, L]),
                                    con("group_mask").unsqueeze(2).broadcast_to([P, G, L]), ALU.mult))
            own.did(v.tensor_tensor(blk_v[:, :, :], rep[:, 96:104].unsqueeze(1).broadcast_to([P, H, HD]),
                                    con("head_mask").unsqueeze(2).broadcast_to([P, H, HD]), ALU.mult))
            own.settle()
            for k in (0, 2):
                src = blk[k][:, :, :].rearrange("p h (i two) -> p (h i) two", two=2)
                dst = blk[k + 1][:, :, :].rearrange("p h (i two) -> p (h i) two", two=2)
                own.did(v.tensor_scalar(dst[:, :, 0:1], src[:, :, 1:2], -1.0, None, ALU.mult))
                own.did(v.tensor_copy(dst[:, :, 1:2], src[:, :, 0:1]))
            own.did(v.tensor_scalar(blk_vb[:, :, :], blk_v[:, :, :], b3[:, 2:3], None, ALU.mult))
            own.settle()
            v.memset(scratch1[:, :], 0.0).then_inc(dve_prep, 1)
            la, lb = layers["a"], layers["b"]

            def halves(hi, lo_, src):
                own.then(v.tensor_copy(hi, src))
                own.did(v.tensor_tensor(lo_, src, hi.bitcast(F32), ALU.subtract))

            for k in range(4):
                dve.wait_ge(pe_prep, 3 + k)
                halves(la["hi"][k][:, :], la["lo"][k][:, :], bank[k][:, :])
            dve.wait_ge(pe_prep, 7)
            halves(la["v_hi"][:, :], la["v_lo"][:, :], bank[4][:, 0:D])
            own.did(v.tensor_copy(la["v_bias"][:, :], bank[4][:, D:2 * D]))
            own.did(v.tensor_copy(la["bias"][:, :, :], bank[5][:, 0:4 * G].rearrange("p (m g) -> p m g", m=4)))
            own.did(v.tensor_copy(wqk_bias[:, :], bank[5][:, 4 * G:4 * G + 1]))
            dve.wait_ge(pe_prep, 8)
            own.did(v.tensor_copy(la["out_w"][:, :], bank[6][:, 0:D]))
            own.did(v.tensor_copy(lb["out_w"][:, :], bank[6][:, D:2 * D]))
            for copy in range(3):
                cols = slice(copy * HD, (copy + 1) * HD)
                own.did(v.tensor_scalar(pad[0][:, :, cols], bank[7][:, 0:D].rearrange("p (h d) -> p h d", h=H), float(HD) ** -0.5, None, ALU.mult))
                own.did(v.tensor_copy(pad[1][:, :, cols], bank[7][:, D:2 * D].rearrange("p (h d) -> p h d", h=H)))
            own.settle()
            halves(lb["v_hi"][:, :], lb["v_lo"][:, :], bank[7][:, 2 * D:3 * D])
            for k in range(2):
                halves(lb["hi"][k][:, :], lb["lo"][k][:, :], pad[k][:, :, :].rearrange("p h l -> p (h l)"))
            own.settle()
            v.memset(scratch1[:, :], 0.0).then_inc(dve_prep, 1)

            def statistics(m, c):
                first_tile = c * CT
                for t in range(CT):
                    own.did(v.bn_stats(stats[:, t, :], X[:, bass.ds(first_tile + t, 1), :].rearrange("p a d -> p (a d)")))
                own.settle()
                v.memset(scratch2[:, :], 0.0)
                for t in range(CT):
                    own.did(v.bn_aggr(mv[:, t, :], stats[:, t, :]))
                own.settle()
                v.tensor_scalar(var_eps[:, :].unsqueeze(2), mv[:, :, 1:2], EPS, None, ALU.add).then_inc(m["var_ready"], 1)

            def normalise_rows(m, c, nth):
                first_tile = c * CT
                dve.wait_ge(m["rstd_ready"], nth)
                for t in range(CT):
                    ins = v.tensor_scalar(xn[:, t, :], X[:, bass.ds(first_tile + t, 1), :].rearrange("p a d -> p (a d)"),
                                          mv[:, t, 0:1], rstd[:, t:t + 1], ALU.subtract, ALU.mult)
                ins.then_inc(m["ln_ready"], 1)
            LN_OWN = 2 * CT

            def attention(n):
                m, w, steps = att_sems[n], layers[n], Steps(n)
                v.memset(v_aug[:, :, :, :, :].rearrange("p a t h l -> p (a t h) l"), 0.0).then_inc(dve_own, 1)
                own.n += 1
                own.settle()
                own.then(v.memset(v_aug[:, :, :, :, HD:HD + 1].rearrange("p a t h l -> p (a t h) l"), 1.0))

                def step(kind, g, c, par, k):
                    dve.wait_ge(m["shared_ready"], k + 1)
                    free = m["shared_free"]
                    a0, a1 = w_bank[0], w_bank[1]
                    hi_per = steps.hi_per
                    two = lambda ap: ap.rearrange("p (b s) -> p b s", b=2)
                    if kind == "prep":
                        dve.wait_ge(m["hi_ready"], c * hi_per + 1)
                        v.tensor_tensor(xt_lo[:, :], a0[:, :], xt_hi[:, :].bitcast(F32), ALU.subtract).then_inc(free, 1)
                    elif kind == "value":
                        v.tensor_tensor(v_aug[:, par, :, :, 0:HD], a1[:, :].rearrange("p (t h d) -> p t h d", t=CT, h=H),
                                        w["v_bias"][:, :].rearrange("p (h d) -> p h d", h=H).unsqueeze(1).broadcast_to([P, CT, H, HD]),
                                        ALU.add).then_inc(free, 1)
                    elif kind in ("query", "key") and steps.rotary:
                        dst, w0 = (rope_q, 0) if kind == "query" else (rope_k, 2)
                        if kind == "key" and not (isinstance(c, int) and c == 0 and g == 0):
                            dve.wait_ge(m["key_lo_ready"], c * G + g)
                        for part, (bank_, table) in enumerate(((a0, "cos"), (a1, "sin"))):
                            ins = v.scalar_tensor_tensor(two(dst[:, part, :]), two(bank_[:, :]), w["bias"][:, w0 + part, g:g + 1],
                                                         con(table).unsqueeze(1).broadcast_to([P, 2, S]), ALU.add, ALU.mult)
                        ins.then_inc(free, 1)
                    elif kind == "query2":
                        dve.wait_ge(m["hi_ready"], c * hi_per + (g + 2))
                        v.scalar_tensor_tensor(q_lo[:, par, g, :], a0[:, :], wqk_bias[:, 0:1], q_hi[:, par, g, :].bitcast(F32),
                                               ALU.add, ALU.subtract).then_inc(free, 1)
                    elif kind in ("query", "key"):
                        which = 0 if kind == "query" else 1
                        dve.wait_ge(m["hi_ready"], c * hi_per + (2 * g + 2 + which))
                        v.tensor_scalar((rope_q, rope_k)[which][:, 1, :].bitcast(F32R), a0[:, :], w["bias"][:, which, g:g + 1],
                                        con("stack")[:, which:which + 1], ALU.add, ALU.mult).then_inc(free, 1)
                    elif kind == "out_t":
                        v.tensor_copy(y_t[:, :], a0[:, :]).then_inc(free, 1)
                    elif kind == "out":
                        xs = X[:, bass.ds(c * CT, CT), :]
                        own.then(v.tensor_tensor(xs, a1[:, :].rearrange("p (t d) -> p t d", t=CT), xs, ALU.add))
                        v.tensor_tensor(xs, xs, w["out_b"][:, :].unsqueeze(1).broadcast_to([P, CT, D]), ALU.add).then_inc(free, 1)
                    elif kind == "gate_t":
                        v.tensor_copy(y_t[:, :], a0[:, :]).then_inc(free, 1)
                    elif kind == "gate":
                        v.tensor_tensor(logit[:, bass.ds(c * CT, CT), :], a1[:, 0:CT * E].rearrange("p (t e) -> p t e", t=CT),
                                        gate_bias[:, :].unsqueeze(1).broadcast_to([P, CT, E]), ALU.add).then_inc(free, 1)

                def row_max(unit, nb):
                    heads = G if nb == 0 else 2
                    dve.wait_ge(m["scores_ready"], unit * 3 + (nb + 1))
                    v.tensor_reduce(neg_max[:, nb, 0:heads], s_bank[nb][:, :].rearrange("p (h k) -> p h k", h=heads), AX, ALU.max,
                                    negate=True).then_inc(m["max_ready"], 1)

                def copy_o(unit):
                    dve.wait_ge(m["pv_ready"], unit + 1)
                    v.tensor_copy(o_t[:, :], o_bank[:, 0:S]).then_inc(m["o_copied"], 1)

                def normalise(unit, u, par):
                    b_, j = u // G, u % G
                    dve.wait_ge(m["o_ready"], unit + 1)
                    o = o_bank[:, S:2 * S].rearrange("p (q g l) -> p q g l", q=2, g=G)
                    own.then(v.reciprocal(inv_sum[:, :, :].unsqueeze(3), o[:, :, :, HD:HD + 1]))
                    v.tensor_tensor(Y[:, par, 2 * b_:2 * b_ + 2, :].rearrange("p q (g j d) -> p q g j d", g=G, j=G)[:, :, :, j, :],
                                    o[:, :, :, 0:HD], inv_sum[:, :, :].unsqueeze(3).broadcast_to([P, 2, G, HD]),
                                    ALU.mult).then_inc(m["y_ready"], 1)

                if n == "b":
                    add_expert_rows("1", 0, range(2 * CT))
                statistics(m, 0)
                normalise_rows(m, 0, norm_no(0))
                for k, (kind, g) in enumerate(steps.all_make()):
                    step(kind, g, 0, 0, k)
                for nb in range(3):
                    row_max(0, nb)

                def period(c, par, first, last):
                    k = steps.before(c)
                    for u in range(UNITS):
                        unit = c * UNITS + u
                        prev = not (first and u == 0)
                        prev_par = par if u else 1 - par
                        for nb in range(3):
                            if nb == 1:
                                dve.wait_ge(m["pt_ready"], unit * 3 + 2)
                                v.tensor_copy(prob_t[:, u % 2, 1, :], t_bank[(3 * u + 1) % 2][:, :]).then_inc(m["pt_copied_dve"], 1)
                            if not (last and u == UNITS - 1):
                                row_max(unit + 1, nb)
                            if nb == 0 and prev:
                                copy_o(unit - 1)
                            if nb == 2 and prev:
                                normalise(unit - 1, (u - 1) % UNITS, prev_par)
                            if not last:
                                if (u, nb) == steps.norm[0]:
                                    statistics(m, c + 1)
                                if (u, nb) in steps.add:
                                    add_expert_rows("1", c + 1, steps.add[u, nb])
                                if (u, nb) == steps.norm[1]:
                                    normalise_rows(m, c + 1, norm_no(1) if first else norm_no(c + 1))
                            if not first:
                                if (u, nb) == steps.gate_norm[0]:
                                    statistics(m, c - 1)
                                if (u, nb) == steps.gate_norm[1]:
                                    normalise_rows(m, c - 1, gate_norm_no(c - 1))
                            for kind, g in steps.at(u, nb, not last, not first):
                                step(kind, g, c - 1 if kind in CLOSING else c + 1, 1 - par, k)
                                k = k + 1
                    if not first:
                        dve.wait_ge(kept[n], c * 16)
                        v.memset(scratch2[:, :], 0.0)

                periods(dve, period, own, 2 * (UNITS + 2 * LN_OWN + 1))
                end = NCH * UNITS - 1
                copy_o(end)
                normalise(end, UNITS - 1, 1)
                k = steps.before(NCH - 1) + steps.n_close
                step("out_t", 0, NCH - 1, 1, k)
                step("out", 0, NCH - 1, 1, k + 1)
                dve.wait_ge(m["shared_free"], k + 2)
                statistics(m, NCH - 1)
                normalise_rows(m, NCH - 1, gate_norm_no(NCH - 1))
                step("gate_t", 0, NCH - 1, 1, k + 2)
                step("gate", 0, NCH - 1, 1, k + 3)
                dve.wait_ge(m["shared_free"], k + 4)
                v.memset(scratch1[:, :], 0.0).then_inc(attended[n], 1)
                dve.wait_ge(attended[n], 1)

            def experts(n):
                m = moe_sems[n]

                over_t = lambda ap: ap.unsqueeze(1).broadcast_to([P, NT, E])
                over_e = lambda ap: ap.unsqueeze(2).broadcast_to([P, NT, E])
                best, scratch = col[0:2], col[2:5]
                first_hot, second_hot, rest, work, cum_a, cum_b = route

                def choose(values, top, hot):
                    own.then(v.tensor_reduce(top[:, :], values[:, :, :], AX, ALU.max))
                    own.then(v.tensor_tensor(work[:, :, :], values[:, :, :], over_e(top[:, :]), ALU.is_equal))
                    own.then(v.tensor_tensor(work[:, :, :], work[:, :, :], over_t(con("prefer")), ALU.mult))
                    own.then(v.tensor_reduce(scratch[0][:, :], work[:, :, :], AX, ALU.max))
                    own.then(v.tensor_tensor(hot[:, :, :], work[:, :, :], over_e(scratch[0][:, :]), ALU.is_equal))

                choose(logit, best[0], first_hot)
                own.then(v.scalar_tensor_tensor(rest[:, :, :], first_hot[:, :, :], -3e38, logit[:, :, :], ALU.mult, ALU.add))
                choose(rest, best[1], second_hot)
                v.tensor_tensor(scratch[1][:, :], best[1][:, :], best[0][:, :], ALU.subtract).then_inc(m["gap_ready"], 1)
                v.tensor_tensor(chosen_b[:, :, :], first_hot[:, :, :], second_hot[:, :, :], ALU.add).then_inc(m["mask_ready"], 1)
                dve.wait_ge(m["exp_ready"], 1)
                own.then(v.tensor_scalar(scratch[0][:, :], scratch[2][:, :], 1.0, None, ALU.add))
                own.then(v.reciprocal(weight[0][:, :], scratch[0][:, :]))
                own.then(v.tensor_tensor(weight[1][:, :], weight[0][:, :], scratch[2][:, :], ALU.mult))
                dve.wait_ge(m["rank_ready"], 1)
                flat = lambda ap: ap[:, :, :].rearrange("p t e -> p (t e)")
                own.then(v.tensor_copy(flat(cum_a), w_bank[1][:, 0:NT * E]))
                a, b_ = cum_a, cum_b
                shift = 1
                while shift < NT:
                    own.did(v.tensor_copy(b_[:, 0:shift, :], a[:, 0:shift, :]))
                    own.then(v.tensor_tensor(b_[:, shift:NT, :], a[:, shift:NT, :], a[:, 0:NT - shift, :], ALU.add))
                    a, b_ = b_, a
                    shift *= 2
                own.then(v.tensor_scalar(ecol[0][:, :], a[:, NT - 1, :], float(ROWS - 1), None, ALU.add))
                own.then(v.tensor_copy(ecol_i[0][:, :], ecol[0][:, :]))
                own.then(v.tensor_scalar(ecol_i[1][:, :], ecol_i[0][:, :], ROWS.bit_length() - 1, None, ALU.logical_shift_right))
                own.then(v.tensor_copy(ecol[1][:, :], ecol_i[1][:, :]))
                ca, cb = ecol[1], ecol[2]
                spare = [ecol[2], ecol[3], ecol[4]]
                for k, shift in enumerate((1, 2, 4)):
                    cb = spare[k]
                    own.did(v.tensor_copy(cb[:, 0:shift], ca[:, 0:shift]))
                    own.then(v.tensor_tensor(cb[:, shift:E], ca[:, shift:E], ca[:, 0:E - shift], ALU.add))
                    ca = cb
                own.then(v.tensor_tensor(ecol[0][:, :], ca[:, :], ecol[1][:, :], ALU.subtract))
                own.then(v.tensor_scalar(ecol[0][:, :], ecol[0][:, :], float(ROWS), None, ALU.mult))
                own.then(v.tensor_tensor(flat(b_), flat(a), w_bank[1][:, 0:NT * E], ALU.subtract))
                own.then(v.tensor_tensor(flat(a), w_bank[0][:, 0:NT * E], flat(b_), ALU.add))
                own.then(v.tensor_tensor(b_[:, :, :], a[:, :, :], over_t(ecol[0][:, :]), ALU.add))
                for k, hot in enumerate((first_hot, second_hot)):
                    own.then(v.tensor_tensor(work[:, :, :], hot[:, :, :], b_[:, :, :], ALU.mult))
                    own.then(v.tensor_reduce(slot_f[:, k * NT:(k + 1) * NT], work[:, :, :], AX, ALU.add))
                own.then(v.tensor_copy(slot_of[:, :], slot_f[:, :]))
                own.then(v.tensor_scalar(block_i[:, :], slot_of[:, :], P.bit_length() - 1, None, ALU.logical_shift_right))
                own.then(v.tensor_copy(block_f[:, :], block_i[:, :]))
                own.then(v.scalar_tensor_tensor(lane_f[:, :], block_f[:, :], -float(P), slot_f[:, :], ALU.mult, ALU.add))

                def hot(t, k, n_):
                    ring = hot_ring[0]
                    if not (isinstance(n_, int) and n_ < 4):
                        dve.wait_ge(m["hot_used"], n_ - 3)
                    where = bass.ds(t + k * NT, 1)
                    v.tensor_scalar(lane_hot[:, ring, :], con("lane_no"), lane_f[:, where], None, ALU.is_equal)
                    v.tensor_scalar(block_hot[:, ring, :], con("block_no"), block_f[:, where], con("token_no")[:, bass.ds(t, 1)],
                                    ALU.is_equal, ALU.mult).then_inc(m["hot_ready"], 1)
                    hot_ring[0] = (ring + 1) % 4

                hot_ring = [0]
                hot_tiles(dve, hot)
                own.then(v.tensor_tensor(emap_f[:, :, :], con("block_no", 1)[:, 0:TILES].unsqueeze(2).broadcast_to([1, TILES, E]),
                                         ca[0:1, :].unsqueeze(1).broadcast_to([1, TILES, E]), ALU.is_ge))
                own.then(v.tensor_reduce(emap_s[:, 0, :], emap_f[:, :, :], AX, ALU.add))
                own.then(v.tensor_scalar(emap_s[:, 1, :], emap_s[:, 0, :], float(E - 1), None, ALU.min))
                own.then(v.tensor_copy(expert_of[:, :], emap_s[:, 1, :]))
                dve.wait_ge(m["hot_used"], 2 * NT)
                own.then(v.tensor_copy(source_f[:, 0, :], bank[0][:, 0:BLOCKS]))
                own.then(v.scalar_tensor_tensor(source_f[:, 1, :], source_f[:, 0, :], -1.0, bank[1][:, 0:BLOCKS], ALU.add, ALU.add))
                own.then(v.tensor_scalar(source_f[:, 0, :], source_f[:, 1, :], 0.0, None, ALU.max))
                v.tensor_copy(source[:, :], source_f[:, 0, :]).then_inc(m["slots_ready"], 1)
                dve.wait_ge(m["slots_ready"], 1)

                def expert(i):
                    return dve.value_load(expert_of[0:1, bass.ds(i, 1)], min_val=0, max_val=E - 1)

                def split_rows(i, r):
                    dve.wait_ge(m["turned_hi"], i + 1)
                    v.tensor_tensor(xg_lo[:, r % 2, :], r_bank[r % 2][:, 0:ROWS], xg_hi[:, r % 2, :].bitcast(F32), ALU.subtract).then_inc(m["split"], 1)

                def stage(i, r, least):
                    e = expert(i)
                    if least >= 2:
                        dve.wait_ge(m["up_ready"], i - 1)
                    w = W1[:, bass.ds(e * F, F)]
                    v.tensor_copy(w1_hi[:, r % 2, :], w).then_inc(m["staged"], 1)
                    dve.wait_ge(m["staged"], i * 2 + 1)
                    v.tensor_tensor(w1_lo[:, r % 2, :], w, w1_hi[:, r % 2, :].bitcast(F32), ALU.subtract).then_inc(m["staged"], 1)

                def finish(i, r, least):
                    e = expert(i)
                    if least >= 4:
                        dve.wait_ge(m[f"stored{r}"], stores_before(i, r))
                    dve.wait_ge(m["down_ready"], i + 1)
                    v.tensor_tensor(y_rows[:, r, :, :], y_bank[r % 2][:, 0:ROWS].rearrange("p (b d) -> p b d", b=RB),
                                    b2_rows[:, bass.ds(e, 1), :].broadcast_to([P, RB, D]), ALU.add).then_inc(m["y_ready"], 1)

                dve.wait_ge(experts_loaded, 32)
                stage(0, 0, 0)
                stage(1, 1, 1)
                split_rows(0, 0)
                split_rows(1, 1)
                dve.wait_ge(m["bias_ready"], 16)

                def slot(i, r, least):
                    if least + 2 < TILES:
                        split_rows(i + 2, (r + 2) % 4)
                        stage(i + 2, (r + 2) % 4, least + 2)
                    finish(i, r, least)

                tile_slots(dve, slot)

            def add_expert_rows(n, c, rows):
                m = moe_sems[n]
                for k in rows:
                    t, which = c * CT + k // 2, k % 2
                    dve.wait_ge(m[f"got{k}"], c * 16 + 16)
                    if which:
                        dve.wait_ge(m["got_used"], c * (2 * CT) + k)
                    xs = X[:, bass.ds(t, 1), :].rearrange("p a d -> p (a d)")
                    ins = v.scalar_tensor_tensor(xs, got[:, k, :], weight[which][:, bass.ds(t, 1)], xs, ALU.mult, ALU.add)
                    ins.then_inc(m["got_used"], 1)
                dve.wait_ge(m["got_used"], c * (2 * CT) + (rows[-1] + 1))
                v.memset(scratch2[:, :], 0.0)

            attention("a")
            experts("1")
            attention("b")
            experts("2")
            for c in range(NCH):
                add_expert_rows("2", c, range(2 * CT))

        @block.scalar
        def _(act):
            s = nc.scalar

            def attention(n):
                m, w, steps = att_sems[n], layers[n], Steps(n)

                def probs(unit, nb):
                    heads, width = (G, P) if nb == 0 else (2, S)
                    act.wait_ge(m["max_ready"], unit * 3 + (nb + 1))
                    for h in range(heads):
                        cols = slice(h * width, (h + 1) * width)
                        ins = s.activation(prob[:, nb, cols], s_bank[nb][:, cols], ACT.Exp, bias=neg_max[:, nb, h:h + 1])
                    ins.then_inc(m["probs_ready"], 1)

                def copy_t(unit, u, nb):
                    act.wait_ge(m["pt_ready"], unit * 3 + (nb + 1))
                    s.activation(prob_t[:, u % 2, nb, :], t_bank[(3 * u + nb) % 2][:, :], ACT.Copy).then_inc(m["pt_copied_act"], 1)

                def step(kind, g, c, par, k):
                    if kind == "prep":
                        act.wait_ge(m["shared_ready"], k + 1)
                        s.activation(xt_hi[:, :], w_bank[0][:, :], ACT.Copy).then_inc(m["hi_ready"], 1)
                    elif kind == "query2":
                        act.wait_ge(m["shared_ready"], k + 1)
                        s.activation(q_hi[:, par, g, :], w_bank[0][:, :], ACT.Identity, bias=wqk_bias[:, 0:1]).then_inc(m["hi_ready"], 1)
                        act.wait_ge(m["summed"], c * 2 * G + (2 * g + 2))
                        s.activation(k_hi[:, par, g, :], rope_k[:, 0, :], ACT.Copy).then_inc(m["key_hi_ready"], 1)
                    elif kind in ("query", "key") and not steps.rotary:
                        which = 0 if kind == "query" else 1
                        act.wait_ge(m["shared_ready"], k + 1)
                        if not (isinstance(c, int) and c == 0 and g == 0):
                            act.wait_ge(m["summed"], c * 2 * G + (2 * g - 1 + which))
                        s.activation((rope_q, rope_k)[which][:, 0, :], w_bank[0][:, :], ACT.Identity,
                                     bias=w["bias"][:, which, g:g + 1]).then_inc(m["hi_ready"], 1)

                for k, (kind, g) in enumerate(steps.all_make()):
                    step(kind, g, 0, 0, k)
                for nb in range(3):
                    probs(0, nb)

                def period(c, par, first, last):
                    k = steps.before(c)
                    for u in range(UNITS):
                        unit = c * UNITS + u
                        for nb in range(3):
                            if nb != 1:
                                copy_t(unit, u, nb)
                            if not (last and u == UNITS - 1):
                                probs(unit + 1, nb)
                            for kind, g in steps.at(u, nb, not last, not first):
                                step(kind, g, c + 1, 1 - par, k)
                                k = k + 1

                periods(act, period)

            def experts(n):
                m = moe_sems[n]
                act.wait_ge(m["gap_ready"], 1)
                s.activation(col[4][:, :], col[3][:, :], ACT.Exp).then_inc(m["exp_ready"], 1)

                def turned_high(i, r, least):
                    act.wait_ge(m["turned"], i + 1)
                    if least >= 2:
                        act.wait_ge(m["up_ready"], i - 1)
                    s.activation(xg_hi[:, r % 2, :], r_bank[r % 2][:, 0:ROWS], ACT.Copy).then_inc(m["turned_hi"], 1)

                def gelu(i, r, least):
                    e = act.value_load(expert_of[0:1, bass.ds(i, 1)], min_val=0, max_val=E - 1)
                    act.wait_ge(m["up_ready"], i + 1)
                    if least >= 2:
                        act.wait_ge(m["down_ready"], i - 1)
                    for k in range(FT):
                        ins = s.activation(hid[:, r % 2, k, :], h_bank[r % 2][k // 2][:, k % 2 * ROWS:(k % 2 + 1) * ROWS], ACT.Gelu,
                                           bias=b1_cols[:, bass.ds(e * FT + k, 1)])
                    ins.then_inc(m["gelu_ready"], 1)

                act.wait_ge(m["slots_ready"], 1)
                turned_high(0, 0, 0)
                turned_high(1, 1, 1)
                gelu(0, 0, 0)

                def slot(i, r, least):
                    if least + 1 < TILES:
                        gelu(i + 1, (r + 1) % 4, least + 1)
                    if least + 2 < TILES:
                        turned_high(i + 2, (r + 2) % 4, least + 2)

                tile_slots(act, slot)

            attention("a")
            experts("1")
            attention("b")
            experts("2")

        @block.tensor
        def _(pe):
            t_ = nc.tensor

            pe.wait_ge(dve_prep, 1)
            t_.matmul(bank[0][0:HD, 0:HD], kv2l_n[:, :], l2o_t[:, :], start=True, stop=True).then_inc(pe_prep, 1)
            pe.wait_ge(dve_prep, 2)
            for k, (lhs, rhs) in enumerate(((con("rep8", HD), q2l_t), (con("rep8", HD), kv2l_t), (con("rep32", L), wqk_t))):
                t_.matmul(bank[1][:, k * L:(k + 1) * L], lhs, rhs[:, :], start=True, stop=True)
            t_.matmul(bank[1][:, 3 * L:3 * L + HD], con("rep8", HD), m_t[:, :], start=True, stop=True).then_inc(pe_prep, 1)
            pe.wait_ge(dve_prep, 3)
            for k in range(4):
                t_.matmul(bank[k][:, :], cw[:, k // 2, :], blk[k][:, :, :].rearrange("p h l -> p (h l)"), start=True, stop=True).then_inc(pe_prep, 1)
            t_.matmul(bank[4][:, 0:D], cw[:, 2, :], blk_v[:, :, :].rearrange("p h d -> p (h d)"), start=True, stop=True)
            t_.matmul(bank[4][:, D:2 * D], ones[:, :], blk_vb[:, :, :].rearrange("p h d -> p (h d)"), start=True, stop=False)
            t_.matmul(bank[4][:, D:2 * D], kvb_rep[:, :], l2o_t[:, :].unsqueeze(1).broadcast_to([L, H, HD]), start=False, stop=False)
            t_.matmul(bank[4][:, D:2 * D], ones[0:1, :], l2o_row[:, :].unsqueeze(1).broadcast_to([1, H, HD]), start=False, stop=True)
            for k in range(4):
                for g in range(G):
                    o = bank[5][:, k * G + g:k * G + g + 1]
                    t_.matmul(o, blk[k][:, g * G:(g + 1) * G, :].rearrange("p h l -> p (h l)"), b3[:, k // 2:k // 2 + 1], start=True, stop=False)
                    t_.matmul(o, con("rot32" if k % 2 else "rep32", L), lat_b[:, k // 2:k // 2 + 1], start=False, stop=True)
            t_.matmul(bank[5][:, 4 * G:4 * G + 1], con("rep32", L), lat_b[:, 2:3], start=True, stop=True).then_inc(pe_prep, 1)
            for dst, src in ((bank[6][:, 0:D], cp[:, :]), (bank[6][:, D:2 * D], wb[:, 3, :]), (bank[7][:, 0:D], wb[:, 0, :]),
                             (bank[7][:, D:2 * D], wb[:, 1, :]), (bank[7][:, 2 * D:3 * D], wb[:, 2, :])):
                ins = t_.transpose(dst, src, ident)
            ins.then_inc(pe_prep, 1)
            pe.wait_ge(dve_prep, 4)

            def product(o, w_hi, w_lo, x_hi, x_lo, start=True):
                t_.matmul(o, w_hi, x_hi, start=start, stop=False, skip_group_check=True)
                t_.matmul(o, w_lo, x_hi, start=False, stop=False, skip_group_check=True)
                return t_.matmul(o, w_hi, x_lo, start=False, stop=True, skip_group_check=True)

            def attention(n):
                m, w, steps = att_sems[n], layers[n], Steps(n)

                def step(kind, g, c, par, k, norm=None):
                    if not (isinstance(k, int) and k == 0):
                        pe.wait_ge(m["shared_free"], k)
                    a0, a1 = w_bank[0], w_bank[1]
                    if kind in ("prep", "gate_t"):
                        pe.wait_ge(m["ln_ready"], norm)
                        for t in range(CT):
                            ins = t_.transpose(a0[:, t * P:(t + 1) * P], xn[:, t, :], ident)
                    elif kind == "value":
                        for t in range(CT):
                            cols = slice(t * P, (t + 1) * P)
                            ins = product(a1[:, cols], xt_hi[:, cols], xt_lo[:, cols], w["v_hi"][:, :], w["v_lo"][:, :])
                    elif kind in ("query", "key"):
                        mats = (((a0, 0), (a1, 1)) if kind == "query" else ((a0, 2), (a1, 3))) if steps.rotary else ((a0, 0 if kind == "query" else 1),)
                        cols = slice(g * P, (g + 1) * P)
                        for bank_, k_ in mats:
                            ins = product(bank_[:, :], w["hi"][k_][:, cols], w["lo"][k_][:, cols], xt_hi[:, :], xt_lo[:, :])
                    elif kind == "query2":
                        pe.wait_ge(m["summed"], c * 2 * G + (2 * g + 1))
                        ins = t_.matmul(a0[:, :], wqk_blk[:, :], rope_q[:, 0, :], start=True, stop=True)
                    elif kind == "out_t":
                        for t in range(CT):
                            ins = t_.transpose(a0[:, t * P:(t + 1) * P], Y[:, par, t, :], ident)
                    elif kind == "out":
                        for t in range(CT):
                            ins = t_.matmul(a1[:, t * P:(t + 1) * P], y_t[:, t * P:(t + 1) * P], w["out_w"][:, :], start=True, stop=True)
                    elif kind == "gate":
                        for t in range(CT):
                            ins = t_.matmul(a1[:, t * E:(t + 1) * E], y_t[:, t * P:(t + 1) * P], gate[:, :], start=True, stop=True)
                    ins.then_inc(m["shared_ready"], 1)

                def scores(u, par, nb):
                    b_, j = u // G, u % G
                    rows = slice(j * L, (j + 1) * L)
                    heads = range(G) if nb == 0 else range(2 * nb - 2, 2 * nb)
                    width = P if nb == 0 else S
                    q0 = b_ * S + (0 if nb == 0 else P)
                    for k, g in enumerate(heads):
                        kk = slice(b_ * S, b_ * S + width)
                        if not steps.rotary:
                            t_.matmul(s_bank[nb][:, k * width:(k + 1) * width], q_hi[rows, par, g, q0:q0 + P], k_hi[rows, par, g, kk],
                                      start=(k == 0), stop=False, skip_group_check=True)
                            continue
                        product(s_bank[nb][:, k * width:(k + 1) * width], q_hi[rows, par, g, q0:q0 + P], q_lo[rows, par, g, q0:q0 + P],
                                k_hi[rows, par, g, kk], k_lo[rows, par, g, kk], start=(k == 0))
                    o = s_bank[nb][:, :].rearrange("p (h k) -> p h k", h=len(heads))[:, :, width - P:width]
                    t_.matmul(o, ident_b[:, :], causal_b[:, :].unsqueeze(1).broadcast_to([P, len(heads), P]), start=False, stop=True,
                              skip_group_check=True).then_inc(m["scores_ready"], 1)

                def transposes(unit, u, nb, first):
                    pe.wait_ge(m["probs_ready"], unit * 3 + (nb + 1))
                    if nb == 0 and not first:
                        pe.wait_ge(m["pt_copied_dve"], unit)
                    elif nb == 1 and not first:
                        pe.wait_ge(m["pt_copied_act"], unit * 2)
                    elif nb == 2:
                        pe.wait_ge(m["pt_copied_act"], unit * 2 + 1)
                    for k in range(4):
                        cols = slice(k * P, (k + 1) * P)
                        ins = t_.transpose(t_bank[(3 * u + nb) % 2][:, cols], prob[:, nb, cols], ident)
                    ins.then_inc(m["pt_ready"], 1)

                def weighted(unit, u, par, first):
                    b_, j = u // G, u % G
                    pe.wait_ge(m["pt_copied_dve"], unit + 1)
                    pe.wait_ge(m["pt_copied_act"], unit * 2 + 2)
                    if not first:
                        pe.wait_ge(m["y_ready"], unit)
                    pt = prob_t[:, u % 2, :, :]
                    for q, kb in ((0, 0), (1, 0), (1, 1)):
                        for g in range(G):
                            if q == 0:
                                rhs = pt[:, 0, g * P:(g + 1) * P]
                            else:
                                at = ((g % 2) * 2 + kb) * P
                                rhs = pt[:, 1 + g // 2, at:at + P]
                            ins = t_.matmul(o_bank[g * L:(g + 1) * L, q * P:(q + 1) * P], v_aug[:, par, 2 * b_ + kb, g * G + j, :], rhs,
                                            start=(q == 0), stop=(kb == q), skip_group_check=True)
                    ins.then_inc(m["pv_ready"], 1)

                def turn_back(unit):
                    pe.wait_ge(m["o_copied"], unit + 1)
                    for q in range(2):
                        ins = t_.transpose(o_bank[:, S + q * P:S + (q + 1) * P], o_t[:, q * P:(q + 1) * P], ident)
                    ins.then_inc(m["o_ready"], 1)

                def operands(c_next, k_end):
                    pe.wait_ge(m["shared_free"], k_end)
                    if steps.rotary:
                        pe.wait_ge(m["key_lo_ready"], c_next * G + G)
                    else:
                        pe.wait_ge(m["summed"], c_next * (2 * G) + 2 * G)

                for k, (kind, g) in enumerate(steps.all_make()):
                    step(kind, g, 0, 0, k, norm_no(0))
                operands(0, steps.n_make)
                for nb in range(3):
                    scores(0, 0, nb)

                def period(c, par, first, last):
                    k = steps.before(c)
                    for u in range(UNITS):
                        unit = c * UNITS + u
                        prev = not (first and u == 0)
                        prev_par = par if u else 1 - par
                        for nb in range(3):
                            transposes(unit, u, nb, first and u == 0)
                            if u < UNITS - 1:
                                scores(u + 1, par, nb)
                            elif not last:
                                if nb == 0:
                                    operands(c + 1, steps.made(c + 1, steps.last_made))
                                scores(0, 1 - par, nb)
                            if nb == 0 and prev:
                                weighted(unit - 1, (u - 1) % UNITS, prev_par, first and u == 1)
                            if nb == 2 and prev:
                                turn_back(unit - 1)
                            for kind, g in steps.at(u, nb, not last, not first):
                                if kind in CLOSING:
                                    step(kind, g, c - 1, 1 - par, k, gate_norm_no(c - 1) if kind == "gate_t" else None)
                                else:
                                    step(kind, g, c + 1, 1 - par, k, norm_no(1) if first else norm_no(c + 1) if kind == "prep" else None)
                                k = k + 1

                periods(pe, period)
                end = NCH * UNITS - 1
                weighted(end, UNITS - 1, 1, False)
                turn_back(end)
                pe.wait_ge(m["y_ready"], end + 1)
                k = steps.before(NCH - 1) + steps.n_close
                step("out_t", 0, NCH - 1, 1, k)
                step("out", 0, NCH - 1, 1, k + 1)
                step("gate_t", 0, NCH - 1, 1, k + 2, gate_norm_no(NCH - 1))
                step("gate", 0, NCH - 1, 1, k + 3)

            def experts(n):
                m = moe_sems[n]

                pe.wait_ge(m["mask_ready"], 1)
                mask = chosen_b[:, :, :].rearrange("p t e -> p (t e)")
                t_.matmul(w_bank[0][:, 0:NT * E], before_b[:, :], mask, start=True, stop=True)
                t_.matmul(w_bank[1][:, 0:NT * E], ones_b[:, :], mask, start=True, stop=True).then_inc(m["rank_ready"], 1)

                def token_of(t, k, n_):
                    pe.wait_ge(m["hot_ready"], n_ + 1)
                    ring = hot_ring[0]
                    t_.matmul(bank[k][:, 0:BLOCKS], lane_hot[:, ring, :], block_hot[:, ring, :], start=(isinstance(t, int) and t == 0),
                              stop=(isinstance(t, int) and t == NT - 1)).then_inc(m["hot_used"], 1)
                    hot_ring[0] = (ring + 1) % 4

                hot_ring = [0]
                hot_tiles(pe, token_of)
                pe.wait_ge(m["slots_ready"], 1)

                def turn_rows(i, r, least):
                    pe.wait_ge(m[f"row{r}"], (stores_before(i, r) + 16) * RB)
                    if least >= 2:
                        pe.wait_ge(m["split"], i - 1)
                    for b_ in range(RB):
                        ins = t_.transpose(r_bank[r % 2][:, b_ * P:(b_ + 1) * P], xg[:, r, b_, :], ident)
                    ins.then_inc(m["turned"], 1)

                def up(i, r, least):
                    pe.wait_ge(m["split"], i + 1)
                    pe.wait_ge(m["staged"], i * 2 + 2)
                    if least >= 2:
                        pe.wait_ge(m["gelu_ready"], i - 1)
                    for k in range(FT):
                        cols = slice(k * P, (k + 1) * P)
                        ins = product(h_bank[r % 2][k // 2][:, k % 2 * ROWS:(k % 2 + 1) * ROWS], w1_hi[:, r % 2, cols], w1_lo[:, r % 2, cols],
                                      xg_hi[:, r % 2, :], xg_lo[:, r % 2, :])
                    ins.then_inc(m["up_ready"], 1)

                def down(i, r, least):
                    e = pe.value_load(expert_of[0:1, bass.ds(i, 1)], min_val=0, max_val=E - 1)
                    pe.wait_ge(m["gelu_ready"], i + 1)
                    if least >= 2:
                        pe.wait_ge(m["y_ready"], i - 1)
                    for b_ in range(RB):
                        for k in range(FT):
                            ins = t_.matmul(y_bank[r % 2][:, b_ * P:(b_ + 1) * P], hid[:, r % 2, k, b_ * P:(b_ + 1) * P],
                                            W2[:, bass.ds(e * F + k * D, D)], start=(k == 0), stop=(k == FT - 1))
                    ins.then_inc(m["down_ready"], 1)

                turn_rows(0, 0, 0)
                turn_rows(1, 1, 1)
                up(0, 0, 0)

                def slot(i, r, least):
                    if least + 1 < TILES:
                        up(i + 1, (r + 1) % 4, least + 1)
                    if least + 2 < TILES:
                        turn_rows(i + 2, (r + 2) % 4, least + 2)
                    down(i, r, least)

                tile_slots(pe, slot)

            attention("a")
            experts("1")
            attention("b")
            experts("2")


_INS = ["L0_attn_a_x"] + [f"L0_attn_a_{k}" for k in (
    "c_attn_w", "c_attn_b", "q2l_w", "q2l_b", "kv2l_w", "kv2l_b", "l2o_w", "l2o_b", "wqk_w", "wqk_b", "cproj_w", "cproj_b")] + [
    f"L0_attn_b_{k}" for k in ("Wq", "bq", "Wk", "bk", "Wv", "bv", "Wo", "bo")] + [
    f"L0_ffn_{k}" for k in ("gate_w", "gate_b", "w1", "b1", "w2", "b2")]
_OUTS = [((B, S, D), "float32")]


def kernel(**inputs):
    import numpy as _np
    import concourse.bacc as _bacc
    from concourse import mybir as _mybir
    from concourse.bass_utils import run_bass_kernel_spmd as _run

    nc = _bacc.Bacc("TRN2", target_bir_lowering=False, num_devices=1)
    arrays, args = {}, []
    for name in _INS:
        a = _np.ascontiguousarray(inputs[name])
        arrays[f"in_{name}_dram"] = a
        args.append(nc.dram_tensor(f"in_{name}_dram", a.shape, _mybir.dt.from_np(a.dtype), kind="ExternalInput").ap())
    arrays["const_dram"] = constants()
    args.append(nc.dram_tensor("const_dram", (P, CONST_W), F32, kind="ExternalInput").ap())
    for i, (shape, dtype) in enumerate(_OUTS):
        dt = _mybir.dt.from_np(_np.dtype(dtype))
        args.append(nc.dram_tensor(f"out_{i}_dram", shape, dt, kind="ExternalOutput").ap())
    program(nc, *args)
    r = _run(nc, [arrays], core_ids=[0])
    return r.results[0]["out_0_dram"]
```

```python
from contextlib import ExitStack

import numpy as np

import concourse.bass as bass
from concourse import mybir

F32 = mybir.dt.float32
F32R = mybir.dt.float32r
BF16 = mybir.dt.bfloat16
I32 = mybir.dt.int32
ALU = mybir.AluOpType
ACT = mybir.ActivationFunctionType
AX = mybir.AxisListType.X

P = 128
B, S, D = 16, 256, 128
T = B * S
NT = T // P
H, HD, L = 16, 8, 32
G = 4
CH = 512
NCH = T // CH
CT = CH // P
UNITS = 8
E, F = 8, 512
FT = F // P
ROWS = 256
RB = ROWS // P
TILES = 2 * T // ROWS + E - 1
BLOCKS = TILES * RB
EPS = 1e-5
MASKED = -1e30

_COLS = {}
_at = 0
for _name, _n in (("ident", P), ("cos", S), ("sin", S), ("block_no", BLOCKS), ("lane_no", P), ("token_no", NT), ("prefer", E),
                  ("stack", 2),
                  ("head_mask", H), ("group_mask", G), ("rep8", P), ("rep32", P), ("rot32", P),
                  ("stack8", P), ("causal", P), ("before", P)):
    _COLS[_name] = (_at, _at + _n)
    _at += _n
CONST_W = _at
KEPT_W = _COLS["head_mask"][0]


def constants():
    c = np.zeros((P, CONST_W), np.float32)

    def put(name, a):
        c[:a.shape[0], _COLS[name][0]:_COLS[name][1]] = a

    p = np.arange(P)
    put("ident", np.eye(P, dtype=np.float32))
    put("head_mask", (p[:, None] // HD == np.arange(H)).astype(np.float32))
    put("group_mask", (p[:, None] // L == np.arange(G)).astype(np.float32))
    put("rep8", (np.arange(HD)[:, None] == p % HD).astype(np.float32))
    put("stack8", ((np.arange(HD)[:, None] == p % HD) & (p % L < 3 * HD)).astype(np.float32))
    put("rep32", (np.arange(L)[:, None] == p % L).astype(np.float32))
    rot = np.zeros((L, P), np.float32)
    for q in range(P):
        l = q % L
        rot[l + 1 if l % 2 == 0 else l - 1, q] = -1.0 if l % 2 == 0 else 1.0
    put("rot32", rot)
    inv = (np.float32(1.0) / np.power(np.float32(10000.0), np.arange(0, L, 2, dtype=np.float32) / np.float32(L))).astype(np.float32)
    ang = np.outer(np.arange(S, dtype=np.float32), inv).astype(np.float32)
    cos = np.repeat(np.cos(ang), 2, axis=1).T
    sin = np.repeat(np.sin(ang), 2, axis=1).T
    put("cos", np.tile(cos, (G, 1)).astype(np.float32))
    put("sin", np.tile(sin, (G, 1)).astype(np.float32))
    put("causal", np.where(np.arange(P)[None, :] > p[:, None], np.float32(MASKED), np.float32(0)))
    put("before", (p[:, None] < np.arange(P)[None, :]).astype(np.float32))
    put("block_no", np.broadcast_to(np.arange(BLOCKS, dtype=np.float32), (P, BLOCKS)))
    put("lane_no", np.broadcast_to(np.arange(P, dtype=np.float32), (P, P)))
    put("token_no", (p[:, None] + P * np.arange(NT) + 1).astype(np.float32))
    octet = p % L // HD
    put("stack", np.stack([-1.0 * (octet == 2), -1.0 * (octet == 1)], axis=1).astype(np.float32))
    put("prefer", np.broadcast_to(E - np.arange(E, dtype=np.float32), (P, E)))
    return c


class Order:

    def __init__(self, eng, sem):
        self.eng, self.sem, self.base, self.n = eng, sem, 0, 0

    def did(self, ins):
        self.n += 1
        return ins.then_inc(self.sem, 1)

    def settle(self):
        self.eng.wait_ge(self.sem, self.n + self.base)

    def then(self, ins):
        self.did(ins)
        self.settle()

    def loop(self, i, per):
        self.outside, self.per = self.n, per
        self.base, self.n = i * per + self.outside, 0

    def end(self, iterations):
        assert self.n == self.per, (self.n, self.per)
        self.base, self.n = 0, self.outside + iterations * self.per


class Steps:

    def __init__(self, layer):
        self.rotary = layer == "a"
        if self.rotary:
            self.make = {(1, 1): [("prep", 0)], (2, 0): [("value", 0)]}
            for g in range(G):
                self.make[(2 + g, 1)] = [("query", g)]
                self.make[(2 + g, 2)] = [("key", g)]
                self.make[(3 + g, 0)] = [("query2", g)]
            self.last_made = ("query2", G - 1)
            turns, outs = ((5, 0), (0, 2)), ((1, 1), (1, 2))
        else:
            self.make = {(2, 2): [("prep", 0)], (3, 1): [("value", 0), ("query", 0)], (3, 2): [("key", 0)]}
            for g, slots in enumerate((((4, 0), (4, 1)), ((4, 2), (5, 0)), ((5, 1), (5, 2)))):
                self.make[slots[0]] = [("query", g + 1)]
                self.make[slots[1]] = [("key", g + 1)]
            self.last_made = ("key", G - 1)
            turns, outs = ((6, 0), (1, 0)), ((1, 2), (2, 1))
        self.turn = {turns[0]: [("turn", 0)]}
        self.close = {turns[1]: [("turn", 1)], outs[0]: [("out_t", 0)], outs[1]: [("out", 0)], (7, 1): [("gate_t", 0)], (7, 2): [("gate", 0)]}
        self.hi_per = 1 + (G if self.rotary else 0)
        self.add = {} if self.rotary else {(0, 0): range(0, CT), (0, 1): range(CT, 2 * CT)}
        self.norm = ((0, 0), (0, 1)) if self.rotary else ((1, 0), (1, 1))
        self.gate_norm = ((5, 0), (6, 1)) if self.rotary else ((5, 0), (6, 2))
        self.n_make = sum(self.uses(kind) for kind, g in self.all_make())
        self.n_close = len(self.close)
        assert self.n_make % 2 == 0 and (self.n_make + 1 + self.n_close) % 2 == 0

    def uses(self, kind):
        return 2 if self.rotary and kind in ("query", "key") else 1

    def order(self, make, close):
        return [s for u in range(UNITS) for nb in range(3) for s in self.at(u, nb, make, close)]

    def at(self, u, nb, make, close):
        return (self.close.get((u, nb), []) if close else []) + (self.make.get((u, nb), []) if make else []) + self.turn.get((u, nb), [])

    def all_make(self):
        return [s for k in sorted(self.make) for s in self.make[k]]

    def made(self, c, step):
        if isinstance(c, int) and c == 0:
            order = self.all_make()
        else:
            closing = not (isinstance(c, int) and c == 1)
            order = self.order(True, closing)
        done = sum(self.uses(kind) for kind, g in order[:order.index(step) + 1])
        return done if isinstance(c, int) and c == 0 else self.before(c - 1) + done

    def before(self, c):
        if isinstance(c, int) and c == 0:
            return self.n_make
        return (c - 1) * (self.n_make + 1 + self.n_close) + (2 * self.n_make + 1)

    def readers(self, order):
        by_scalar = sum(kind in ("query", "key") for kind, g in order)
        return len(order) - by_scalar, by_scalar

    def read_before(self, c):
        vector, scalar = self.readers(self.all_make())
        if isinstance(c, int) and c == 0:
            return vector, scalar
        return (c - 1) * (vector + 1 + self.n_close) + (2 * vector + 1), (c + 1) * scalar

    def to_wait(self, c, order, at, behind):
        vector, scalar = (0, 0) if c is None else self.read_before(c)
        if at < behind:
            return (None, None) if c is None else (vector, scalar)
        more_vector, more_scalar = self.readers(order[:at - behind + 1])
        return (None, scalar + more_scalar) if order[at - behind][0] in ("query", "key") else (vector + more_vector, None)


def periods(eng, period, own=None, per=0):
    period(0, 0, True, False)
    with eng.Fori(0, NCH // 2 - 1) as i:
        if own:
            own.loop(i, per)
        period(i * 2 + 1, 1, False, False)
        period(i * 2 + 2, 0, False, False)
    if own:
        own.end(NCH // 2 - 1)
    period(NCH - 1, 1, False, True)


def stores_before(i, r):
    return 16 * (i // 4) if isinstance(i, int) else i * 4 - 4 * r


CLOSING = ("turn", "out_t", "out", "gate_t", "gate")


def hot_tiles(eng, do):
    for t in (0, 1):
        for k in (0, 1):
            do(t, k, 2 * t + k)
    with eng.Fori(0, NT // 2 - 2) as i:
        for t in (2, 3):
            for k in (0, 1):
                do(i * 2 + t, k, i * 4 + (2 * t + k))
    for t in (NT - 2, NT - 1):
        for k in (0, 1):
            do(t, k, 2 * t + k)


def norm_no(c):
    return c + 1 if isinstance(c, int) and c < 2 else c * 2 - 1


def gate_norm_no(c):
    return (2 * NCH - 1 if c == NCH - 2 else 2 * NCH) if isinstance(c, int) and c >= NCH - 2 else c * 2 + 4


PEEL = 7
assert (TILES - 4 - PEEL) % 4 == 0


def tile_slots(eng, slot):
    for i in range(PEEL):
        slot(i, i % 4, i)
    with eng.Fori(0, (TILES - 4 - PEEL) // 4) as it:
        for r in range(4):
            slot(it * 4 + (PEEL + r), (PEEL + r) % 4, PEEL + r)
    for i in range(TILES - 4, TILES):
        slot(i, i % 4, i)


def program(nc, x, c_attn_w, c_attn_b, q2l_w, q2l_b, kv2l_w, kv2l_b, l2o_w, l2o_b, wqk_w, wqk_b, cproj_w, cproj_b,
            Wq, bq, Wk, bk, Wv, bv, Wo, bo, gate_w, gate_b, w1, b1, w2, b2, const, out):
    x_tiles = x.rearrange("b s d -> (b s) d").rearrange("(t p) d -> p t d", p=P)
    out_tiles = out.rearrange("b s d -> (b s) d").rearrange("(t p) d -> p t d", p=P)
    normed = nc.dram_tensor("normed", [T, D], F32, kind="Internal").ap()
    normed_tiles = normed.rearrange("(t p) d -> p t d", p=P)
    rows_out = nc.dram_tensor("expert_rows", [TILES * ROWS, D], F32, kind="Internal").ap()

    with ExitStack() as ctx:
        def sb(name, shape, dt=F32, scope=ctx):
            return scope.enter_context(nc.sbuf_tensor(name, shape, dt))

        def sem(name):
            return ctx.enter_context(nc.semaphore(name))

        X = sb("X", [P, NT, D])
        C = sb("C", [P, KEPT_W])
        ident = C[:, _COLS["ident"][0]:_COLS["ident"][1]]

        def con(name, rows=P):
            at, end = _COLS[name]
            return C[0:rows, at:end] if end <= KEPT_W else C_prep[0:rows, at - KEPT_W:end - KEPT_W]

        ident_b = sb("ident_b", [P, P], BF16)
        causal_b = sb("causal_b", [P, P], BF16)
        before_b = sb("before_b", [P, P], BF16)
        ones_b = sb("ones_b", [P, P], BF16)
        W1 = sb("W1", [P, E * F])
        W2 = sb("W2", [P, E * FT * D])
        gate = sb("gate", [P, E])
        gate_bias = sb("gate_bias", [P, E])
        stats = sb("stats", [P, CT, 6])
        mv = sb("mv", [P, CT, 2])
        rstd = sb("rstd", [P, CT])
        var_eps = sb("var_eps", [P, CT])
        scratch1 = sb("scratch1", [1, 1])
        scratch2 = sb("scratch2", [1, 1])
        neg_half = sb("neg_half", [P, CT])
        xn = sb("xn", [P, CT, D])
        layers = {}
        for name, n_mats in (("a", 4), ("b", 2)):
            layers[name] = dict(
                hi=[sb(f"{name}_proj{m}_hi", [P, H * L], F32R) for m in range(n_mats)],
                lo=[sb(f"{name}_proj{m}_lo", [P, H * L], F32R) for m in range(n_mats)],
                v_hi=sb(f"{name}_v_hi", [P, D], F32R), v_lo=sb(f"{name}_v_lo", [P, D], F32R),
                bias=sb(f"{name}_bias", [P, n_mats, G]), v_bias=sb(f"{name}_v_bias", [P, D]),
                out_w=sb(f"{name}_out_w", [P, D]), out_b=sb(f"{name}_out_b", [P, D]))
        wqk_blk = sb("wqk_blk", [P, P])
        wqk_bias = sb("wqk_bias", [P, 1])
        b1_cols = sb("b1_cols", [P, E * FT])
        logit = sb("logit", [P, NT, E])
        slot_of = sb("slot_of", [P, 2 * NT], I32)
        weight = [sb(f"weight{k}", [P, NT]) for k in range(2)]
        got = sb("got", [P, 2 * CT, D])
        v_aug = sb("v_aug", [P, 2, CT, H, L])

        with ExitStack() as att:
            xt_hi = sb("xt_hi", [P, CH], F32R, att)
            xt_lo = sb("xt_lo", [P, CH], F32R, att)
            q_hi = sb("q_hi", [P, 2, G, 2, P], F32R, att)
            q_lo = sb("q_lo", [P, 2, G, 2, P], F32R, att)
            q_whole = sb("q_whole", [P, 2, G, 2, P], F32, att)
            k_hi = sb("k_hi", [P, 2, G, 2, S], F32R, att)
            k_lo = sb("k_lo", [P, 2, G, 2, S], F32R, att)
            k_whole = sb("k_whole", [P, 2, G, 2, P], F32, att)
            prob = sb("prob", [P, 3, 512], F32, att)
            prob_t = sb("prob_t", [P, 2, 3, 512], F32, att)
            sums = sb("sums", [P, 2, 2, H], F32, att)
            o_t = sb("o_t", [P, S], F32, att)
            Y = sb("Y", [P, 2, CT, D], F32, att)
            y_t = sb("y_t", [P, CH], F32, att)
            rope_q = sb("rope_q", [P, 2, CH], F32, att)
            rope_k = sb("rope_k", [P, 2, CH], F32, att)
            neg_max = sb("neg_max", [P, 3, G], F32, att)
            inv_sum = sb("inv_sum", [P, 2, H], F32, att)
        with ExitStack() as moe:
            xg = sb("xg", [P, 4, RB, D], F32, moe)
            xg_hi = sb("xg_hi", [P, 2, ROWS], F32R, moe)
            xg_lo = sb("xg_lo", [P, 2, ROWS], F32R, moe)
            w1_hi = sb("w1_hi", [P, 2, F], F32R, moe)
            w1_lo = sb("w1_lo", [P, 2, F], F32R, moe)
            hid = sb("hid", [P, 2, FT, ROWS], F32, moe)
            b2_rows = sb("b2_rows", [P, E, D], F32, moe)
            y_rows = sb("y_rows", [P, 4, RB, D], F32, moe)
            route = [sb(f"route{k}", [P, NT, E], F32, moe) for k in range(6)]
            chosen_b = sb("chosen_b", [P, NT, E], BF16, moe)
            col = [sb(f"col{k}", [P, NT], F32, moe) for k in range(5)]
            ecol = [sb(f"ecol{k}", [P, E], F32, moe) for k in range(5)]
            ecol_i = [sb(f"ecol_i{k}", [P, E], I32, moe) for k in range(2)]
            slot_f = sb("slot_f", [P, 2 * NT], F32, moe)
            block_i = sb("block_i", [P, 2 * NT], I32, moe)
            block_f = sb("block_f", [P, 2 * NT], F32, moe)
            lane_f = sb("lane_f", [P, 2 * NT], F32, moe)
            lane_hot = sb("lane_hot", [P, 4, P], F32R, moe)
            block_hot = sb("block_hot", [P, 4, BLOCKS], F32R, moe)
            source_f = sb("source_f", [P, 2, BLOCKS], F32, moe)
            source = sb("source", [P, BLOCKS], I32, moe)
            emap_f = sb("emap_f", [1, TILES, E], F32, moe)
            emap_s = sb("emap_s", [1, 2, TILES], F32, moe)
            expert_of = sb("expert_of", [1, TILES], I32, moe)
        with ExitStack() as prep:
            C_prep = sb("C_prep", [P, CONST_W - KEPT_W], F32, prep)
            cw = sb("cw", [P, 3, D], F32, prep)
            cp = sb("cp", [P, D], F32, prep)
            wb = sb("wb", [P, 4, D], F32, prep)
            q2l_t = sb("q2l_t", [HD, L], F32, prep)
            kv2l_t = sb("kv2l_t", [HD, L], F32, prep)
            kv2l_n = sb("kv2l_n", [L, HD], F32, prep)
            l2o_t = sb("l2o_t", [L, HD], F32, prep)
            wqk_t = sb("wqk_t", [L, L], F32, prep)
            b3 = sb("b3", [P, 3], F32, prep)
            lat_b = sb("lat_b", [L, 3], F32, prep)
            l2o_row = sb("l2o_row", [1, HD], F32, prep)
            rep = sb("rep", [P, 104], F32, prep)
            m_t = sb("m_t", [HD, HD], F32, prep)
            blk = [sb(f"blk{k}", [P, H, L], F32, prep) for k in range(4)]
            blk_v = sb("blk_v", [P, H, HD], F32, prep)
            blk_vb = sb("blk_vb", [P, H, HD], F32, prep)
            kvb_rep = sb("kvb_rep", [L, P], F32, prep)
            ones = sb("ones", [P, P], F32, prep)
            pad = [sb(f"pad{k}", [P, H, L], F32, prep) for k in range(2)]
            bqk = sb("bqk", [HD, 2, H], F32, prep)
            bqk_all = sb("bqk_all", [P, 2, G, G], F32, prep)
            bias_part = sb("bias_part", [P, 4], F32, prep)

        bank = [ctx.enter_context(nc.psum_tensor(f"bank{k}", [P, 512], F32)) for k in range(8)]
        s_bank, t_bank, o_bank, w_bank = bank[0:3], bank[3:5], bank[5], bank[6:8]
        r_bank, h_bank, y_bank = bank[6:8], (bank[0:2], bank[2:4]), bank[4:6]

        first_loaded = sem("first_loaded")
        x0_loaded = sem("x0_loaded")
        rest_loaded = sem("rest_loaded")
        experts_loaded = sem("experts_loaded")
        constant_ready = sem("constant_ready")
        pe_prep = sem("pe_prep")
        dve_prep = sem("dve_prep")
        dve_own = sem("dve_own")
        att_sems = {n: {k: sem(f"{n}_{k}") for k in (
            "scores_ready", "max_ready", "probs_ready", "pt_ready", "pt_copied_act", "pt_copied_dve", "pv_ready",
            "o_copied", "shared_ready", "shared_free", "ln_ready", "var_ready", "rstd_ready", "hi_ready",
            "read", "negated", "summed", "key_hi_ready", "key_lo_ready")} for n in "ab"}
        moe_sems = {n: {k: sem(f"m{n}_{k}") for k in (
            "gap_ready", "exp_ready", "mask_ready", "rank_ready", "hot_ready", "blocks_ready", "block_hot_ready", "hot_used", "slots_ready",
            "row0", "row1", "row2", "row3", "turned", "turned_hi", "split", "staged", "up_ready", "gelu_ready",
            "down_ready", "bias_ready", "y_ready", "stored0", "stored1", "stored2", "stored3",
            *(f"got{k}" for k in range(2 * CT)), "got_used")} for n in "12"}
        kept = {n: sem(f"kept_{n}") for n in "ab"}
        attended = {n: sem(f"attended_{n}") for n in "ab"}
        stored = sem("stored")

        block = ctx.enter_context(nc.Block())

        N_FIRST, N_REST = 13, 15

        @block.sync
        def _(sp):
            firsts = [(C_prep[:, :], const[:, KEPT_W:CONST_W]), (kv2l_n[:, :], kv2l_w), (l2o_t[:, :], l2o_w.rearrange("o l -> l o")),
                      (q2l_t[:, :], q2l_w.rearrange("l d -> d l")), (kv2l_t[:, :], kv2l_w.rearrange("l d -> d l")),
                      (wqk_t[:, :], wqk_w.rearrange("o l -> l o")),
                      *((lat_b[:, k:k + 1], v.rearrange("(l a) -> l a", a=1)) for k, v in enumerate((q2l_b, kv2l_b, wqk_b))),
                      (cw[:, :, :], c_attn_w.rearrange("(s p) c -> p s c", p=P)), (b3[:, :], c_attn_b.rearrange("(s p) -> p s", p=P)),
                      (l2o_row[:, :], l2o_b.rearrange("(a o) -> a o", a=1)), (cp[:, :], cproj_w)]
            assert len(firsts) == N_FIRST
            with nc.allow_non_contiguous_dma(reason="small transposed weights"):
                for dst, src in firsts:
                    sp.dma_start(dst, src).then_inc(first_loaded, 16)
            sp.dma_start(W1[:, :].rearrange("p (e f) -> p e f", e=E), w1.rearrange("e d f -> d e f")).then_inc(experts_loaded, 16)
            sp.dma_start(W2[:, :].rearrange("p (e k d) -> p e k d", e=E, k=FT), w2.rearrange("e (k p) d -> p e k d", p=P)).then_inc(experts_loaded, 16)
            for n, e_ in (("a", "1"), ("b", "2")):
                m, me = att_sems[n], moe_sems[e_]

                def keep(c):
                    sp.wait_ge(m["ln_ready"], gate_norm_no(c))
                    sp.dma_start(normed_tiles[:, bass.ds(c * CT, CT), :], xn[:, :, :]).then_inc(kept[n], 16)

                with sp.Fori(0, NCH - 2) as c:
                    keep(c)
                keep(NCH - 2)
                keep(NCH - 1)

                sp.wait_ge(attended[n], 1)
                sp.dma_start(b2_rows[:, :, :].rearrange("p e d -> p (e d)"), b2.rearrange("e d -> (e d)").partition_broadcast(P)).then_inc(me["bias_ready"], 16)

                def store(i, r, least):
                    sp.wait_ge(me["y_ready"], i + 1)
                    sp.dma_start(rows_out[bass.ds(i * ROWS, ROWS), :].rearrange("(b p) d -> p b d", p=P), y_rows[:, r, :, :]).then_inc(me[f"stored{r}"], 16)

                tile_slots(sp, store)
            for c in range(NCH):
                sp.wait_ge(moe_sems["2"]["got_used"], 2 * CT * (c + 1))
                sp.dma_start(out_tiles[:, c * CT:(c + 1) * CT, :], X[:, c * CT:(c + 1) * CT, :]).then_inc(stored, 16)
            sp.wait_ge(stored, 16 * NCH)

        @block.gpsimd
        def _(pool):
            nc.gpsimd.memset(neg_half[:, :], -0.5).then_inc(constant_ready, 1)
            pool.wait_ge(constant_ready, 1)

            def inverse_root(m, nth):
                pool.wait_ge(m["var_ready"], nth)
                nc.gpsimd.tensor_tensor(rstd[:, :], var_eps[:, :], neg_half[:, :], ALU.pow).then_inc(m["rstd_ready"], 1)

            def rotary(c, par):
                m, steps = att_sems["a"], Steps("a")
                inverse_root(m, norm_no(c))
                for g in range(G):
                    pool.wait_ge(m["shared_free"], steps.made(c, ("query", g)))
                    nc.gpsimd.tensor_tensor(rope_q[:, 0, :], rope_q[:, 0, :], rope_q[:, 1, :], ALU.add).then_inc(m["summed"], 1)
                    pool.wait_ge(m["shared_free"], steps.made(c, ("key", g)))
                    half = lambda part, at: rope_k[:, part, :].rearrange("p (b s) -> p b s", b=2)[:, :, at * P:(at + 1) * P]
                    nc.gpsimd.tensor_tensor(k_whole[:, par, g, :, :], half(0, 0), half(1, 0), ALU.add)
                    nc.gpsimd.tensor_tensor(half(0, 1), half(0, 1), half(1, 1), ALU.add).then_inc(m["summed"], 1)
                    pool.wait_ge(m["key_hi_ready"], c * G + (g + 1))
                    nc.gpsimd.tensor_tensor(k_lo[:, par, g, :, 0:P], k_whole[:, par, g, :, :], k_hi[:, par, g, :, 0:P].bitcast(F32), ALU.subtract)
                    nc.gpsimd.tensor_tensor(k_lo[:, par, g, :, P:S], half(0, 1), k_hi[:, par, g, :, P:S].bitcast(F32), ALU.subtract).then_inc(m["key_lo_ready"], 1)

            def stacked(c, par):
                m = att_sems["b"]
                inverse_root(m, norm_no(c))
                for g in range(G):
                    half = lambda part, at: rope_q[:, part, :].rearrange("p (b s) -> p b s", b=2)[:, :, at * P:(at + 1) * P]
                    pool.wait_ge(m["negated"], c * 2 * G + 2 * g + 1)
                    nc.gpsimd.tensor_tensor(q_lo[:, par, g, :, :], half(0, 0), half(1, 0), ALU.add)
                    nc.gpsimd.tensor_tensor(q_hi[:, par, g, :, :], half(0, 1), half(1, 1), ALU.add).then_inc(m["summed"], 1)
                    pool.wait_ge(m["negated"], c * 2 * G + 2 * g + 2)
                    nc.gpsimd.tensor_tensor(k_hi[:, par, g, :, :].rearrange("p b s -> p (b s)"), rope_k[:, 0, :], rope_k[:, 1, :], ALU.add).then_inc(m["summed"], 1)
                    if c + 1 < NCH:
                        gather_results("1", c + 1, range(2 * g, 2 * g + 2))

            def gather_results(n, c, rows=range(2 * CT)):
                m = moe_sems[n]
                for k in rows:
                    t, which = c * CT + k // 2, k % 2
                    if c:
                        pool.wait_ge(m["got_used"], 2 * CT * (c - 1) + k + 1)
                    nc.gpsimd.indirect_dma_start(
                        out=got[:, k, :], out_offset=None, in_=rows_out,
                        in_offset=bass.IndirectOffsetOnAxis(ap=slot_of[:, which * NT + t:which * NT + t + 1], axis=0)).then_inc(m[f"got{k}"], 16)

            def block_hots(n):
                m = moe_sems[n]
                pool.wait_ge(m["blocks_ready"], 1)
                for t in range(NT):
                    n_, k = 2 * t + 1, 1
                    if n_ >= 4:
                        pool.wait_ge(m["hot_used"], n_ - 3)
                    where = t + k * NT
                    nc.gpsimd.tensor_scalar(block_hot[:, n_ % 4, :], con("block_no"), block_f[:, where:where + 1],
                                            con("token_no")[:, t:t + 1], ALU.is_equal, ALU.mult).then_inc(m["block_hot_ready"], 1)

            def gather_rows(n):
                m = moe_sems[n]
                pool.wait_ge(m["slots_ready"], 1)
                pool.wait_ge(kept["a" if n == "1" else "b"], 16 * NCH)
                for i in range(TILES):
                    if i >= 4:
                        pool.wait_ge(m["turned"], i - 3)
                    for b_ in range(RB):
                        k = i * RB + b_
                        nc.gpsimd.indirect_dma_start(
                            out=xg[:, i % 4, b_, :], out_offset=None, in_=normed,
                            in_offset=bass.IndirectOffsetOnAxis(ap=source[:, k:k + 1], axis=0)).then_inc(m[f"row{i % 4}"], 16)
                for r in range(4):
                    pool.wait_ge(m[f"stored{r}"], 16 * len(range(r, TILES, 4)))

            rotary(0, 0)
            rotary(1, 1)
            with pool.Fori(0, NCH // 2 - 1) as i:
                for odd in (0, 1):
                    rotary(i * 2 + (2 + odd), odd)
                    inverse_root(att_sems["a"], gate_norm_no(i * 2 + odd))
            inverse_root(att_sems["a"], gate_norm_no(NCH - 2))
            inverse_root(att_sems["a"], gate_norm_no(NCH - 1))
            block_hots("1")
            gather_rows("1")
            gather_results("1", 0)
            for c in range(NCH):
                stacked(c, c % 2)
                if c >= 2:
                    inverse_root(att_sems["b"], gate_norm_no(c - 2))
            inverse_root(att_sems["b"], gate_norm_no(NCH - 2))
            inverse_root(att_sems["b"], gate_norm_no(NCH - 1))
            block_hots("2")
            gather_rows("2")
            for c in range(NCH):
                gather_results("2", c)

        @block.vector
        def _(dve):
            own = Order(dve, dve_own)
            v = nc.vector

            def statistics(m, c):
                first_tile = c * CT
                for t in range(CT):
                    own.did(v.bn_stats(stats[:, t, :], X[:, bass.ds(first_tile + t, 1), :].rearrange("p a d -> p (a d)")))
                own.settle()
                v.memset(scratch2[:, :], 0.0)
                for t in range(CT):
                    own.did(v.bn_aggr(mv[:, t, :], stats[:, t, :]))
                own.settle()
                v.tensor_scalar(var_eps[:, :].unsqueeze(2), mv[:, :, 1:2], EPS, None, ALU.add).then_inc(m["var_ready"], 1)

            def normalise_rows(m, c, nth):
                first_tile = c * CT
                dve.wait_ge(m["rstd_ready"], nth)
                for t in range(CT):
                    ins = v.tensor_scalar(xn[:, t, :], X[:, bass.ds(first_tile + t, 1), :].rearrange("p a d -> p (a d)"),
                                          mv[:, t, 0:1], rstd[:, t:t + 1], ALU.subtract, ALU.mult)
                ins.then_inc(m["ln_ready"], 1)
            LN_OWN = 2 * CT

            own.did(v.memset(v_aug[:, :, :, :, :].rearrange("p a t h l -> p (a t h) l"), 0.0))
            own.did(v.memset(ones[:, :], 1.0))
            own.did(v.memset(ones_b[:, :], 1.0))
            for k in range(2):
                own.did(v.memset(pad[k][:, :, :], 0.0))
            own.settle()
            dve.wait_ge(first_loaded, 16 * N_FIRST)
            own.did(v.tensor_scalar(kvb_rep[:, :], ones[0:L, :], lat_b[:, 1:2], None, ALU.mult))
            own.did(v.tensor_scalar(wqk_t[:, :], wqk_t[:, :], float(L) ** -0.5, None, ALU.mult))
            own.did(v.tensor_scalar(lat_b[:, 2:3], lat_b[:, 2:3], float(L) ** -0.5, None, ALU.mult))
            own.settle()
            v.memset(scratch1[:, :], 0.0).then_inc(dve_prep, 1)
            dve.wait_ge(pe_prep, 1)
            v.tensor_copy(m_t[:, :], bank[0][0:HD, 0:HD]).then_inc(dve_prep, 1)
            dve.wait_ge(pe_prep, 2)
            own.then(v.tensor_copy(rep[:, :], bank[1][:, 0:104]))
            mask_h = con("head_mask").unsqueeze(2).broadcast_to([P, H, L])
            for k, lo_ in ((0, 0), (2, L)):
                own.did(v.tensor_tensor(blk[k][:, :, :], rep[:, lo_:lo_ + L].unsqueeze(1).broadcast_to([P, H, L]), mask_h, ALU.mult))
            own.did(v.tensor_tensor(wqk_blk[:, :].rearrange("p (j l) -> p j l", j=G),
                                    rep[:, 2 * L:3 * L].unsqueeze(1).broadcast_to([P, G, L]),
                                    con("group_mask").unsqueeze(2).broadcast_to([P, G, L]), ALU.mult))
            own.did(v.tensor_tensor(blk_v[:, :, :], rep[:, 96:104].unsqueeze(1).broadcast_to([P, H, HD]),
                                    con("head_mask").unsqueeze(2).broadcast_to([P, H, HD]), ALU.mult))
            own.settle()
            for k in (0, 2):
                src = blk[k][:, :, :].rearrange("p h (i two) -> p (h i) two", two=2)
                dst = blk[k + 1][:, :, :].rearrange("p h (i two) -> p (h i) two", two=2)
                own.did(v.tensor_scalar(dst[:, :, 0:1], src[:, :, 1:2], -1.0, None, ALU.mult))
                own.did(v.tensor_copy(dst[:, :, 1:2], src[:, :, 0:1]))
            own.did(v.tensor_scalar(blk_vb[:, :, :], blk_v[:, :, :], b3[:, 2:3], None, ALU.mult))
            own.settle()
            v.memset(scratch1[:, :], 0.0).then_inc(dve_prep, 1)
            la, lb = layers["a"], layers["b"]

            def halves(hi, lo_, src):
                own.then(v.tensor_copy(hi, src))
                own.did(v.tensor_tensor(lo_, src, hi.bitcast(F32), ALU.subtract))

            dve.wait_ge(x0_loaded, 16)
            statistics(att_sems["a"], 0)
            for k in range(4):
                dve.wait_ge(pe_prep, 3 + k)
                halves(la["hi"][k][:, :], la["lo"][k][:, :], bank[k][:, :])
                if k == 0:
                    normalise_rows(att_sems["a"], 0, norm_no(0))
            dve.wait_ge(pe_prep, 7)
            halves(la["v_hi"][:, :], la["v_lo"][:, :], bank[4][:, 0:D])
            own.did(v.tensor_copy(la["v_bias"][:, :], bank[4][:, D:2 * D]))
            dve.wait_ge(rest_loaded, 16 * N_REST)
            for dst, src in ((ident_b, "ident"), (causal_b, "causal"), (before_b, "before")):
                own.did(v.tensor_copy(dst[:, :], con(src)))
            dve.wait_ge(pe_prep, 8)
            own.did(v.tensor_copy(la["out_w"][:, :], bank[6][:, 0:D]))
            own.did(v.tensor_copy(lb["out_w"][:, :], bank[6][:, D:2 * D]))
            for copy in range(3):
                cols = slice(copy * HD, (copy + 1) * HD)
                own.did(v.tensor_scalar(pad[0][:, :, cols], bank[7][:, 0:D].rearrange("p (h d) -> p h d", h=H), float(HD) ** -0.5, None, ALU.mult))
                own.did(v.tensor_copy(pad[1][:, :, cols], bank[7][:, D:2 * D].rearrange("p (h d) -> p h d", h=H)))
            own.settle()
            halves(lb["v_hi"][:, :], lb["v_lo"][:, :], bank[7][:, 2 * D:3 * D])
            for k in range(2):
                halves(lb["hi"][k][:, :], lb["lo"][k][:, :], pad[k][:, :, :].rearrange("p h l -> p (h l)"))
            dve.wait_ge(pe_prep, 9)
            own.then(v.tensor_copy(bias_part[:, :], bank[5][:, 4 * G:4 * G + 4]))
            own.did(v.tensor_tensor(la["bias"][:, :, :], bank[5][:, 0:4 * G].rearrange("p (m g) -> p m g", m=4),
                                    bias_part[:, :].unsqueeze(2).broadcast_to([P, 4, G]), ALU.add))
            own.did(v.tensor_copy(wqk_bias[:, :], bank[5][:, 4 * G + 4:4 * G + 5]))
            own.then(v.tensor_tensor(bqk_all[:, :, :, :].rearrange("p m g j -> p (m g) j"), bank[5][:, 32:32 + 2 * H].rearrange("p (m j) -> p m j", j=G),
                                     con("group_mask").unsqueeze(1).broadcast_to([P, 2 * G, G]), ALU.mult))
            own.then(v.tensor_reduce(lb["bias"][:, :, :], bqk_all[:, :, :, :], AX, ALU.add))
            own.then(v.tensor_scalar(lb["bias"][:, 0, :], lb["bias"][:, 0, :], float(HD) ** -0.5, None, ALU.mult))
            v.memset(scratch1[:, :], 0.0).then_inc(dve_prep, 1)

            def attention(n):
                m, w, steps = att_sems[n], layers[n], Steps(n)

                def step(kind, g, c, par, k, at):
                    if steps.rotary or kind not in ("query", "key"):
                        dve.wait_ge(m["shared_ready"], k + 1)
                    free = m["shared_free"]
                    bank_ = w_bank[at % 2]
                    hi_per = steps.hi_per
                    two = lambda ap: ap.rearrange("p (b s) -> p b s", b=2)
                    if kind == "prep":
                        dve.wait_ge(m["hi_ready"], c * hi_per + 1)
                        v.tensor_tensor(xt_lo[:, :], bank_[:, :], xt_hi[:, :].bitcast(F32), ALU.subtract).then_inc(free, 1)
                    elif kind == "value":
                        for j in range(G):
                            heads = lambda ap: ap.rearrange("p (g j d) -> p g j d", g=G, j=G)[:, :, j, :]
                            ins = v.tensor_tensor(v_aug[:, par, :, j::G, j * HD:(j + 1) * HD],
                                                  bank_[:, :].rearrange("p (t g j d) -> p t g j d", t=CT, g=G, j=G)[:, :, :, j, :],
                                                  heads(w["v_bias"][:, :]).unsqueeze(1).broadcast_to([P, CT, G, HD]), ALU.add)
                        ins.then_inc(free, 1)
                    elif kind == "turn":
                        own.then(v.reciprocal(inv_sum[:, :, :], sums[:, g, :, :]))
                        v.tensor_tensor(Y[:, par, 2 * g:2 * g + 2, :].rearrange("p q (h d) -> p q h d", h=H),
                                        bank_[:, 0:S].rearrange("p (q h d) -> p q h d", q=2, h=H),
                                        inv_sum[:, :, :].unsqueeze(3).broadcast_to([P, 2, H, HD]), ALU.mult).then_inc(free, 1)
                    elif kind in ("query", "key") and steps.rotary:
                        dst, w0 = (rope_q, 0) if kind == "query" else (rope_k, 2)
                        if kind == "key" and not (isinstance(c, int) and c == 0 and g == 0):
                            dve.wait_ge(m["key_lo_ready"], c * G + g)
                        for part, table in enumerate(("cos", "sin")):
                            bank_ = w_bank[(at + part) % 2]
                            if part:
                                dve.wait_ge(m["shared_ready"], k + 2)
                            v.scalar_tensor_tensor(two(dst[:, part, :]), two(bank_[:, :]), w["bias"][:, w0 + part, g:g + 1],
                                                         con(table).unsqueeze(1).broadcast_to([P, 2, S]), ALU.add, ALU.mult).then_inc(free, 1)
                    elif kind == "query2":
                        dve.wait_ge(m["hi_ready"], c * hi_per + (g + 2))
                        v.scalar_tensor_tensor(q_lo[:, par, g, :, :], two(bank_[:, :])[:, :, P:S], wqk_bias[:, 0:1],
                                               q_hi[:, par, g, :, :].bitcast(F32), ALU.add, ALU.subtract).then_inc(free, 1)
                    elif kind in ("query", "key"):
                        which = 0 if kind == "query" else 1
                        dve.wait_ge(m["read"], c * 2 * G + (2 * g + 1 + which))
                        values = (rope_q, rope_k)[which]
                        v.tensor_scalar(values[:, 1, :].bitcast(F32R), values[:, 0, :], con("stack")[:, which:which + 1], None,
                                        ALU.mult).then_inc(m["negated"], 1)
                    elif kind == "out_t":
                        v.tensor_copy(y_t[:, :], bank_[:, :]).then_inc(free, 1)
                    elif kind == "out":
                        xs = X[:, bass.ds(c * CT, CT), :]
                        own.then(v.tensor_tensor(xs, bank_[:, :].rearrange("p (t d) -> p t d", t=CT), xs, ALU.add))
                        v.tensor_tensor(xs, xs, w["out_b"][:, :].unsqueeze(1).broadcast_to([P, CT, D]), ALU.add).then_inc(free, 1)
                    elif kind == "gate_t":
                        v.tensor_copy(y_t[:, :], bank_[:, :]).then_inc(free, 1)
                    elif kind == "gate":
                        v.tensor_tensor(logit[:, bass.ds(c * CT, CT), :], bank_[:, 0:CT * E].rearrange("p (t e) -> p t e", t=CT),
                                        gate_bias[:, :].unsqueeze(1).broadcast_to([P, CT, E]), ALU.add).then_inc(free, 1)

                def row_max(unit, nb):
                    heads = G if nb == 0 else 2
                    dve.wait_ge(m["scores_ready"], unit * 3 + (nb + 1))
                    v.tensor_reduce(neg_max[:, nb, 0:heads], s_bank[nb][:, :].rearrange("p (h k) -> p h k", h=heads), AX, ALU.max,
                                    negate=True).then_inc(m["max_ready"], 1)

                def copy_o(unit):
                    dve.wait_ge(m["pv_ready"], unit + 1)
                    v.tensor_copy(o_t[:, :], o_bank[:, 0:S]).then_inc(m["o_copied"], 1)

                if n == "b":
                    add_expert_rows("1", 0, range(2 * CT))
                    statistics(m, 0)
                    normalise_rows(m, 0, norm_no(0))
                k = 0
                for kind, g in steps.all_make():
                    step(kind, g, 0, 0, k, k)
                    k += steps.uses(kind)
                for nb in range(3):
                    row_max(0, nb)

                def period(c, par, first, last):
                    at = 0
                    for u in range(UNITS):
                        unit = c * UNITS + u
                        for nb in range(3):
                            if nb == 1:
                                dve.wait_ge(m["pt_ready"], unit * 3 + 2)
                                v.tensor_copy(prob_t[:, u % 2, 1, :], t_bank[(3 * u + 1) % 2][:, :]).then_inc(m["pt_copied_dve"], 1)
                            if not (last and u == UNITS - 1):
                                row_max(unit + 1, nb)
                            if nb == 1 and u % G == 0 and not (first and u == 0):
                                copy_o(unit - 1)
                            if not last:
                                if (u, nb) == steps.norm[0]:
                                    statistics(m, c + 1)
                                if (u, nb) in steps.add:
                                    add_expert_rows("1", c + 1, steps.add[u, nb])
                                if (u, nb) == steps.norm[1]:
                                    normalise_rows(m, c + 1, norm_no(1) if first else norm_no(c + 1))
                            if not first:
                                if (u, nb) == steps.gate_norm[0]:
                                    statistics(m, c - 1)
                                if (u, nb) == steps.gate_norm[1]:
                                    normalise_rows(m, c - 1, gate_norm_no(c - 1))
                            for kind, g in steps.at(u, nb, not last, not first):
                                where = (c, par) if (kind, g) == ("turn", 0) else (c - 1 if kind in CLOSING else c + 1, 1 - par)
                                step(kind, g, *where, steps.before(c) + at, at + 1 - first)
                                at += steps.uses(kind)
                    if not first:
                        dve.wait_ge(kept[n], c * 16)
                        v.memset(scratch2[:, :], 0.0)

                periods(dve, period, own, 2 * (2 + 2 * LN_OWN + 1))
                end = NCH * UNITS - 1
                copy_o(end)
                k = steps.before(NCH - 1) + 1 + steps.n_close
                free = k if steps.rotary else steps.read_before(NCH - 1)[0] + 1 + steps.n_close
                step("turn", 1, NCH - 1, 1, k, k)
                dve.wait_ge(m["shared_free"], free + 1)
                step("out_t", 0, NCH - 1, 1, k + 1, k + 1)
                step("out", 0, NCH - 1, 1, k + 2, k + 2)
                dve.wait_ge(m["shared_free"], free + 3)
                statistics(m, NCH - 1)
                normalise_rows(m, NCH - 1, gate_norm_no(NCH - 1))
                step("gate_t", 0, NCH - 1, 1, k + 3, k + 3)
                step("gate", 0, NCH - 1, 1, k + 4, k + 4)
                dve.wait_ge(m["shared_free"], free + 5)
                v.memset(scratch1[:, :], 0.0).then_inc(attended[n], 1)
                dve.wait_ge(attended[n], 1)

            def experts(n):
                m = moe_sems[n]

                over_t = lambda ap: ap.unsqueeze(1).broadcast_to([P, NT, E])
                over_e = lambda ap: ap.unsqueeze(2).broadcast_to([P, NT, E])
                best, scratch = col[0:2], col[2:5]
                first_hot, second_hot, rest, work, cum_a, cum_b = route

                def choose(values, top, hot):
                    own.then(v.tensor_reduce(top[:, :], values[:, :, :], AX, ALU.max))
                    own.then(v.tensor_tensor(work[:, :, :], values[:, :, :], over_e(top[:, :]), ALU.is_equal))
                    own.then(v.tensor_tensor(work[:, :, :], work[:, :, :], over_t(con("prefer")), ALU.mult))
                    own.then(v.tensor_reduce(scratch[0][:, :], work[:, :, :], AX, ALU.max))
                    own.then(v.tensor_tensor(hot[:, :, :], work[:, :, :], over_e(scratch[0][:, :]), ALU.is_equal))

                choose(logit, best[0], first_hot)
                own.then(v.scalar_tensor_tensor(rest[:, :, :], first_hot[:, :, :], -3e38, logit[:, :, :], ALU.mult, ALU.add))
                choose(rest, best[1], second_hot)
                v.tensor_tensor(scratch[1][:, :], best[1][:, :], best[0][:, :], ALU.subtract).then_inc(m["gap_ready"], 1)
                v.tensor_tensor(chosen_b[:, :, :], first_hot[:, :, :], second_hot[:, :, :], ALU.add).then_inc(m["mask_ready"], 1)
                dve.wait_ge(m["exp_ready"], 1)
                own.then(v.tensor_scalar(scratch[0][:, :], scratch[2][:, :], 1.0, None, ALU.add))
                own.then(v.reciprocal(weight[0][:, :], scratch[0][:, :]))
                own.then(v.tensor_tensor(weight[1][:, :], weight[0][:, :], scratch[2][:, :], ALU.mult))
                dve.wait_ge(m["rank_ready"], 1)
                flat = lambda ap: ap[:, :, :].rearrange("p t e -> p (t e)")
                own.then(v.tensor_copy(flat(cum_a), w_bank[1][:, 0:NT * E]))
                a, b_ = cum_a, cum_b
                shift = 1
                while shift < NT:
                    own.did(v.tensor_copy(b_[:, 0:shift, :], a[:, 0:shift, :]))
                    own.then(v.tensor_tensor(b_[:, shift:NT, :], a[:, shift:NT, :], a[:, 0:NT - shift, :], ALU.add))
                    a, b_ = b_, a
                    shift *= 2
                own.then(v.tensor_scalar(ecol[0][:, :], a[:, NT - 1, :], float(ROWS - 1), None, ALU.add))
                own.then(v.tensor_copy(ecol_i[0][:, :], ecol[0][:, :]))
                own.then(v.tensor_scalar(ecol_i[1][:, :], ecol_i[0][:, :], ROWS.bit_length() - 1, None, ALU.logical_shift_right))
                own.then(v.tensor_copy(ecol[1][:, :], ecol_i[1][:, :]))
                ca, cb = ecol[1], ecol[2]
                spare = [ecol[2], ecol[3], ecol[4]]
                for k, shift in enumerate((1, 2, 4)):
                    cb = spare[k]
                    own.did(v.tensor_copy(cb[:, 0:shift], ca[:, 0:shift]))
                    own.then(v.tensor_tensor(cb[:, shift:E], ca[:, shift:E], ca[:, 0:E - shift], ALU.add))
                    ca = cb
                own.then(v.tensor_tensor(ecol[0][:, :], ca[:, :], ecol[1][:, :], ALU.subtract))
                own.then(v.tensor_scalar(ecol[0][:, :], ecol[0][:, :], float(ROWS), None, ALU.mult))
                own.then(v.tensor_tensor(flat(b_), flat(a), w_bank[1][:, 0:NT * E], ALU.subtract))
                own.then(v.tensor_tensor(flat(a), w_bank[0][:, 0:NT * E], flat(b_), ALU.add))
                own.then(v.tensor_tensor(b_[:, :, :], a[:, :, :], over_t(ecol[0][:, :]), ALU.add))
                for k, hot in enumerate((first_hot, second_hot)):
                    own.then(v.tensor_tensor(work[:, :, :], hot[:, :, :], b_[:, :, :], ALU.mult))
                    own.then(v.tensor_reduce(slot_f[:, k * NT:(k + 1) * NT], work[:, :, :], AX, ALU.add))
                own.then(v.tensor_copy(slot_of[:, :], slot_f[:, :]))
                own.then(v.tensor_scalar(block_i[:, :], slot_of[:, :], P.bit_length() - 1, None, ALU.logical_shift_right))
                own.did(v.tensor_copy(block_f[:, :], block_i[:, :]))
                own.settle()
                v.memset(scratch1[:, :], 0.0).then_inc(m["blocks_ready"], 1)
                own.then(v.scalar_tensor_tensor(lane_f[:, :], block_f[:, :], -float(P), slot_f[:, :], ALU.mult, ALU.add))

                def hot(t, k, n_):
                    ring = hot_ring[0]
                    if not (isinstance(n_, int) and n_ < 4):
                        dve.wait_ge(m["hot_used"], n_ - 3)
                    where = bass.ds(t + k * NT, 1)
                    if k == 0:
                        v.tensor_scalar(block_hot[:, ring, :], con("block_no"), block_f[:, where], con("token_no")[:, bass.ds(t, 1)],
                                        ALU.is_equal, ALU.mult)
                    v.tensor_scalar(lane_hot[:, ring, :], con("lane_no"), lane_f[:, where], None, ALU.is_equal).then_inc(m["hot_ready"], 1)
                    hot_ring[0] = (ring + 1) % 4

                hot_ring = [0]
                hot_tiles(dve, hot)
                own.then(v.tensor_tensor(emap_f[:, :, :], con("block_no", 1)[:, 0:TILES].unsqueeze(2).broadcast_to([1, TILES, E]),
                                         ca[0:1, :].unsqueeze(1).broadcast_to([1, TILES, E]), ALU.is_ge))
                own.then(v.tensor_reduce(emap_s[:, 0, :], emap_f[:, :, :], AX, ALU.add))
                own.then(v.tensor_scalar(emap_s[:, 1, :], emap_s[:, 0, :], float(E - 1), None, ALU.min))
                own.then(v.tensor_copy(expert_of[:, :], emap_s[:, 1, :]))
                dve.wait_ge(m["hot_used"], 2 * NT)
                own.then(v.tensor_copy(source_f[:, 0, :], bank[0][:, 0:BLOCKS]))
                own.then(v.scalar_tensor_tensor(source_f[:, 1, :], source_f[:, 0, :], -1.0, bank[1][:, 0:BLOCKS], ALU.add, ALU.add))
                own.then(v.tensor_scalar(source_f[:, 0, :], source_f[:, 1, :], 0.0, None, ALU.max))
                v.tensor_copy(source[:, :], source_f[:, 0, :]).then_inc(m["slots_ready"], 1)
                dve.wait_ge(m["slots_ready"], 1)

                def expert(i):
                    return dve.value_load(expert_of[0:1, bass.ds(i, 1)], min_val=0, max_val=E - 1)

                def split_rows(i, r):
                    dve.wait_ge(m["turned_hi"], i + 1)
                    v.tensor_tensor(xg_lo[:, r % 2, :], r_bank[r % 2][:, 0:ROWS], xg_hi[:, r % 2, :].bitcast(F32), ALU.subtract).then_inc(m["split"], 1)

                def stage(i, r, least):
                    e = expert(i)
                    if least >= 2:
                        dve.wait_ge(m["up_ready"], i - 1)
                    w = W1[:, bass.ds(e * F, F)]
                    v.tensor_copy(w1_hi[:, r % 2, :], w).then_inc(m["staged"], 1)
                    dve.wait_ge(m["staged"], i * 2 + 1)
                    v.tensor_tensor(w1_lo[:, r % 2, :], w, w1_hi[:, r % 2, :].bitcast(F32), ALU.subtract).then_inc(m["staged"], 1)

                def finish(i, r, least):
                    e = expert(i)
                    if least >= 4:
                        dve.wait_ge(m[f"stored{r}"], stores_before(i, r))
                    dve.wait_ge(m["down_ready"], i + 1)
                    v.tensor_tensor(y_rows[:, r, :, :], y_bank[r % 2][:, 0:ROWS].rearrange("p (b d) -> p b d", b=RB),
                                    b2_rows[:, bass.ds(e, 1), :].broadcast_to([P, RB, D]), ALU.add).then_inc(m["y_ready"], 1)

                dve.wait_ge(experts_loaded, 32)
                stage(0, 0, 0)
                stage(1, 1, 1)
                split_rows(0, 0)
                split_rows(1, 1)
                dve.wait_ge(m["bias_ready"], 16)

                def slot(i, r, least):
                    if least + 2 < TILES:
                        stage(i + 2, (r + 2) % 4, least + 2)
                        split_rows(i + 2, (r + 2) % 4)
                    finish(i, r, least)

                tile_slots(dve, slot)

            def add_expert_rows(n, c, rows):
                m = moe_sems[n]
                for k in rows:
                    t, which = c * CT + k // 2, k % 2
                    dve.wait_ge(m[f"got{k}"], c * 16 + 16)
                    if which:
                        dve.wait_ge(m["got_used"], c * (2 * CT) + k)
                    xs = X[:, bass.ds(t, 1), :].rearrange("p a d -> p (a d)")
                    ins = v.scalar_tensor_tensor(xs, got[:, k, :], weight[which][:, bass.ds(t, 1)], xs, ALU.mult, ALU.add)
                    ins.then_inc(m["got_used"], 1)
                dve.wait_ge(m["got_used"], c * (2 * CT) + (rows[-1] + 1))
                v.memset(scratch2[:, :], 0.0)

            attention("a")
            experts("1")
            attention("b")
            experts("2")
            for c in range(NCH):
                add_expert_rows("2", c, range(2 * CT))

        @block.scalar
        def _(act):
            s = nc.scalar

            def attention(n):
                m, w, steps = att_sems[n], layers[n], Steps(n)

                def probs(unit, u, nb):
                    heads, width = (G, P) if nb == 0 else (2, S)
                    act.wait_ge(m["max_ready"], unit * 3 + (nb + 1))
                    for h in range(heads):
                        cols = slice(h * width, (h + 1) * width)
                        head = (h if nb == 0 else 2 * (nb - 1) + h) * G + u % G
                        ins = s.activation(prob[:, nb, cols], s_bank[nb][:, cols], ACT.Exp, bias=neg_max[:, nb, h:h + 1],
                                           accum_out=sums[:, u // G, min(nb, 1), head:head + 1])
                    ins.then_inc(m["probs_ready"], 1)

                def copy_t(unit, u, nb):
                    act.wait_ge(m["pt_ready"], unit * 3 + (nb + 1))
                    s.activation(prob_t[:, u % 2, nb, :], t_bank[(3 * u + nb) % 2][:, :], ACT.Copy).then_inc(m["pt_copied_act"], 1)

                def step(kind, g, c, par, k, at):
                    bank_ = w_bank[at % 2]
                    if kind == "prep":
                        act.wait_ge(m["shared_ready"], k + 1)
                        s.activation(xt_hi[:, :], bank_[:, :], ACT.Copy).then_inc(m["hi_ready"], 1)
                    elif kind == "query2":
                        act.wait_ge(m["shared_ready"], k + 1)
                        two = lambda ap: ap.rearrange("p (b s) -> p b s", b=2)
                        s.activation(q_whole[:, par, g, :, :], two(bank_[:, :])[:, :, 0:P], ACT.Identity, bias=wqk_bias[:, 0:1])
                        s.activation(q_hi[:, par, g, :, :], two(bank_[:, :])[:, :, P:S], ACT.Identity, bias=wqk_bias[:, 0:1]).then_inc(m["hi_ready"], 1)
                        act.wait_ge(m["summed"], c * 2 * G + (2 * g + 2))
                        s.activation(k_hi[:, par, g, :, 0:P], k_whole[:, par, g, :, :], ACT.Copy)
                        s.activation(k_hi[:, par, g, :, P:S], two(rope_k[:, 0, :])[:, :, P:S], ACT.Copy).then_inc(m["key_hi_ready"], 1)
                    elif kind in ("query", "key") and not steps.rotary:
                        which = 0 if kind == "query" else 1
                        act.wait_ge(m["shared_ready"], k + 1)
                        if not (isinstance(c, int) and c == 0 and g == 0):
                            act.wait_ge(m["summed"], c * 2 * G + (2 * g - 1 + which))
                        s.activation((rope_q, rope_k)[which][:, 0, :], bank_[:, :], ACT.Identity,
                                     bias=w["bias"][:, which, g:g + 1]).then_inc(m["read"], 1)

                k = 0
                for kind, g in steps.all_make():
                    step(kind, g, 0, 0, k, k)
                    k += steps.uses(kind)
                for nb in range(3):
                    probs(0, 0, nb)

                def period(c, par, first, last):
                    at = 0
                    for u in range(UNITS):
                        unit = c * UNITS + u
                        for nb in range(3):
                            if nb != 1:
                                copy_t(unit, u, nb)
                            if not (last and u == UNITS - 1):
                                probs(unit + 1, (u + 1) % UNITS, nb)
                            for kind, g in steps.at(u, nb, not last, not first):
                                step(kind, g, c + 1, 1 - par, steps.before(c) + at, at + 1 - first)
                                at += steps.uses(kind)

                periods(act, period)

            def experts(n):
                m = moe_sems[n]
                act.wait_ge(m["gap_ready"], 1)
                s.activation(col[4][:, :], col[3][:, :], ACT.Exp).then_inc(m["exp_ready"], 1)

                def turned_high(i, r, least):
                    act.wait_ge(m["turned"], i + 1)
                    if least >= 2:
                        act.wait_ge(m["up_ready"], i - 1)
                    s.activation(xg_hi[:, r % 2, :], r_bank[r % 2][:, 0:ROWS], ACT.Copy).then_inc(m["turned_hi"], 1)

                def gelu(i, r, least):
                    e = act.value_load(expert_of[0:1, bass.ds(i, 1)], min_val=0, max_val=E - 1)
                    act.wait_ge(m["up_ready"], i + 1)
                    if least >= 2:
                        act.wait_ge(m["down_ready"], i - 1)
                    for k in range(FT):
                        ins = s.activation(hid[:, r % 2, k, :], h_bank[r % 2][k // 2][:, k % 2 * ROWS:(k % 2 + 1) * ROWS], ACT.Gelu,
                                           bias=b1_cols[:, bass.ds(e * FT + k, 1)])
                    ins.then_inc(m["gelu_ready"], 1)

                act.wait_ge(m["slots_ready"], 1)
                turned_high(0, 0, 0)
                turned_high(1, 1, 1)
                gelu(0, 0, 0)

                def slot(i, r, least):
                    if least + 2 < TILES:
                        turned_high(i + 2, (r + 2) % 4, least + 2)
                    if least + 1 < TILES:
                        gelu(i + 1, (r + 1) % 4, least + 1)

                tile_slots(act, slot)

            act.dma_start(X[:, 0:CT, :], x_tiles[:, 0:CT, :]).then_inc(x0_loaded, 16)
            rest = [(C[:, :], const[:, 0:KEPT_W]), *((wb[:, k, :], w) for k, w in enumerate((Wq, Wk, Wv, Wo))),
                    *((bqk[:, k, :], v.rearrange("(h d) -> d h", d=HD)) for k, v in enumerate((bq, bk))),
                    (layers["a"]["out_b"][:, :], cproj_b.partition_broadcast(P)), (layers["b"]["out_b"][:, :], bo.partition_broadcast(P)),
                    (layers["b"]["v_bias"][:, :], bv.partition_broadcast(P)), (gate_bias[:, :], gate_b.partition_broadcast(P)),
                    (gate[:, :], gate_w), (X[:, CT:2 * CT, :], x_tiles[:, CT:2 * CT, :]), (X[:, 2 * CT:NT, :], x_tiles[:, 2 * CT:NT, :]),
                    (b1_cols[:, :].rearrange("p (e k) -> p e k", e=E), b1.rearrange("e (k p) -> p e k", p=P))]
            assert len(rest) == N_REST
            with nc.allow_non_contiguous_dma(reason="biases as columns"):
                for dst, src in rest:
                    act.dma_start(dst, src).then_inc(rest_loaded, 16)

            attention("a")
            experts("1")
            attention("b")
            experts("2")

        @block.tensor
        def _(pe):
            t_ = nc.tensor

            pe.wait_ge(dve_prep, 1)
            t_.matmul(bank[0][0:HD, 0:HD], kv2l_n[:, :], l2o_t[:, :], start=True, stop=True).then_inc(pe_prep, 1)
            pe.wait_ge(dve_prep, 2)
            for k, (lhs, rhs) in enumerate(((con("rep8", HD), q2l_t), (con("rep8", HD), kv2l_t), (con("rep32", L), wqk_t))):
                t_.matmul(bank[1][:, k * L:(k + 1) * L], lhs, rhs[:, :], start=True, stop=True)
            t_.matmul(bank[1][:, 3 * L:3 * L + HD], con("rep8", HD), m_t[:, :], start=True, stop=True).then_inc(pe_prep, 1)
            pe.wait_ge(dve_prep, 3)
            for k in range(4):
                t_.matmul(bank[k][:, :], cw[:, k // 2, :], blk[k][:, :, :].rearrange("p h l -> p (h l)"), start=True, stop=True).then_inc(pe_prep, 1)
            t_.matmul(bank[4][:, 0:D], cw[:, 2, :], blk_v[:, :, :].rearrange("p h d -> p (h d)"), start=True, stop=True)
            t_.matmul(bank[4][:, D:2 * D], ones[:, :], blk_vb[:, :, :].rearrange("p h d -> p (h d)"), start=True, stop=False)
            t_.matmul(bank[4][:, D:2 * D], kvb_rep[:, :], l2o_t[:, :].unsqueeze(1).broadcast_to([L, H, HD]), start=False, stop=False)
            ins = t_.matmul(bank[4][:, D:2 * D], ones[0:1, :], l2o_row[:, :].unsqueeze(1).broadcast_to([1, H, HD]), start=False, stop=True)
            ins.then_inc(pe_prep, 1)
            pe.wait_ge(rest_loaded, 16 * N_REST)
            for dst, src in ((bank[6][:, 0:D], cp[:, :]), (bank[6][:, D:2 * D], wb[:, 3, :]), (bank[7][:, 0:D], wb[:, 0, :]),
                             (bank[7][:, D:2 * D], wb[:, 1, :]), (bank[7][:, 2 * D:3 * D], wb[:, 2, :])):
                ins = t_.transpose(dst, src, ident)
            ins.then_inc(pe_prep, 1)
            for k in range(4):
                for g in range(G):
                    t_.matmul(bank[5][:, k * G + g:k * G + g + 1], blk[k][:, g * G:(g + 1) * G, :].rearrange("p h l -> p (h l)"), b3[:, k // 2:k // 2 + 1],
                              start=True, stop=True)
                t_.matmul(bank[5][:, 4 * G + k:4 * G + k + 1], con("rot32" if k % 2 else "rep32", L), lat_b[:, k // 2:k // 2 + 1], start=True, stop=True)
            t_.matmul(bank[5][:, 4 * G + 4:4 * G + 5], con("rep32", L), lat_b[:, 2:3], start=True, stop=True)
            t_.matmul(bank[5][:, 32:32 + 2 * H], con("stack8", HD), bqk[:, :, :].rearrange("p m h -> p (m h)"), start=True, stop=True).then_inc(pe_prep, 1)
            pe.wait_ge(dve_prep, 4)

            def product(o, w_hi, w_lo, x_hi, x_lo, start=True):
                t_.matmul(o, w_hi, x_hi, start=start, stop=False, skip_group_check=True)
                t_.matmul(o, w_lo, x_hi, start=False, stop=False, skip_group_check=True)
                return t_.matmul(o, w_hi, x_lo, start=False, stop=True, skip_group_check=True)

            def attention(n):
                m, w, steps = att_sems[n], layers[n], Steps(n)

                def step(kind, g, c, par, k, at, norm=None, place=(None, (), 0)):

                    def free(behind):
                        if not steps.rotary:
                            by_vector, by_scalar = steps.to_wait(*place, behind)
                            if by_vector is not None:
                                pe.wait_ge(m["shared_free"], by_vector)
                            if by_scalar is not None:
                                pe.wait_ge(m["read"], by_scalar)
                        elif not (isinstance(k, int) and k < behind):
                            pe.wait_ge(m["shared_free"], k - (behind - 1))

                    free(1 if kind in ("value", "out_t", "out", "gate") else 2)
                    bank_ = w_bank[at % 2]
                    if kind in ("prep", "gate_t"):
                        pe.wait_ge(m["ln_ready"], norm)
                        for t in range(CT):
                            ins = t_.transpose(bank_[:, t * P:(t + 1) * P], xn[:, t, :], ident)
                    elif kind == "value":
                        for t in range(CT):
                            cols = slice(t * P, (t + 1) * P)
                            ins = product(bank_[:, cols], xt_hi[:, cols], xt_lo[:, cols], w["v_hi"][:, :], w["v_lo"][:, :])
                    elif kind in ("query", "key"):
                        cols = slice(g * P, (g + 1) * P)
                        first_mat = 0 if kind == "query" else steps.uses(kind)
                        for part in range(steps.uses(kind)):
                            if part:
                                ins.then_inc(m["shared_ready"], 1)
                                k, bank_ = k + 1, w_bank[(at + 1) % 2]
                                free(2)
                            ins = product(bank_[:, :], w["hi"][first_mat + part][:, cols], w["lo"][first_mat + part][:, cols], xt_hi[:, :], xt_lo[:, :])
                    elif kind == "query2":
                        pe.wait_ge(m["summed"], c * 2 * G + (2 * g + 1))
                        ins = t_.matmul(bank_[:, :], wqk_blk[:, :], rope_q[:, 0, :], start=True, stop=True)
                    elif kind == "turn":
                        pe.wait_ge(m["o_copied"], c * 2 + (g + 1))
                        for q in range(2):
                            ins = t_.transpose(bank_[:, q * P:(q + 1) * P], o_t[:, q * P:(q + 1) * P], ident)
                    elif kind == "out_t":
                        for t in range(CT):
                            ins = t_.transpose(bank_[:, t * P:(t + 1) * P], Y[:, par, t, :], ident)
                    elif kind == "out":
                        for t in range(CT):
                            ins = t_.matmul(bank_[:, t * P:(t + 1) * P], y_t[:, t * P:(t + 1) * P], w["out_w"][:, :], start=True, stop=True)
                    elif kind == "gate":
                        for t in range(CT):
                            ins = t_.matmul(bank_[:, t * E:(t + 1) * E], y_t[:, t * P:(t + 1) * P], gate[:, :], start=True, stop=True)
                    ins.then_inc(m["shared_ready"], 1)

                def scores(u, par, nb):
                    b_, j = u // G, u % G
                    rows = slice(j * L, (j + 1) * L)
                    heads = range(G) if nb == 0 else range(2 * nb - 2, 2 * nb)
                    width = P if nb == 0 else S
                    for k, g in enumerate(heads):
                        o = s_bank[nb][:, k * width:(k + 1) * width]
                        kk = k_hi[rows, par, g, b_, 0:width]
                        if not steps.rotary:
                            t_.matmul(o, (q_lo if nb == 0 else q_hi)[rows, par, g, b_, :], kk, start=(k == 0), stop=False, skip_group_check=True)
                        elif nb == 0:
                            t_.matmul(o, q_whole[rows, par, g, b_, :], k_whole[rows, par, g, b_, :], start=(k == 0), stop=False, skip_group_check=True)
                        else:
                            product(o, q_hi[rows, par, g, b_, :], q_lo[rows, par, g, b_, :], kk, k_lo[rows, par, g, b_, :], start=(k == 0))
                    o = s_bank[nb][:, :].rearrange("p (h k) -> p h k", h=len(heads))[:, :, width - P:width]
                    t_.matmul(o, ident_b[:, :], causal_b[:, :].unsqueeze(1).broadcast_to([P, len(heads), P]), start=False, stop=True,
                              skip_group_check=True).then_inc(m["scores_ready"], 1)

                def transposes(unit, u, nb, first):
                    pe.wait_ge(m["probs_ready"], unit * 3 + (nb + 1))
                    if nb == 0 and not first:
                        pe.wait_ge(m["pt_copied_dve"], unit)
                    elif nb == 1 and not first:
                        pe.wait_ge(m["pt_copied_act"], unit * 2)
                    elif nb == 2:
                        pe.wait_ge(m["pt_copied_act"], unit * 2 + 1)
                    for k in range(4):
                        cols = slice(k * P, (k + 1) * P)
                        ins = t_.transpose(t_bank[(3 * u + nb) % 2][:, cols], prob[:, nb, cols], ident)
                    ins.then_inc(m["pt_ready"], 1)

                def weighted(c, unit, u, par):
                    b_, j = u // G, u % G
                    pe.wait_ge(m["pt_copied_dve"], unit + 1)
                    pe.wait_ge(m["pt_copied_act"], unit * 2 + 2)
                    if j == 0 and not (isinstance(c, int) and c == 0 and b_ == 0):
                        pe.wait_ge(m["o_copied"], c * 2 + b_)
                    pt = prob_t[:, u % 2, :, :]
                    for q, kb in ((0, 0), (1, 0), (1, 1)):
                        for g in range(G):
                            if q == 0:
                                rhs = pt[:, 0, g * P:(g + 1) * P]
                            else:
                                at = ((g % 2) * 2 + kb) * P
                                rhs = pt[:, 1 + g // 2, at:at + P]
                            ins = t_.matmul(o_bank[g * L:(g + 1) * L, q * P:(q + 1) * P], v_aug[:, par, 2 * b_ + kb, g * G + j, :], rhs,
                                            start=(j == 0 and q == 0), stop=(j == G - 1 and kb == q), skip_group_check=True)
                    ins.then_inc(m["pv_ready"], 1)

                def operands(c_next, k_end):
                    if steps.rotary:
                        pe.wait_ge(m["shared_free"], k_end)
                        pe.wait_ge(m["key_lo_ready"], c_next * G + G)
                    else:
                        pe.wait_ge(m["summed"], c_next * (2 * G) + 2 * G)

                k = 0
                for kind, g in steps.all_make():
                    step(kind, g, 0, 0, k, k, norm_no(0), (None, steps.all_make(), k))
                    k += steps.uses(kind)
                operands(0, steps.n_make)
                for nb in range(3):
                    scores(0, 0, nb)

                def period(c, par, first, last):
                    at = 0
                    for u in range(UNITS):
                        unit = c * UNITS + u
                        for nb in range(3):
                            transposes(unit, u, nb, first and u == 0)
                            if u < UNITS - 1:
                                scores(u + 1, par, nb)
                            elif not last:
                                if nb == 0:
                                    operands(c + 1, steps.made(c + 1, steps.last_made))
                                scores(0, 1 - par, nb)
                            if nb == 1 and not (first and u < 1):
                                weighted(c if u else c - 1, unit - 1, (u - 1) % UNITS, par if u else 1 - par)
                            for kind, g in steps.at(u, nb, not last, not first):
                                place = (c, steps.order(not last, not first), at)
                                if (kind, g) == ("turn", 0):
                                    step(kind, g, c, par, steps.before(c) + at, at + 1 - first, None, place)
                                elif kind in CLOSING:
                                    step(kind, g, c - 1, 1 - par, steps.before(c) + at, at + 1 - first, gate_norm_no(c - 1) if kind == "gate_t" else None, place)
                                else:
                                    step(kind, g, c + 1, 1 - par, steps.before(c) + at, at + 1 - first, norm_no(1) if first else norm_no(c + 1), place)
                                at += steps.uses(kind)

                periods(pe, period)
                end = NCH * UNITS - 1
                weighted(NCH - 1, end, UNITS - 1, 1)
                k = steps.before(NCH - 1) + 1 + steps.n_close
                for kind, g in (("turn", 1), ("out_t", 0), ("out", 0), ("gate_t", 0), ("gate", 0)):
                    order = steps.order(False, True)
                    place = (NCH - 1, order + [(kind, g)] * 5, k - steps.before(NCH - 1))
                    step(kind, g, NCH - 1, 1, k, k, gate_norm_no(NCH - 1) if kind == "gate_t" else None, place)
                    k += 1

            def experts(n):
                m = moe_sems[n]

                pe.wait_ge(m["mask_ready"], 1)
                mask = chosen_b[:, :, :].rearrange("p t e -> p (t e)")
                t_.matmul(w_bank[0][:, 0:NT * E], before_b[:, :], mask, start=True, stop=True)
                t_.matmul(w_bank[1][:, 0:NT * E], ones_b[:, :], mask, start=True, stop=True).then_inc(m["rank_ready"], 1)

                def token_of(t, k, n_):
                    pe.wait_ge(m["hot_ready"], n_ + 1)
                    if k == 1:
                        pe.wait_ge(m["block_hot_ready"], t + 1)
                    ring = hot_ring[0]
                    t_.matmul(bank[k][:, 0:BLOCKS], lane_hot[:, ring, :], block_hot[:, ring, :], start=(isinstance(t, int) and t == 0),
                              stop=(isinstance(t, int) and t == NT - 1)).then_inc(m["hot_used"], 1)
                    hot_ring[0] = (ring + 1) % 4

                hot_ring = [0]
                hot_tiles(pe, token_of)
                pe.wait_ge(m["slots_ready"], 1)

                def turn_rows(i, r, least):
                    pe.wait_ge(m[f"row{r}"], (stores_before(i, r) + 16) * RB)
                    if least >= 2:
                        pe.wait_ge(m["split"], i - 1)
                    for b_ in range(RB):
                        ins = t_.transpose(r_bank[r % 2][:, b_ * P:(b_ + 1) * P], xg[:, r, b_, :], ident)
                    ins.then_inc(m["turned"], 1)

                def up(i, r, least):
                    pe.wait_ge(m["split"], i + 1)
                    pe.wait_ge(m["staged"], i * 2 + 2)
                    if least >= 2:
                        pe.wait_ge(m["gelu_ready"], i - 1)
                    for k in range(FT):
                        cols = slice(k * P, (k + 1) * P)
                        ins = product(h_bank[r % 2][k // 2][:, k % 2 * ROWS:(k % 2 + 1) * ROWS], w1_hi[:, r % 2, cols], w1_lo[:, r % 2, cols],
                                      xg_hi[:, r % 2, :], xg_lo[:, r % 2, :])
                    ins.then_inc(m["up_ready"], 1)

                def down(i, r, least):
                    e = pe.value_load(expert_of[0:1, bass.ds(i, 1)], min_val=0, max_val=E - 1)
                    pe.wait_ge(m["gelu_ready"], i + 1)
                    if least >= 2:
                        pe.wait_ge(m["y_ready"], i - 1)
                    for b_ in range(RB):
                        for k in range(FT):
                            ins = t_.matmul(y_bank[r % 2][:, b_ * P:(b_ + 1) * P], hid[:, r % 2, k, b_ * P:(b_ + 1) * P],
                                            W2[:, bass.ds(e * F + k * D, D)], start=(k == 0), stop=(k == FT - 1))
                    ins.then_inc(m["down_ready"], 1)

                turn_rows(0, 0, 0)
                turn_rows(1, 1, 1)
                up(0, 0, 0)

                def slot(i, r, least):
                    if least + 2 < TILES:
                        turn_rows(i + 2, (r + 2) % 4, least + 2)
                    if least + 1 < TILES:
                        up(i + 1, (r + 1) % 4, least + 1)
                    down(i, r, least)

                tile_slots(pe, slot)

            attention("a")
            experts("1")
            attention("b")
            experts("2")


_INS = ["L0_attn_a_x"] + [f"L0_attn_a_{k}" for k in (
    "c_attn_w", "c_attn_b", "q2l_w", "q2l_b", "kv2l_w", "kv2l_b", "l2o_w", "l2o_b", "wqk_w", "wqk_b", "cproj_w", "cproj_b")] + [
    f"L0_attn_b_{k}" for k in ("Wq", "bq", "Wk", "bk", "Wv", "bv", "Wo", "bo")] + [
    f"L0_ffn_{k}" for k in ("gate_w", "gate_b", "w1", "b1", "w2", "b2")]
_OUTS = [((B, S, D), "float32")]


def kernel(**inputs):
    import numpy as _np
    import concourse.bacc as _bacc
    from concourse import mybir as _mybir
    from concourse.bass_utils import run_bass_kernel_spmd as _run

    nc = _bacc.Bacc("TRN2", target_bir_lowering=False, num_devices=1)
    arrays, args = {}, []
    for name in _INS:
        a = _np.ascontiguousarray(inputs[name])
        arrays[f"in_{name}_dram"] = a
        args.append(nc.dram_tensor(f"in_{name}_dram", a.shape, _mybir.dt.from_np(a.dtype), kind="ExternalInput").ap())
    arrays["const_dram"] = constants()
    args.append(nc.dram_tensor("const_dram", (P, CONST_W), F32, kind="ExternalInput").ap())
    for i, (shape, dtype) in enumerate(_OUTS):
        dt = _mybir.dt.from_np(_np.dtype(dtype))
        args.append(nc.dram_tensor(f"out_{i}_dram", shape, dt, kind="ExternalOutput").ap())
    program(nc, *args)
    r = _run(nc, [arrays], core_ids=[0])
    return r.results[0]["out_0_dram"]
```
